# Optimizing a Trainium2 kernel written in Bass

```python
import numpy as np
import jax
import jax.numpy as jnp

def _softmax(x, axis=-1):
    return jax.nn.softmax(x, axis=axis)

def _gelu(x):
    return jax.nn.gelu(x, approximate=True)

def _silu(x):
    return jax.nn.silu(x)

def _sigmoid(x):
    return jax.nn.sigmoid(x)

def _layernorm(x, axis=-1, eps=1e-05):
    m = jnp.mean(x, axis=axis, keepdims=True)
    v = jnp.var(x, axis=axis, keepdims=True)
    return (x - m) / jnp.sqrt(v + eps)

def _scatter_add(tgt, idx, src, axis=0):
    return tgt.at[idx].add(src)

def _segment_sum(src, seg, n):
    return jax.ops.segment_sum(src, seg, n)
kernel_name = 'mk_gnn_resnorm_d2_gnn_r32_1f75dd'

def setup_inputs(seed: int=0):
    np.random.seed(seed)
    _w = jnp.asarray

    def _rec_inputs():
        import jax
        import jax.numpy as jnp
        _gk = jax.random.key(seed)
        x = -1.686e-05 + 1 * jax.random.normal(jax.random.fold_in(_gk, 1), (50000, 160), jnp.float32)
        src = jax.random.randint(jax.random.fold_in(_gk, 2), (25000,), 0, 50000, jnp.int32)
        dst = jnp.minimum((50000 * jax.random.uniform(jax.random.fold_in(_gk, 3), (25000,)) ** 2.0).astype(jnp.int32), 49999)
        _o = jnp.argsort(dst, stable=True)
        src = src[_o]
        dst = dst[_o]
        edge_attr_3 = 0.00047201 + 1.00023 * jax.random.normal(jax.random.fold_in(_gk, 11), (25000, 3), jnp.float32)
        edge_attr_4 = 0.0007022 + 0.999661 * jax.random.normal(jax.random.fold_in(_gk, 12), (25000, 4), jnp.float32)
        edge_attr_64 = 0.000279952 + 1.00013 * jax.random.normal(jax.random.fold_in(_gk, 13), (25000, 64), jnp.float32)
        node_vec1 = -0.00915711 + 0.999674 * jax.random.normal(jax.random.fold_in(_gk, 15), (50000, 1), jnp.float32)
        return (x, src, dst, edge_attr_3, edge_attr_4, edge_attr_64, node_vec1)
    x, src, dst, edge_attr_3, edge_attr_4, edge_attr_64, node_vec1 = _rec_inputs()

    def _L0_gnn_setup():
        import jax, jax.numpy as jnp
        import numpy as np
        MUL0, MUL1 = (64, 32)
        INV_SQRT3 = 1.0 / np.sqrt(3.0)

        def _split(x):
            return (x[:, :MUL0], x[:, MUL0:].reshape(x.shape[0], MUL1, 3))

        def _merge(o0, o1):
            return jnp.concatenate([o0, o1.reshape(o1.shape[0], -1)], axis=-1)

        def _tp(x0, x1, y0, y1, w000, w011, w101, w110):
            fan0 = x0.shape[1] * y0.shape[1] + x1.shape[1] * y1.shape[1]
            fan1 = x0.shape[1] * y1.shape[1] + x1.shape[1] * y0.shape[1]
            out0 = (jnp.einsum('eu,ev,uvw->ew', x0, y0, w000) + INV_SQRT3 * jnp.einsum('euk,evk,uvw->ew', x1, y1, w110)) / np.sqrt(fan0)
            out1 = (jnp.einsum('eu,evk,uvw->ewk', x0, y1, w011) + jnp.einsum('euk,ev,uvw->ewk', x1, y0, w101)) / np.sqrt(fan1)
            return (out0, out1)

        def _lin(x0, x1, w0, w1):
            return (x0 @ w0 / np.sqrt(x0.shape[1]), jnp.einsum('euk,uv->evk', x1, w1) / np.sqrt(x1.shape[1]))
        key = jax.random.key(seed)
        ks = jax.random.split(key, 20)
        N, E = (50000, 15625)
        inp = {'node_features': jax.random.normal(ks[0], (N, MUL0 + 3 * MUL1), dtype=jnp.float32), 'edge_index': jax.random.randint(ks[1], (2, E), 0, N, dtype=jnp.int64), 'edge_attr_tensor': jax.random.normal(ks[2], (E, 4), dtype=jnp.float32), 'node_attr_scalar_raw': jax.random.normal(ks[3], (N, 1), dtype=jnp.float32), 'wm000': jax.random.normal(ks[4], (MUL0, 1, MUL0), dtype=jnp.float32), 'wm011': jax.random.normal(ks[5], (MUL0, 1, MUL1), dtype=jnp.float32), 'wm101': jax.random.normal(ks[6], (MUL1, 1, MUL1), dtype=jnp.float32), 'wm110': jax.random.normal(ks[7], (MUL1, 1, MUL0), dtype=jnp.float32), 'lm0': jax.random.normal(ks[8], (MUL0, MUL0), dtype=jnp.float32), 'lm1': jax.random.normal(ks[9], (MUL1, MUL1), dtype=jnp.float32), 'wu000': jax.random.normal(ks[10], (MUL0, MUL0, MUL0), dtype=jnp.float32), 'wu011': jax.random.normal(ks[11], (MUL0, MUL1, MUL1), dtype=jnp.float32), 'wu101': jax.random.normal(ks[12], (MUL1, MUL0, MUL1), dtype=jnp.float32), 'wu110': jax.random.normal(ks[13], (MUL1, MUL1, MUL0), dtype=jnp.float32), 'lu0': jax.random.normal(ks[14], (MUL0, MUL0), dtype=jnp.float32), 'lu1': jax.random.normal(ks[15], (MUL1, MUL1), dtype=jnp.float32)}
        return inp
    _L0_gnn_all = _L0_gnn_setup()
    _L0_gnn_in = {k: v for k, v in _L0_gnn_all.items() if k in ('wm000', 'wm011', 'wm101', 'wm110', 'lm0', 'lm1', 'wu000', 'wu011', 'wu101', 'wu110', 'lu0', 'lu1')}
    del _L0_gnn_all

    def _L1_gnn_setup():
        import jax, jax.numpy as jnp
        import numpy as np
        N_NODES = 10000
        N_EDGES = 10000
        MUL0, MUL1 = (64, 32)
        EDGE_DIM = 64
        W_NUMEL = 224
        DENOM = 32.0
        SQRT3 = 3.0 ** 0.5
        INV_SQRT3 = 1.0 / SQRT3
        INV_SQRT2 = 2.0 ** (-0.5)

        def _forward(node_feature, edge_attr, edge_feature, W_skip0, W_skip1, W_nl0, W_nl1, W_fc1, W_fc2, W_out_s, W_out_v, edge_index):
            N = node_feature.shape[0]
            E = edge_attr.shape[0]
            s = node_feature[:, :MUL0]
            v = node_feature[:, MUL0:].reshape(N, MUL1, 3)
            skip_s = s @ W_skip0
            skip_v = jnp.einsum('nmi,mk->nki', v, W_skip1)
            s = s @ W_nl0
            v = jnp.einsum('nmi,mk->nki', v, W_nl1)
            rhat = edge_attr / jnp.linalg.norm(edge_attr, axis=-1, keepdims=True)
            sh1 = SQRT3 * rhat
            w = jax.nn.relu(edge_feature @ W_fc1) @ W_fc2
            w0, w1, w2, w3, w4 = jnp.split(w, [64, 128, 160, 192], axis=-1)
            src, dst = (edge_index[0], edge_index[1])
            xs = s[dst]
            xv = v[dst]
            out0a = w0 * xs
            out0b = w3 * (jnp.einsum('emi,ei->em', xv, sh1) * INV_SQRT3)
            out1a = (w1 * xs)[:, :, None] * sh1[:, None, :]
            out1b = w2[:, :, None] * xv
            out1c = w4[:, :, None] * (jnp.cross(xv, sh1[:, None, :]) * INV_SQRT2)
            tp = jnp.concatenate([out0a, out0b, out1a.reshape(E, -1), out1b.reshape(E, -1), out1c.reshape(E, -1)], axis=-1)
            agg = jax.ops.segment_sum(tp, src, num_segments=N) / DENOM
            agg_s = agg[:, :96]
            agg_v = agg[:, 96:].reshape(N, 128, 3)
            out_s = agg_s @ W_out_s + skip_s
            out_v = jnp.einsum('nmi,mk->nki', agg_v, W_out_v) + skip_v
            fs = jax.nn.silu(out_s[:, :MUL0])
            gate = jax.nn.sigmoid(out_s[:, MUL0:MUL0 + 32])
            gv = gate[:, :, None] * out_v
            return jnp.concatenate([fs, gv.reshape(N, -1)], axis=-1)
        key = jax.random.key(seed)
        ks = jax.random.split(key, 12)

        def lin(k, fi, fo):
            return jax.random.normal(k, (fi, fo), jnp.float32) / np.float32(np.sqrt(fi))
        return {'node_feature': jax.random.normal(ks[0], (N_NODES, MUL0 + 3 * MUL1), jnp.float32), 'edge_attr': jax.random.normal(ks[1], (N_EDGES, 3), jnp.float32), 'edge_feature': jax.random.normal(ks[2], (N_EDGES, EDGE_DIM), jnp.float32), 'W_skip0': lin(ks[3], MUL0, 96), 'W_skip1': lin(ks[4], MUL1, 32), 'W_nl0': lin(ks[5], MUL0, MUL0), 'W_nl1': lin(ks[6], MUL1, MUL1), 'W_fc1': lin(ks[7], EDGE_DIM, 64), 'W_fc2': lin(ks[8], 64, W_NUMEL), 'W_out_s': lin(ks[9], 96, 96), 'W_out_v': lin(ks[10], 128, 32), 'edge_index': jax.random.randint(ks[11], (2, N_EDGES), 0, N_NODES)}
    _L1_gnn_all = _L1_gnn_setup()
    _L1_gnn_in = {k: v for k, v in _L1_gnn_all.items() if k in ('W_skip0', 'W_skip1', 'W_nl0', 'W_nl1', 'W_fc1', 'W_fc2', 'W_out_s', 'W_out_v')}
    del _L1_gnn_all
    return {'x': x, 'src': src, 'dst': dst, 'edge_attr_3': edge_attr_3, 'edge_attr_4': edge_attr_4, 'edge_attr_64': edge_attr_64, 'node_vec1': node_vec1, 'L0_gnn_wm000': _L0_gnn_in['wm000'], 'L0_gnn_wm011': _L0_gnn_in['wm011'], 'L0_gnn_wm101': _L0_gnn_in['wm101'], 'L0_gnn_wm110': _L0_gnn_in['wm110'], 'L0_gnn_lm0': _L0_gnn_in['lm0'], 'L0_gnn_lm1': _L0_gnn_in['lm1'], 'L0_gnn_wu000': _L0_gnn_in['wu000'], 'L0_gnn_wu011': _L0_gnn_in['wu011'], 'L0_gnn_wu101': _L0_gnn_in['wu101'], 'L0_gnn_wu110': _L0_gnn_in['wu110'], 'L0_gnn_lu0': _L0_gnn_in['lu0'], 'L0_gnn_lu1': _L0_gnn_in['lu1'], 'L1_gnn_W_skip0': _L1_gnn_in['W_skip0'], 'L1_gnn_W_skip1': _L1_gnn_in['W_skip1'], 'L1_gnn_W_nl0': _L1_gnn_in['W_nl0'], 'L1_gnn_W_nl1': _L1_gnn_in['W_nl1'], 'L1_gnn_W_fc1': _L1_gnn_in['W_fc1'], 'L1_gnn_W_fc2': _L1_gnn_in['W_fc2'], 'L1_gnn_W_out_s': _L1_gnn_in['W_out_s'], 'L1_gnn_W_out_v': _L1_gnn_in['W_out_v']}

def reference(x, src, dst, edge_attr_3, edge_attr_4, edge_attr_64, node_vec1, L0_gnn_wm000, L0_gnn_wm011, L0_gnn_wm101, L0_gnn_wm110, L0_gnn_lm0, L0_gnn_lm1, L0_gnn_wu000, L0_gnn_wu011, L0_gnn_wu101, L0_gnn_wu110, L0_gnn_lu0, L0_gnn_lu1, L1_gnn_W_skip0, L1_gnn_W_skip1, L1_gnn_W_nl0, L1_gnn_W_nl1, L1_gnn_W_fc1, L1_gnn_W_fc2, L1_gnn_W_out_s, L1_gnn_W_out_v):
    import jax
    import jax.numpy as jnp

    def _L0_gnn_ref(node_features, edge_index, edge_attr_tensor, node_attr_scalar_raw, wm000, wm011, wm101, wm110, lm0, lm1, wu000, wu011, wu101, wu110, lu0, lu1):
        import jax, jax.numpy as jnp
        import numpy as np
        MUL0, MUL1 = (64, 32)
        INV_SQRT3 = 1.0 / np.sqrt(3.0)

        def _split(x):
            return (x[:, :MUL0], x[:, MUL0:].reshape(x.shape[0], MUL1, 3))

        def _merge(o0, o1):
            return jnp.concatenate([o0, o1.reshape(o1.shape[0], -1)], axis=-1)

        def _tp(x0, x1, y0, y1, w000, w011, w101, w110):
            fan0 = x0.shape[1] * y0.shape[1] + x1.shape[1] * y1.shape[1]
            fan1 = x0.shape[1] * y1.shape[1] + x1.shape[1] * y0.shape[1]
            out0 = (jnp.einsum('eu,ev,uvw->ew', x0, y0, w000) + INV_SQRT3 * jnp.einsum('euk,evk,uvw->ew', x1, y1, w110)) / np.sqrt(fan0)
            out1 = (jnp.einsum('eu,evk,uvw->ewk', x0, y1, w011) + jnp.einsum('euk,ev,uvw->ewk', x1, y0, w101)) / np.sqrt(fan1)
            return (out0, out1)

        def _lin(x0, x1, w0, w1):
            return (x0 @ w0 / np.sqrt(x0.shape[1]), jnp.einsum('euk,uv->evk', x1, w1) / np.sqrt(x1.shape[1]))
        N = node_features.shape[0]
        row, col = (edge_index[0], edge_index[1])
        r_vec = edge_attr_tensor[:, :3]
        dist = edge_attr_tensor[:, 3:4]
        e0 = dist
        e1 = r_vec[:, None, :]
        xj0, xj1 = _split(node_features[col])
        m0, m1 = _tp(xj0, xj1, e0, e1, wm000, wm011, wm101, wm110)
        d0, d1 = _lin(xj0, xj1, lm0, lm1)
        msgs = _merge(m0 + d0, m1 + d1)
        agg = jax.ops.segment_sum(msgs, row, num_segments=N)
        a0, a1 = _split(agg)
        x0, x1 = _split(node_features)
        u0, u1 = _tp(x0, x1, a0, a1, wu000, wu011, wu101, wu110)
        ud0, ud1 = _lin(x0, x1, lu0, lu1)
        return node_features + _merge(u0 + ud0, u1 + ud1)

    def _L1_gnn_ref(node_feature, edge_attr, edge_feature, W_skip0, W_skip1, W_nl0, W_nl1, W_fc1, W_fc2, W_out_s, W_out_v, edge_index):
        import jax, jax.numpy as jnp
        import numpy as np
        N_NODES = 10000
        N_EDGES = 10000
        MUL0, MUL1 = (64, 32)
        EDGE_DIM = 64
        W_NUMEL = 224
        DENOM = 32.0
        SQRT3 = 3.0 ** 0.5
        INV_SQRT3 = 1.0 / SQRT3
        INV_SQRT2 = 2.0 ** (-0.5)

        def _forward(node_feature, edge_attr, edge_feature, W_skip0, W_skip1, W_nl0, W_nl1, W_fc1, W_fc2, W_out_s, W_out_v, edge_index):
            N = node_feature.shape[0]
            E = edge_attr.shape[0]
            s = node_feature[:, :MUL0]
            v = node_feature[:, MUL0:].reshape(N, MUL1, 3)
            skip_s = s @ W_skip0
            skip_v = jnp.einsum('nmi,mk->nki', v, W_skip1)
            s = s @ W_nl0
            v = jnp.einsum('nmi,mk->nki', v, W_nl1)
            rhat = edge_attr / jnp.linalg.norm(edge_attr, axis=-1, keepdims=True)
            sh1 = SQRT3 * rhat
            w = jax.nn.relu(edge_feature @ W_fc1) @ W_fc2
            w0, w1, w2, w3, w4 = jnp.split(w, [64, 128, 160, 192], axis=-1)
            src, dst = (edge_index[0], edge_index[1])
            xs = s[dst]
            xv = v[dst]
            out0a = w0 * xs
            out0b = w3 * (jnp.einsum('emi,ei->em', xv, sh1) * INV_SQRT3)
            out1a = (w1 * xs)[:, :, None] * sh1[:, None, :]
            out1b = w2[:, :, None] * xv
            out1c = w4[:, :, None] * (jnp.cross(xv, sh1[:, None, :]) * INV_SQRT2)
            tp = jnp.concatenate([out0a, out0b, out1a.reshape(E, -1), out1b.reshape(E, -1), out1c.reshape(E, -1)], axis=-1)
            agg = jax.ops.segment_sum(tp, src, num_segments=N) / DENOM
            agg_s = agg[:, :96]
            agg_v = agg[:, 96:].reshape(N, 128, 3)
            out_s = agg_s @ W_out_s + skip_s
            out_v = jnp.einsum('nmi,mk->nki', agg_v, W_out_v) + skip_v
            fs = jax.nn.silu(out_s[:, :MUL0])
            gate = jax.nn.sigmoid(out_s[:, MUL0:MUL0 + 32])
            gv = gate[:, :, None] * out_v
            return jnp.concatenate([fs, gv.reshape(N, -1)], axis=-1)
        return _forward(node_feature, edge_attr, edge_feature, W_skip0, W_skip1, W_nl0, W_nl1, W_fc1, W_fc2, W_out_s, W_out_v, edge_index)
    edge_index = jnp.stack([src, dst])
    x = _layernorm(x + _L0_gnn_ref(x, edge_index, edge_attr_4, node_vec1, L0_gnn_wm000, L0_gnn_wm011, L0_gnn_wm101, L0_gnn_wm110, L0_gnn_lm0, L0_gnn_lm1, L0_gnn_wu000, L0_gnn_wu011, L0_gnn_wu101, L0_gnn_wu110, L0_gnn_lu0, L0_gnn_lu1), axis=-1)
    x = _layernorm(x + _L1_gnn_ref(x, edge_attr_3, edge_attr_64, L1_gnn_W_skip0, L1_gnn_W_skip1, L1_gnn_W_nl0, L1_gnn_W_nl1, L1_gnn_W_fc1, L1_gnn_W_fc2, L1_gnn_W_out_s, L1_gnn_W_out_v, edge_index), axis=-1)
    return x

_drawn_inputs = setup_inputs


def setup_inputs(seed=0):
    import zlib

    import numpy as np

    out = dict(_drawn_inputs(seed))
    spreads = {}
    factors = {'edge_attr_3': 8.0,
     'edge_attr_64': 8.0,
     'L1_gnn_W_nl0': 8.0,
     'L1_gnn_W_nl1': 8.0,
     'L1_gnn_W_fc1': 8.0,
     'L1_gnn_W_fc2': 7.182,
     'L1_gnn_W_out_s': 8.0,
     'L1_gnn_W_out_v': 8.0}
    for name, (base, spread) in spreads.items():
        noise = np.random.default_rng([zlib.crc32(name.encode()), seed]).standard_normal(out[name].shape)
        drawn = base * np.exp(spread * noise) if base else spread * noise
        out[name] = jnp.asarray(drawn.astype(out[name].dtype))
    for name, factor in factors.items():
        out[name] = (out[name] * factor).astype(out[name].dtype)
    return out
```

```python
from contextlib import ExitStack

import numpy as np

import concourse.bass as bass
from concourse import mybir

F32 = mybir.dt.float32
BF16 = mybir.dt.bfloat16
I32 = mybir.dt.int32
ALU = mybir.AluOpType
ACT = mybir.ActivationFunctionType
AX = mybir.AxisListType

P = 125
T = 4
W = P * T
M0, M1, D = 64, 32, 160
V3 = 3 * M1
EPS = 1e-5

SOURCES = []
OPS = []
UNITS = []
GROUPS = 8
for _g in range(GROUPS):
    _s = len(SOURCES)
    SOURCES += [("z011", _g), ("x0", 4 * _g), ("z101", _g), ("x0", 4 * _g + 1), ("x1", 0, _g),
                ("x0", 4 * _g + 2), ("x1", 1, _g), ("x1", 2, _g), ("x0", 4 * _g + 3)]
    _o = 13 * (_g % 2)

    def _unit(kind, n, k, slot):
        UNITS.append((kind, n, k, _o + slot, len(OPS) - 1, len(SOURCES) - 9 + _need))
    for _k in range(3):
        OPS.append(("mul", _o + _k, _s, "a1", _k))
    OPS.append(("mul", _o + 3, _s + 1, "a0", 0))
    _need = 1
    _unit("w000", 4 * _g, 0, 3)
    for _k in range(3):
        OPS.append(("mul", _o + 4 + _k, _s + 2, "x1", _k))
    _need = 2
    for _k in range(3):
        OPS.append(("add", _o + _k, _o + 4 + _k))
        _unit("sel", _g, _k, _k)
    OPS.append(("mul", _o + 7, _s + 3, "a0", 0))
    _need = 3
    _unit("w000", 4 * _g + 1, 0, 7)
    OPS.append(("mul", _o + 8, _s + 4, "a1", 0))
    OPS.append(("mul", _o + 9, _s + 5, "a0", 0))
    _need = 5
    _unit("w000", 4 * _g + 2, 0, 9)
    OPS.append(("mul", _o + 10, _s + 6, "a1", 1))
    OPS.append(("mul", _o + 12, _s + 7, "a1", 2))
    OPS.append(("add", _o + 8, _o + 10))
    OPS.append(("mul", _o + 11, _s + 8, "a0", 0))
    _need = 8
    _unit("w000", 4 * _g + 3, 0, 11)
    OPS.append(("add", _o + 8, _o + 12))
    _unit("w110", _g, 0, 8)
NS, NO, NU = len(SOURCES), len(OPS), len(UNITS)
LAST = {op[2]: n for n, op in enumerate(OPS) if op[0] == "mul"}
RING = 4
SLOTS = 26

J_IDX, J_X0, J_STK, J_XE, J_S, J_X1, J_A0, J_A1 = 0, 1, 2, 7, 11, 12, 15, 16
NPREP = 19
NSUM = 4
NJOB = NPREP + NSUM


PASSED = []


def ds(start, size):
    return bass.DynSlice(start, size)


def hold(eng, sem, value):
    eng.wait_ge(sem, value)
    eng.sem_inc(PASSED[0], 1)


def build(nc, x, src, dst, edge_attr_3, edge_attr_4, edge_attr_64, wm000, wm011, wm101, wm110, lm0, lm1,
          wu000, wu011, wu101, wu110, lu0, lu1, w_skip0, w_skip1, w_nl0, w_nl1, w_fc1, w_fc2,
          w_out_s, w_out_v, out):
    N, E = x.shape[0], src.shape[0]
    RN, RE = N // P, E // P
    NBN, NB = RN // T, RE // T
    assert N == P * T * NBN and E == P * T * NB and NB % 2 == 0 and NB >= 4 and NBN % 2 == 0

    upd = nc.dram_tensor("upd", (N + P, D), F32, kind="Internal").ap()
    agg = nc.dram_tensor("agg", (N + P, 2 * V3), F32, kind="Internal").ap()

    src_v = src.rearrange("(p c) -> p c", p=P)
    dst_v = dst.rearrange("(p c) -> p c", p=P)
    ea4_v = edge_attr_4.rearrange("(p c) f -> p (c f)", p=P)
    ea3_v = edge_attr_3.rearrange("(p c) f -> p (c f)", p=P)
    ef_v = edge_attr_64.rearrange("(p c) f -> p (c f)", p=P)
    x_v = x.rearrange("(p c) f -> p (c f)", p=P)
    out_v = out.rearrange("(p c) f -> p (c f)", p=P)
    upd_v = upd[0:N, :].rearrange("(p c) f -> p (c f)", p=P)
    agg_v = agg[0:N, :].rearrange("(p c) f -> p (c f)", p=P)

    top = ExitStack()

    def tools(ctx):
        def sb(name, shape, dt=F32):
            return ctx.enter_context(nc.sbuf_tensor(name, shape, dt))

        def bank(name, dt=F32):
            return ctx.enter_context(nc.psum_tensor(name, [128, 2048 // (4 if dt == F32 else 2)], dt))

        def sem(name):
            return ctx.enter_context(nc.semaphore(name))
        return sb, bank, sem

    with top:
        sb, bank, sem = tools(top)
        PASSED[:] = [sem("passed")]
        ident = sb("ident", [128, 128])
        identb = sb("identb", [128, 128], BF16)
        lower = sb("lower", [128, P])
        spare = sb("spare", [128, 1])
        zero = sb("zero", [128, T * D])
        lin_a = sb("lin_a", [128, D])
        lin_b = sb("lin_b", [32, D])
        nl0d = sb("nl0d", [M0, 128])
        nl1e = sb("nl1e", [V3, 3, V3])
        fc1 = sb("fc1", [M0, 64])
        fc2a = sb("fc2a", [64, 128])
        fc2e = sb("fc2e", [64, 3, 3, M1])
        wo_a = sb("wo_a", [128, 128])
        wo_s = sb("wo_s", [V3, V3])
        wo_v = sb("wo_v", [V3, 2, M1, 3])
        skip0 = sb("skip0", [M0, V3])
        skip1 = sb("skip1", [V3, M1, 3])

        with ExitStack() as c0:
            sb0, _, sem0 = tools(c0)
            k_in = sb0("k_in", [V3, 6])
            k_out = sb0("k_out", [V3, 3])
            lu0_s = sb0("lu0_s", [M0, M0])
            lu1_r = sb0("lu1_r", [V3, M1])
            nl1_r = sb0("nl1_r", [V3, M1])
            sk1_r = sb0("sk1_r", [V3, M1])
            wov_r = sb0("wov_r", [V3, 2, M1])
            lin1e = sb0("lin1e", [V3, M1, 3])
            raw_s = sb0("raw_s", [V3, V3])
            raw_a = sb0("raw_a", [128, 128])
            w_in = sem0("w_in")
            w_on = sem0("w_on")
            c_pool = sem0("c_pool")
            c_vec = sem0("c_vec")
            c_done = sem0("c_done")
            w_mov = sem0("w_mov")
            block = c0.enter_context(nc.Block())

            @block.sync
            def _(sp):
                rows = [(lu0_s[:, :], lu0), (nl0d[:, 0:M0], w_nl0), (nl0d[:, M0:128], w_nl0), (fc1[:, :], w_fc1),
                        (fc2a[:, :], w_fc2[:, 0:128]), (skip0[:, :], w_skip0),
                        (raw_s[0:32, :], w_out_s[64:96, :])]
                rows += [(raw_s[32 * k:32 * k + 32, :], w_out_s[64:96, :]) for k in range(1, 3)]
                rows += [(fc2e[:, j, k, :], w_fc2[:, 128 + 32 * j:160 + 32 * j]) for j in range(3) for k in range(3)]
                for to, of in rows:
                    sp.dma_start(to, of).then_inc(w_in, 16)
                for k in range(3):
                    for j in range(2):
                        sp.dma_start(wov_r[32 * k:32 * k + 32, j, :],
                                     w_out_v[64 + 32 * j:96 + 32 * j, :]).then_inc(w_in, 16)
                    for tile, of in ((lu1_r, lu1), (nl1_r, w_nl1), (sk1_r, w_skip1)):
                        sp.dma_start(tile[k:k + 3 * (M1 - 1) + 1:3, :], of).then_inc(w_in, 16)
                sp.wait_ge(c_pool, 3)
                sp.dma_start(raw_a[64:128, 0:32], w_out_v[0:64, :]).then_inc(w_in, 16)
                sp.dma_start(raw_a[0:64, 32:128], w_out_s[0:64, :]).then_inc(w_in, 16)
                sp.wait_ge(c_done, 2)
                sp.dma_start(lin_a[64:128, 64:160], lin1e[0:64, :, :].rearrange("p m k -> p (m k)")).then_inc(w_mov, 16)
                sp.dma_start(lin_b[:, 64:160], lin1e[64:96, :, :].rearrange("p m k -> p (m k)")).then_inc(w_mov, 16)
                sp.wait_ge(w_mov, 32)

            n_in = 16 * (7 + 2 + 9 + 3 * 5 + 2)

            @block.gpsimd
            def _(pool):
                pool.memset(ident[:, :], 0.0).then_inc(c_pool, 1)
                pool.memset(lower[:, :], 1.0).then_inc(c_pool, 1)
                pool.memset(raw_a[:, :], 0.0).then_inc(c_pool, 1)
                pool.memset(zero[:, :], 0.0).then_inc(c_pool, 1)
                pool.memset(lin_b[:, :], 0.0).then_inc(c_pool, 1)
                pool.wait_ge(c_pool, 5)
                pool.affine_select(out=ident[:, :], in_=ident[:, :], compare_op=ALU.not_equal, fill=1.0, base=0,
                                   pattern=[[-1, 128]], channel_multiplier=1).then_inc(c_pool, 1)
                pool.affine_select(out=lower[:, :], in_=lower[:, :], compare_op=ALU.is_gt, fill=0.0, base=0,
                                   pattern=[[-1, P]], channel_multiplier=1).then_inc(c_pool, 1)
                pool.iota(spare[:, :], pattern=[[0, 1]], base=N, channel_multiplier=1,
                          allow_small_or_imprecise_dtypes=True).then_inc(c_pool, 1)
                pool.wait_ge(c_pool, 8)

            @block.vector
            def _(dve):
                n = [0]

                def step(ins):
                    n[0] += 1
                    ins.then_inc(c_vec, 1)
                    dve.wait_ge(c_vec, n[0])

                dve.wait_ge(c_pool, 8)
                step(dve.tensor_copy(identb[:, :], ident[:, :]))
                step(dve.tensor_reduce(k_in[:, 0:3], ident[0:V3, 0:V3].rearrange("p (m k) -> p k m", k=3), AX.X, ALU.add))
                step(dve.tensor_reduce(k_out[:, :], ident[0:V3, 0:V3].rearrange("p (k m) -> p k m", k=3), AX.X, ALU.add))
                step(dve.tensor_copy(k_in[:, 3:6], k_in[:, 0:3]))
                dve.wait_ge(w_in, n_in)

                def spread(to, rows, mask):
                    return dve.tensor_tensor(to, rows.unsqueeze(2).to_broadcast([V3, M1, 3]),
                                             mask.unsqueeze(1).to_broadcast([V3, M1, 3]), ALU.mult)

                step(spread(lin1e[:, :, :], lu1_r[:, :], k_in[:, 0:3]))
                step(spread(skip1[:, :, :], sk1_r[:, :], k_in[:, 0:3]))
                for j in range(2):
                    step(spread(wo_v[:, j, :, :], wov_r[:, j, :], k_out[:, :]))
                for s in range(3):
                    step(dve.tensor_tensor(nl1e[:, s, :].rearrange("p (k m) -> p k m", k=3),
                                           nl1_r[:, :].unsqueeze(1).to_broadcast([V3, 3, M1]),
                                           k_in[:, s:s + 3].unsqueeze(2).to_broadcast([V3, 3, M1]), ALU.mult))
                step(dve.tensor_scalar(wo_v[:, 0, :, :], wo_v[:, 0, :, :], 1 / 32, None, ALU.mult))
                step(dve.tensor_scalar(wo_v[:, 1, :, :], wo_v[:, 1, :, :], float(np.sqrt(1.5) / 32), None, ALU.mult))
                step(dve.tensor_scalar(wo_s[:, :], raw_s[:, :], 1 / 32, None, ALU.mult))
                step(dve.tensor_scalar(wo_a[:, 32:128], raw_a[:, 32:128], 1 / 32, None, ALU.mult))
                step(dve.tensor_scalar(wo_a[:, 0:32], raw_a[:, 0:32], float(np.sqrt(3.0) / 32), None, ALU.mult))
                step(dve.tensor_scalar(lin1e[:, :, :], lin1e[:, :, :], float(1 / np.sqrt(M1)), None, ALU.mult))
                step(dve.scalar_tensor_tensor(out=lin1e[:, :, :], in0=ident[0:V3, 0:V3].rearrange("p (m k) -> p m k", k=3),
                                              scalar=2.0, in1=lin1e[:, :, :], op0=ALU.mult, op1=ALU.add))
                step(dve.memset(lin_a[:, :], 0.0))
                step(dve.tensor_scalar(lu0_s[:, :], lu0_s[:, :], float(1 / np.sqrt(M0)), None, ALU.mult))
                dve.scalar_tensor_tensor(out=lin_a[0:M0, 0:M0], in0=ident[0:M0, 0:M0], scalar=2.0, in1=lu0_s[:, :],
                                         op0=ALU.mult, op1=ALU.add).then_inc(c_done, 2)

        layer0_edges(nc, tools, x, upd, agg, upd_v, agg_v, src_v, dst_v, ea4_v, N, NB, RN,
                     ident, identb, lower, spare, zero,
                     (wm000, wm011, wm101, wm110, lm0, lm1, wu000, wu011, wu101, wu110))
        layer1_edges(nc, tools, x, upd, agg, src_v, dst_v, ea3_v, ef_v, N, NB, ident, lower, spare,
                     (lin_a, lin_b, nl0d, nl1e, fc1, fc2a, fc2e, wo_a, wo_s, wo_v))
        nodes(nc, tools, x_v, upd_v, agg_v, out_v, NBN, ident, lin_a, lin_b, skip0, skip1)


def layer0_edges(nc, tools, x, upd, agg, upd_v, agg_v, src_v, dst_v, ea4_v, N, NB, RN,
                 ident, identb, lower, spare, zero, weights):
    wm000, wm011, wm101, wm110, lm0, lm1, wu000, wu011, wu101, wu110 = weights
    ctx = ExitStack()
    sb, bank, sem = tools(ctx)
    s_tp0 = float(1 / np.sqrt(M0 * M0 + M1 * M1))
    s_tp1 = float(1 / np.sqrt(2 * M0 * M1))
    s_msg = float(1 / np.sqrt(M0 + M1))
    i3 = float(1 / np.sqrt(3.0))

    w000 = sb("w000", [128, 33, M0])
    w110 = sb("w110", [128, 9, M0])
    w011 = sb("w011", [M0, M1, M1])
    w101 = sb("w101", [M0, M1, M1])
    sel_x0 = sb("sel_x0", [V3, 2 * M1 // 4 * 128], BF16)
    sel_x1 = sb("sel_x1", [V3, 8 * 128], BF16)
    sel_rep = sb("sel_rep", [V3, 128], BF16)
    sel_w = sb("sel_w", [128, 2 * V3])
    msg_a = sb("msg_a", [128, 128])
    msg_s = sb("msg_s", [M1, 128])
    msg_k = sb("msg_k", [128, 128])

    with ExitStack() as c1:
        sb1, _, sem1 = tools(c1)
        t011 = sb1("t011", [M0, M1, M1])
        t101 = sb1("t101", [M0, M1, M1])
        w_in = sem1("w_in0")
        done = sem1("w_made0")
        blk = c1.enter_context(nc.Block())

        @blk.sync
        def _(sp):
            sp.dma_start(w000[:, 0:32, :], wu000.rearrange("(c u) v w -> (u v) c w", u=2)).then_inc(w_in, 16)
            sp.dma_start(w110[:, 0:8, :], wu110.rearrange("(c u) v w -> (u v) c w", u=4)).then_inc(w_in, 16)
            sp.dma_start(t011[:, :, :], wu011).then_inc(w_in, 16)
            sp.dma_start(t101[:, :, :], wu101.rearrange("u v w -> v u w")).then_inc(w_in, 16)
            for j in range(2):
                c = slice(64 * j, 64 * j + 64)
                sp.dma_start(msg_a[0:64, c], wm000[:, 0, :]).then_inc(w_in, 16)
                sp.dma_start(msg_a[64:128, c], lm0).then_inc(w_in, 16)
                sp.dma_start(msg_s[:, c], wm110[:, 0, :]).then_inc(w_in, 16)
            for j in range(4):
                c = slice(32 * j, 32 * j + 32)
                sp.dma_start(msg_k[0:64, c], wm011[:, 0, :]).then_inc(w_in, 16)
                sp.dma_start(msg_k[64:96, c], wm101[:, 0, :]).then_inc(w_in, 16)
                sp.dma_start(msg_k[96:128, c], lm1).then_inc(w_in, 16)

        @blk.vector
        def _(dve):
            n = [0]

            def step(ins):
                n[0] += 1
                ins.then_inc(done, 1)
                dve.wait_ge(done, n[0])

            for r in range(3):
                rows = slice(32 * r, 32 * r + 32)
                one = identb[rows, rows]
                step(dve.tensor_copy(sel_x0[rows, :].rearrange("p (u v) -> p u v", v=64),
                                     one.unsqueeze(2).to_broadcast([32, 32, 64])))
                step(dve.tensor_copy(sel_x1[rows, :].rearrange("p (u v) -> p u v", v=32),
                                     one.unsqueeze(2).to_broadcast([32, 32, 32])))
                step(dve.tensor_copy(sel_rep[rows, :].rearrange("p (j u) -> p j u", u=32),
                                     one.unsqueeze(1).to_broadcast([32, 4, 32])))
            step(dve.memset(sel_w[:, :], 0.0))
            step(dve.tensor_reduce(sel_w[:, V3:V3 + 4], ident[:, :].rearrange("p (j v) -> p j v", v=32), AX.X, ALU.add))
            step(dve.tensor_scalar(sel_w[:, V3:V3 + 4], sel_w[:, V3:V3 + 4], s_tp1, None, ALU.mult))
            step(dve.memset(w000[:, 32, :], 0.0))
            step(dve.memset(w110[:, 8, :], 0.0))
            dve.wait_ge(w_in, 16 * (4 + 6 + 12))
            step(dve.tensor_scalar(w000[:, 0:32, :], w000[:, 0:32, :], s_tp0, None, ALU.mult))
            step(dve.tensor_scalar(w110[:, 0:8, :], w110[:, 0:8, :], s_tp0 * i3, None, ALU.mult))
            step(dve.tensor_copy(w011[:, :, :], t011[:, :, :].rearrange("u v w -> u w v")))
            step(dve.tensor_copy(w101[:, :, :], t101[:, :, :].rearrange("v u w -> v w u")))
            step(dve.tensor_scalar(msg_a[0:64, :], msg_a[0:64, :], s_msg, None, ALU.mult))
            step(dve.tensor_scalar(msg_a[64:128, :], msg_a[64:128, :], float(1 / np.sqrt(M0)), None, ALU.mult))
            step(dve.tensor_scalar(msg_s[:, :], msg_s[:, :], s_msg * i3, None, ALU.mult))
            step(dve.tensor_scalar(msg_k[0:96, :], msg_k[0:96, :], s_msg, None, ALU.mult))
            step(dve.tensor_scalar(msg_k[96:128, :], msg_k[96:128, :], float(1 / np.sqrt(M1)), None, ALU.mult))

    isrc = sb("isrc", [128, 2, T], I32)
    idst = sb("idst", [128, 2, T], I32)
    ea4 = sb("ea4", [128, 2, T, 4])
    xs = sb("xs", [128, 2, T, D])
    xd = sb("xd", [128, 2, T, D])
    xe = sb("xe", [128, T, 4, 128])
    xpe = sb("xpe", [128, T, M1, 3])
    xsum = sb("xsum", [128, T, M1])
    parts = sb("parts", [128, T, 5, 3, M1], BF16)
    rest = sb("rest", [128, T, 5, M1])
    idxf = sb("idxf", [128, 2, T])
    idxrow = sb("idxrow", [128, T, P])
    eq = sb("eq", [128, 2, T, P])
    dup = sb("dup", [128, T, P])
    cnt = sb("cnt", [128, T])
    later = sb("later", [128, T])
    junk = sb("junk", [128, P])
    gap = sb("gap", [128, T])
    move = sb("move", [128, T])
    rowf = sb("rowf", [128, T])
    row = sb("row", [128, 2, T], I32)
    xeT = sb("xeT", [128, 4, W])
    xsumT = sb("xsumT", [M1, W])
    stk = sb("stk", [V3, 2, 5, W], BF16)
    x0T = sb("x0T", [M0, 2, W])
    a0T = sb("a0T", [128, 2, W])
    a1T = sb("a1T", [128, 2, 3, W])
    x1T = sb("x1T", [128, 2, 3, W])
    prod = sb("prod", [128, SLOTS, W])
    acc0T = sb("acc0T", [M0, W])
    acc1T = sb("acc1T", [V3, W])
    accs = sb("accs", [128, T, D])
    osum = sb("osum", [128, T, D])

    ring = [bank(f"ring{i}") for i in range(RING)]
    acc = ctx.enter_context(nc.psum_tensor("acc", [128, 2, 512], F32))
    small = [bank(f"small{i}") for i in range(2)]

    ld = [sem("ld0_even"), sem("ld0_odd")]
    gat = [sem("gat0_even"), sem("gat0_odd")]
    op_steps = sem("op_steps")
    row_steps = sem("row_steps")
    cnt_ready = sem("cnt_ready")
    idxf_ready = sem("idxf_ready")
    eq_ready = sem("eq_ready")
    job_ready = sem("job_ready")
    job_done = sem("job_done")
    src_ready = sem("src_ready")
    op_done = sem("op_done")
    unit_done = sem("unit_done")
    acc_out = sem("acc_out")
    zeroed = sem("zeroed")
    zeroed_agg = sem("zeroed_agg")
    scat = sem("scat0")
    osum_free = sem("osum_free0")

    def loaded(b, q):
        return (b - q) * 24 + 48

    def gathered(b, q):
        return (b - q) * 64 + 128

    def job_no(b, j):
        return b * NJOB + j

    def sum_no(b, h):
        return (b + 2) * NJOB - NSUM + h

    def made(b, o):
        return (b + 1) * NO + o + 1

    def used(b, u):
        return (b + 1) * NU + u + 1

    block = ctx.enter_context(nc.Block())

    def sweep(eng, main):
        with eng.Fori(0, (NB - 2) // 2) as i:
            main(2 * i + 1, 1)
            main(2 * i + 2, 0)

    @block.sync
    def _(sp):
        def load(b, q):
            sp.dma_start(isrc[0:P, q, :], src_v[:, ds(b * T, T)]).then_inc(ld[q], 16)
            sp.dma_start(idst[0:P, q, :], dst_v[:, ds(b * T, T)]).then_inc(ld[q], 16)
            sp.dma_start(ea4[0:P, q, :, :].rearrange("p t f -> p (t f)"), ea4_v[:, ds(b * 16, 16)]).then_inc(ld[q], 16)

        load(0, 0)
        load(1, 1)
        z = zero[0:P, :].unsqueeze(1)
        sp.dma_start(upd_v.rearrange("p (r f) -> p r f", f=T * D), z.to_broadcast([P, RN // T, T * D])).then_inc(zeroed, 16)
        sp.dma_start(upd[N:N + P, :], zero[0:P, 0:D]).then_inc(zeroed, 16)
        sp.dma_start(agg_v.rearrange("p (r f) -> p r f", f=2 * 2 * V3),
                     zero[0:P, 0:4 * V3].unsqueeze(1).to_broadcast([P, RN // 2, 4 * V3])).then_inc(zeroed_agg, 16)
        sp.dma_start(agg[N:N + P, :], zero[0:P, 0:2 * V3]).then_inc(zeroed_agg, 16)

        def loads(b, q):
            sp.wait_ge(op_steps, b * 16)
            sp.wait_ge(row_steps, b * 6 + 1)
            load(b + 1, 1 - q)
        sweep(sp, loads)
        sp.wait_ge(zeroed_agg, 32)

    @block.gpsimd
    def _(pool):
        def gather(b, q, first=False):
            hold(pool, ld[q], loaded(b, q))
            if not first:
                hold(pool, job_ready, job_no(b - 2, J_X0) + 1)
            for t in range(T):
                pool.indirect_dma_start(xs[0:P, q, t, :], None, x,
                                        bass.IndirectOffsetOnAxis(ap=isrc[0:P, q, t:t + 1], axis=0)).then_inc(gat[q], 16)
            for t in range(T):
                pool.indirect_dma_start(xd[0:P, q, t, :], None, x,
                                        bass.IndirectOffsetOnAxis(ap=idst[0:P, q, t:t + 1], axis=0)).then_inc(gat[q], 16)

        def operands(b, q, first=False):
            hold(pool, gat[q], gathered(b, q))
            if not first:
                hold(pool, job_ready, job_no(b - 1, J_S) + 1)
            s0 = xs[0:P, q, :, 0:M0].rearrange("p t (s u) -> p t s u", u=M1)
            s1 = xs[0:P, q, :, M0:D].rearrange("p t (u k) -> p t k u", k=3)
            pool.tensor_copy(parts[0:P, :, 0:2, 0, :], s0).then_inc(op_steps, 1)
            pool.tensor_copy(parts[0:P, :, 2:5, 0, :], s1).then_inc(op_steps, 1)
            hold(pool, op_steps, b * 16 + 2)
            pool.tensor_tensor(rest[0:P, :, 0:2, :], s0, parts[0:P, :, 0:2, 0, :], ALU.subtract).then_inc(op_steps, 1)
            pool.tensor_tensor(rest[0:P, :, 2:5, :], s1, parts[0:P, :, 2:5, 0, :], ALU.subtract).then_inc(op_steps, 1)
            hold(pool, op_steps, b * 16 + 4)
            pool.tensor_copy(parts[0:P, :, :, 1, :], rest[0:P, :, :, :]).then_inc(op_steps, 1)
            hold(pool, op_steps, b * 16 + 5)
            pool.tensor_tensor(parts[0:P, :, :, 2, :], rest[0:P, :, :, :], parts[0:P, :, :, 1, :],
                               ALU.subtract).then_inc(op_steps, 1)
            d0 = xd[0:P, q, :, 0:M0]
            d1 = xd[0:P, q, :, M0:D].rearrange("p t (u k) -> p t u k", k=3)
            d1k = xd[0:P, q, :, M0:D].rearrange("p t (u k) -> p t k u", k=3)
            e1 = ea4[0:P, q, :, 0:3]
            e0 = ea4[0:P, q, :, 3:4]
            pool.tensor_tensor(xpe[0:P, :, :, :], d1, e1.unsqueeze(2).to_broadcast([P, T, M1, 3]), ALU.mult).then_inc(op_steps, 1)
            pool.tensor_tensor(xe[0:P, :, 0, 0:64], d0, e0.to_broadcast([P, T, M0]), ALU.mult).then_inc(op_steps, 1)
            pool.tensor_copy(xe[0:P, :, 0, 64:128], d0).then_inc(op_steps, 1)
            for k in range(3):
                pool.tensor_tensor(xe[0:P, :, 1 + k, 0:64], d0, e1[:, :, k:k + 1].to_broadcast([P, T, M0]),
                                   ALU.mult).then_inc(op_steps, 1)
            pool.tensor_tensor(xe[0:P, :, 1:4, 64:96], d1k, e0.unsqueeze(3).to_broadcast([P, T, 3, M1]),
                               ALU.mult).then_inc(op_steps, 1)
            pool.tensor_copy(xe[0:P, :, 1:4, 96:128], d1k).then_inc(op_steps, 1)
            hold(pool, op_steps, b * 16 + 14)
            pool.tensor_tensor(xsum[0:P, :, :], xpe[0:P, :, :, 0], xpe[0:P, :, :, 1], ALU.add).then_inc(op_steps, 1)
            hold(pool, op_steps, b * 16 + 15)
            pool.tensor_tensor(xsum[0:P, :, :], xsum[0:P, :, :], xpe[0:P, :, :, 2], ALU.add).then_inc(op_steps, 1)

        def rows_of(b, q):
            hold(pool, eq_ready, b + 1)
            n = b * 6 + 1
            pool.tensor_tensor(dup[0:P, :, :], eq[0:P, q, :, :], lower[0:P, :].unsqueeze(1).to_broadcast([P, T, P]),
                               ALU.mult).then_inc(row_steps, 1)
            pool.tensor_tensor(gap[0:P, :], spare[0:P, :].to_broadcast([P, T]), idxf[0:P, q, :],
                               ALU.subtract).then_inc(row_steps, 1)
            hold(pool, row_steps, n + 2)
            hold(pool, cnt_ready, b * T + T)
            pool.tensor_scalar(later[0:P, :], cnt[0:P, :], 1.0, None, ALU.min).then_inc(row_steps, 1)
            hold(pool, row_steps, n + 3)
            pool.tensor_tensor(move[0:P, :], later[0:P, :], gap[0:P, :], ALU.mult).then_inc(row_steps, 1)
            hold(pool, row_steps, n + 4)
            pool.tensor_tensor(rowf[0:P, :], move[0:P, :], idxf[0:P, q, :], ALU.add).then_inc(row_steps, 1)
            hold(pool, row_steps, n + 5)
            pool.tensor_copy(row[0:P, q, :], rowf[0:P, :]).then_inc(row_steps, 1)

        def scatter(b, q):
            hold(pool, row_steps, b * 6 + 7)
            hold(pool, job_done, sum_no(b, 3) + 1)
            for t in range(T):
                pool.indirect_dma_start(upd, bass.IndirectOffsetOnAxis(ap=row[0:P, q, t:t + 1], axis=0),
                                        osum[0:P, t, :], None, compute_op=ALU.add).then_inc(scat, 16)
                hold(pool, scat, b * 64 + t * 16 + 16)
            pool.sem_inc(osum_free, 1)

        def main(b, q):
            gather(b + 1, 1 - q)
            rows_of(b, q)
            scatter(b - 1, 1 - q)
            operands(b + 1, 1 - q)

        pool.sem_inc(row_steps, 1)
        pool.sem_inc(osum_free, 1)
        gather(0, 0, first=True)
        operands(0, 0, first=True)
        gather(1, 1, first=True)
        rows_of(0, 0)
        operands(1, 1)
        pool.wait_ge(zeroed, 32)
        sweep(pool, main)
        rows_of(NB - 1, 1)
        scatter(NB - 2, 0)
        scatter(NB - 1, 1)

    @block.tensor
    def _(pe):
        def job_bank(b, q, j):
            return small[(q + j) % 2]

        def free(n):
            hold(pe, job_done, n - 1)

        def turn(bank_, srcs, K, ops, is_bf16=False):
            out_ = bank_[0:K, 0:512] if not is_bf16 else bank_[0:K, 0:256].bitcast(BF16)
            step = 128 if is_bf16 else P
            for t in range(T):
                m = pe.transpose(out_[:, t * step:t * step + P], srcs(t), ops[0:P, 0:P])
            return m

        def prep(b, q, j, first=False):
            bk = job_bank(b, q, j)
            n = job_no(b, j)
            if not (first and j < 2):
                free(n)
            if j == J_IDX:
                hold(pe, idxf_ready, b + 1)
                m = turn(bk, lambda t: idxf[0:P, q, t:t + 1].to_broadcast([P, P]), P, ident)
            elif j == J_X0:
                hold(pe, gat[q], gathered(b, q))
                m = turn(bk, lambda t: xs[0:P, q, t, 0:M0], M0, ident)
            elif J_STK <= j < J_STK + 5:
                hold(pe, op_steps, b * 16 + 6)
                m = turn(bk, lambda t: parts[0:P, t, j - J_STK, :, :].rearrange("p a u -> p (a u)"), V3, identb, True)
            elif J_XE <= j < J_XE + 4:
                hold(pe, op_steps, b * 16 + 16)
                m = turn(bk, lambda t: xe[0:P, t, j - J_XE, :], 128, ident)
            elif j == J_S:
                m = turn(bk, lambda t: xsum[0:P, t, :], M1, ident)
            elif J_X1 <= j < J_X1 + 3:
                k = j - J_X1
                hold(pe, job_done, job_no(b, J_STK + 4) + 1)
                m = pe.matmul(bk[:, 0:W], sel_rep[:, :], stk[:, q, 2 + k, :], start=True, stop=True)
            elif j == J_A0:
                hold(pe, job_done, job_no(b, J_S) + 1)
                pe.matmul(bk[:, 0:W], msg_a[:, :], xeT[:, 0, :], start=True, stop=False)
                m = pe.matmul(bk[:, 0:W], msg_s[:, :], xsumT[:, :], start=False, stop=True)
            else:
                m = pe.matmul(bk[:, 0:W], msg_k[:, :], xeT[:, 1 + j - J_A1, :], start=True, stop=True)
            m.then_inc(job_ready, 1)

        def sums(b, q, h):
            free(sum_no(b, h))
            bk = small[(q + h) % 2]
            if h < 2:
                hold(pe, acc_out, b * 2 + 4)
            else:
                hold(pe, job_done, sum_no(b, 1) + 1)
                hold(pe, eq_ready, b + 1)
            for i in range(2):
                t = 2 * (h % 2) + i
                o = bk[0:P, i * D:(i + 1) * D]
                if h < 2:
                    pe.transpose(o[:, 0:M0], acc0T[:, t * P:(t + 1) * P], ident[0:M0, 0:M0])
                    m = pe.transpose(o[:, M0:D].rearrange("p (w k) -> p k w", k=3), acc1T[:, t * P:(t + 1) * P],
                                     ident[0:V3, 0:V3])
                else:
                    m = pe.matmul(o, eq[0:P, q, t, :], accs[0:P, t, :], start=True, stop=True)
            m.then_inc(job_ready, 1)

        def source(b, q, s):
            src = SOURCES[s]
            last = LAST[s - RING] if s >= RING else LAST[s - RING + NS] - NO
            pe.wait_ge(op_done, made(b, last))
            o = ring[s % RING][:, 0:W]
            if src[0] == "x0":
                c = src[1]
                m = pe.matmul(o, sel_x0[:, (c % 16) * 128:(c % 16 + 1) * 128], stk[:, q, c // 16, :], start=True, stop=True)
            elif src[0] == "x1":
                m = pe.matmul(o, sel_x1[:, src[2] * 128:(src[2] + 1) * 128], stk[:, q, 2 + src[1], :], start=True, stop=True)
            elif src[0] == "z011":
                m = pe.matmul(o, w011[:, 4 * src[1]:4 * src[1] + 4, :].rearrange("u w v -> u (w v)"), x0T[:, q, :],
                              start=True, stop=True)
            else:
                m = pe.matmul(o, w101[:, 4 * src[1]:4 * src[1] + 4, :].rearrange("v w u -> v (w u)"), a0T[0:M0, q, :],
                              start=True, stop=True)
            m.then_inc(src_ready, 1)

        first0, last0 = min(u for u in range(NU) if UNITS[u][0] != "sel"), max(u for u in range(NU) if UNITS[u][0] != "sel")
        first1, last1 = min(u for u in range(NU) if UNITS[u][0] == "sel"), max(u for u in range(NU) if UNITS[u][0] == "sel")

        def contract(b, u):
            kind, n, k, slot, op, _ = UNITS[u]
            pe.wait_ge(op_done, made(b, op))
            if kind == "sel":
                at = V3 - (32 * k + 4 * n)
                m = pe.matmul(acc[0:V3, 1, 0:W], sel_w[:, at:at + V3], prod[:, slot, :], start=(u == first1), stop=(u == last1))
            else:
                w = w000 if kind == "w000" else w110
                m = pe.matmul(acc[:, 0, 0:W], w[:, n:n + 2, :].rearrange("p c w -> p (c w)"), prod[:, slot, :],
                              start=(u == first0), stop=(u == last0))
            m.then_inc(unit_done, 1)

        def main(b, q, with_sums=True, with_prep=True):
            jobs = {}
            if with_sums:
                for h in range(NSUM):
                    jobs[3 + 3 * h] = lambda h=h: sums(b - 1, 1 - q, h)
            if with_prep:
                jobs[14] = lambda: prep(b + 1, 1 - q, 0)
                jobs[16] = lambda: prep(b + 1, 1 - q, 1)
                for j in range(2, NPREP):
                    at = 28 + (j - 2) * 5 // 2
                    jobs[at] = lambda j=j: prep(b + 1, 1 - q, j)
                assert at < NS - 1
            pe.wait_ge(job_done, job_no(b, J_A0) + 1)
            done = 0
            for s in range(NS + 3):
                if s < NS:
                    source(b, q, s)
                if s == 3:
                    pe.wait_ge(acc_out, b * 2 + 2)
                while done < NU and UNITS[done][5] <= s - 2:
                    contract(b, done)
                    done += 1
                if s in jobs:
                    jobs[s]()
            assert done == NU

        pe.sem_inc(unit_done, NU)
        for j in range(NPREP):
            prep(0, 0, j, first=True)
        pe.wait_ge(job_ready, NPREP)
        pe.sem_inc(job_ready, NSUM)
        main(0, 0, with_sums=False)
        sweep(pe, main)
        main(NB - 1, 1, with_prep=False)
        pe.wait_ge(job_ready, NB * NJOB)
        pe.sem_inc(job_ready, NPREP)
        for h in range(NSUM):
            sums(NB - 1, 1, h)

    @block.vector
    def _(dve):
        def index(b, q):
            dve.wait_ge(ld[q], loaded(b, q))
            dve.tensor_copy(idxf[0:P, q, :], isrc[0:P, q, :]).then_inc(idxf_ready, 1)

        def equal(b, q, first=False):
            dve.wait_ge(job_done, job_no(b, J_IDX) + 1)
            if not first:
                dve.wait_ge(job_ready, sum_no(b - 2, 3) + 1)
                dve.wait_ge(row_steps, (b - 1) * 6 + 1)
            dve.tensor_tensor(eq[0:P, q, :, :], idxrow[0:P, :, :], idxf[0:P, q, :].unsqueeze(2).to_broadcast([P, T, P]),
                              ALU.is_equal).then_inc(eq_ready, 1)

        def main(b, q, first=False, more=True):
            dve.wait_ge(job_done, job_no(b, NPREP - 1) + 1)
            at = None
            for n, op in enumerate(OPS):
                if n % (NO // GROUPS) == 0:
                    dve.wait_ge(unit_done, used(b, (n // (NO // GROUPS) - 1) * (NU // GROUPS) - 1))
                if op[0] == "add":
                    dve.wait_ge(op_done, made(b, max(m for m in range(n) if OPS[m][1] in op[1:3])))
                    dve.tensor_tensor(prod[:, op[1], :], prod[:, op[1], :], prod[:, op[2], :], ALU.add).then_inc(op_done, 1)
                else:
                    if op[2] != at:
                        at = op[2]
                        dve.wait_ge(src_ready, b * NS + at + 1)
                    by = {"a0": a0T[:, q, :], "a1": a1T[:, q, op[4], :], "x1": x1T[:, q, op[4], :]}[op[3]]
                    dve.tensor_tensor(prod[:, op[1], :], ring[at % RING][:, 0:W], by, ALU.mult).then_inc(op_done, 1)
                if n == 3 and not first:
                    equal(b, q)
                if n == 7 and more:
                    dve.wait_ge(row_steps, b * 6 + 1)
                    index(b + 1, 1 - q)

        dve.sem_inc(op_done, NO)
        index(0, 0)
        equal(0, 0, first=True)
        main(0, 0, first=True)
        sweep(dve, main)
        main(NB - 1, 1, more=False)

    @block.scalar
    def _(act):
        def prep(b, q, j, first=False):
            act.wait_ge(job_ready, job_no(b, j) + 1)
            bk = small[(q + j) % 2]
            if j == J_IDX:
                if not first:
                    act.wait_ge(eq_ready, b)
                to, of = idxrow[0:P, :, :].rearrange("p t e -> p (t e)"), bk[0:P, 0:W]
            elif j == J_X0:
                if not first:
                    act.wait_ge(op_done, made(b - 2, NO - 1))
                to, of = x0T[:, q, :], bk[0:M0, 0:W]
            elif J_STK <= j < J_STK + 5:
                to = stk[:, q, j - J_STK, :].rearrange("p (t e) -> p t e", t=T)
                of = bk[0:V3, 0:256].bitcast(BF16).rearrange("p (t e) -> p t e", t=T)[:, :, 0:P]
            elif J_XE <= j < J_XE + 4:
                to, of = xeT[:, j - J_XE, :], bk[:, 0:W]
            elif j == J_S:
                to, of = xsumT[:, :], bk[0:M1, 0:W]
            elif J_X1 <= j < J_X1 + 3:
                to, of = x1T[:, q, j - J_X1, :], bk[:, 0:W]
            elif j == J_A0:
                to, of = a0T[:, q, :], bk[:, 0:W]
            else:
                to, of = a1T[:, q, j - J_A1, :], bk[:, 0:W]
            act.activation(to, of, ACT.Copy).then_inc(job_done, 1)

        def updates(b):
            act.wait_ge(unit_done, used(b, NU - 1))
            act.activation(acc0T[:, :], acc[0:M0, 0, 0:W], ACT.Copy).then_inc(acc_out, 1)
            act.activation(acc1T[:, :], acc[0:V3, 1, 0:W], ACT.Copy).then_inc(acc_out, 1)

        def sums(b, q):
            act.wait_ge(osum_free, b + 1)
            for h in range(NSUM):
                act.wait_ge(job_ready, sum_no(b, h) + 1)
                to, t = accs if h < 2 else osum, 2 * (h % 2)
                act.activation(to[0:P, t:t + 2, :].rearrange("p t f -> p (t f)"),
                               small[(q + h) % 2][0:P, 0:2 * D], ACT.Copy).then_inc(job_done, 1)

        def count(b):
            act.wait_ge(row_steps, b * 6 + 2)
            for t in range(T):
                if t:
                    act.wait_ge(cnt_ready, b * T + t)
                act.activation(junk[0:P, :], dup[0:P, t, :], ACT.Copy, accum_out=cnt[0:P, t:t + 1]).then_inc(cnt_ready, 1)

        def main(b, q):
            updates(b - 1)
            sums(b - 1, 1 - q)
            count(b)
            for j in range(NPREP):
                prep(b + 1, 1 - q, j)

        act.sem_inc(acc_out, 2)
        for j in range(NPREP):
            prep(0, 0, j, first=True)
        act.wait_ge(job_done, NPREP)
        act.sem_inc(job_done, NSUM)
        count(0)
        for j in range(NPREP):
            prep(1, 1, j)
        sweep(act, main)
        updates(NB - 2)
        sums(NB - 2, 0)
        count(NB - 1)
        act.wait_ge(job_done, NB * NJOB)
        act.sem_inc(job_done, NPREP)
        updates(NB - 1)
        sums(NB - 1, 1)

    ctx.close()


def layer1_edges(nc, tools, x, upd, agg, src_v, dst_v, ea3_v, ef_v, N, NB, ident, lower, spare, weights):
    lin_a, lin_b, nl0d, nl1e, fc1, fc2a, fc2e, wo_a, wo_s, wo_v = weights
    ctx = ExitStack()
    sb, bank, sem = tools(ctx)
    RE = NB * T
    G = 2 * V3

    rhat = sb("rhat", [128, RE, 3])
    eps = sb("eps1", [128, 1])

    with ExitStack() as c1:
        sb1, _, sem1 = tools(c1)
        ea3 = sb1("ea3", [128, RE, 3])
        sq = sb1("sq", [128, RE, 3])
        nrm = sb1("nrm", [128, RE])
        inv = sb1("inv", [128, RE])
        a_in = sem1("a_in")
        r_steps = sem1("r_steps")
        blk = c1.enter_context(nc.Block())

        @blk.sync
        def _(sp):
            sp.dma_start(ea3[0:P, :, :].rearrange("p c f -> p (c f)"), ea3_v).then_inc(a_in, 16)

        @blk.scalar
        def _(act):
            act.wait_ge(r_steps, 3)
            act.activation(nrm[0:P, :], nrm[0:P, :], ACT.Sqrt).then_inc(r_steps, 1)

        @blk.vector
        def _(dve):
            dve.memset(eps[:, :], EPS).then_inc(r_steps, 1)
            dve.wait_ge(a_in, 16)
            dve.tensor_tensor(sq[0:P, :, :], ea3[0:P, :, :], ea3[0:P, :, :], ALU.mult).then_inc(r_steps, 1)
            dve.wait_ge(r_steps, 2)
            dve.tensor_reduce(nrm[0:P, :], sq[0:P, :, :], AX.X, ALU.add).then_inc(r_steps, 1)
            dve.wait_ge(r_steps, 4)
            dve.reciprocal(inv[0:P, :], nrm[0:P, :]).then_inc(r_steps, 1)
            dve.wait_ge(r_steps, 5)
            dve.tensor_tensor(rhat[0:P, :, :], ea3[0:P, :, :], inv[0:P, :].unsqueeze(2).to_broadcast([P, RE, 3]),
                              ALU.mult).then_inc(r_steps, 1)

    isrc = sb("isrc1", [128, 2, T], I32)
    idst = sb("idst1", [128, 2, T], I32)
    ef = sb("ef", [128, 2, T, 64])
    xg = sb("xg", [128, 2, T, D])
    ug = sb("ug", [128, 2, T, D])
    rh6 = sb("rh6", [128, 2, T, 6])
    rh3 = sb("rh3", [128, T, 3, 3, M1])
    idxf = sb("idxf1", [128, 2, T])
    idxrow = sb("idxrow1", [128, T, P])
    eq = sb("eq1", [128, 2, T, P])
    dup = sb("dup1", [128, T, P])
    cnt = sb("cnt1", [128, T])
    later = sb("later1", [128, T])
    junk = sb("junk1", [128, P])
    gap = sb("gap1", [128, T])
    move = sb("move1", [128, T])
    rowf = sb("rowf1", [128, T])
    row = sb("row1", [128, 2, T], I32)
    xaT = sb("xaT", [128, W])
    xbT = sb("xbT", [M1, W])
    efT = sb("efT", [64, W])
    hT = sb("hT", [64, W])
    shT = sb("shT", [V3, 2, 3, W])
    w01T = sb("w01T", [128, 2, W])
    w234T = sb("w234T", [V3, 2, 3, W])
    y = sb("y1", [128, T, D])
    st = sb("st1", [128, T, 6])
    mv = sb("mv1", [128, T, 2])
    std = sb("std1", [128, T])
    rstd = sb("rstd1", [128, T])
    x1n = sb("x1n1", [128, T, D])
    n0T = sb("n0T", [M0, W])
    n1T = sb("n1T", [V3, W])
    tA = sb("tA", [128, W])
    t2 = sb("t2", [V3, W])
    b3 = sb("b3", [V3, W])
    t3 = sb("t3", [V3, W])
    c1_ = sb("c1_", [V3, W])
    c2_ = sb("c2_", [V3, W])
    c3_ = sb("c3_", [V3, W])
    t4 = sb("t4", [V3, W])
    qr = sb("qr", [128, T, M1, 3])
    o = sb("o1", [128, T, G])
    osum = sb("osum1", [128, T, G])

    abank = [bank(f"abank{i}") for i in range(4)]
    dbank = [bank(f"dbank{i}") for i in range(4)]

    ld = [sem("ld1_even"), sem("ld1_odd")]
    gat = [sem("gat1_even"), sem("gat1_odd")]
    a_ready = sem("a_ready1")
    a_done = sem("a_done1")
    d_ready = sem("d_ready1")
    d_done = sem("d_done1")
    rh_steps = sem("rh_steps")
    row_steps = sem("row_steps1")
    cnt_ready = sem("cnt_ready1")
    idxf_ready = sem("idxf_ready1")
    eq_ready = sem("eq_ready1")
    prods = sem("prods1")
    o_steps = sem("o_steps")
    ln_steps = sem("ln_steps1")
    std_ready = sem("std_ready1")
    x1n_ready = sem("x1n_ready1")
    scat = sem("scat1")
    osum_free = sem("osum_free1")

    A_SUM, A_XT, A_IN, A_FC1, A_W = 0, 2, 4, 11, 12
    D_V, D_Y, D_OUT = 0, 4, 6

    def aj(b, j):
        return (b + 1) * 16 + j

    def dj(b, j):
        return (b + 1) * 8 + j

    def loaded(b, q):
        return (b - q) * 24 + 48

    def gathered(b, q):
        return (b - q) * 64 + 128

    def sweep(eng, iteration):
        iteration(0, 0, True, True)
        with eng.Fori(0, (NB - 4) // 2) as i:
            iteration(2 * i + 1, 1, True, True)
            iteration(2 * i + 2, 0, True, True)
        iteration(NB - 3, 1, True, True)
        iteration(NB - 2, 0, True, False)
        iteration(NB - 1, 1, False, False)

    block = ctx.enter_context(nc.Block())

    @block.sync
    def _(sp):
        def load(b, q):
            sp.dma_start(isrc[0:P, q, :], src_v[:, ds(b * T, T)]).then_inc(ld[q], 16)
            sp.dma_start(idst[0:P, q, :], dst_v[:, ds(b * T, T)]).then_inc(ld[q], 16)
            sp.dma_start(ef[0:P, q, :, :].rearrange("p t f -> p (t f)"), ef_v[:, ds(b * T * 64, T * 64)]).then_inc(ld[q], 16)

        def iteration(b, q, more, more2):
            if more2:
                sp.wait_ge(idxf_ready, b + 1)
                sp.wait_ge(a_ready, aj(b - 1, A_IN + 2) + 1)
                load(b + 2, q)

        load(0, 0)
        load(1, 1)
        sweep(sp, iteration)

    @block.gpsimd
    def _(pool):
        def gather(b, q, first=False):
            hold(pool, ld[q], loaded(b, q))
            if not first:
                hold(pool, a_ready, aj(b - 3, A_IN + 1) + 1)
                hold(pool, d_done, dj(b - 3, D_Y + 1) + 1)
            for t in range(T):
                at = bass.IndirectOffsetOnAxis(ap=idst[0:P, q, t:t + 1], axis=0)
                pool.indirect_dma_start(xg[0:P, q, t, :], None, x, at).then_inc(gat[q], 16)
                pool.indirect_dma_start(ug[0:P, q, t, :], None, upd, at).then_inc(gat[q], 16)

        def units(b, q, first=False, second=False):
            if not (first or second):
                hold(pool, d_done, dj(b - 2, D_OUT + 1) + 1)
            if not first:
                hold(pool, a_ready, aj(b - 2, A_IN + 6) + 1)
            for j in range(2):
                pool.tensor_copy(rh6[0:P, q, :, 3 * j:3 * j + 3], rhat[0:P, ds(b * T, T), :]).then_inc(rh_steps, 1)
            hold(pool, rh_steps, b * 5 + 2)
            for s in range(3):
                pool.tensor_copy(rh3[0:P, :, s, :, :], rh6[0:P, q, :, s:s + 3].unsqueeze(3).to_broadcast([P, T, 3, M1]))\
                    .then_inc(rh_steps, 1)

        def rows_of(b, q):
            hold(pool, eq_ready, b + 1)
            n = b * 6 + 1
            pool.tensor_tensor(dup[0:P, :, :], eq[0:P, q, :, :], lower[0:P, :].unsqueeze(1).to_broadcast([P, T, P]),
                               ALU.mult).then_inc(row_steps, 1)
            pool.tensor_tensor(gap[0:P, :], spare[0:P, :].to_broadcast([P, T]), idxf[0:P, q, :],
                               ALU.subtract).then_inc(row_steps, 1)
            hold(pool, row_steps, n + 2)
            hold(pool, cnt_ready, b * T + T)
            pool.tensor_scalar(later[0:P, :], cnt[0:P, :], 1.0, None, ALU.min).then_inc(row_steps, 1)
            hold(pool, row_steps, n + 3)
            pool.tensor_tensor(move[0:P, :], later[0:P, :], gap[0:P, :], ALU.mult).then_inc(row_steps, 1)
            hold(pool, row_steps, n + 4)
            pool.tensor_tensor(rowf[0:P, :], move[0:P, :], idxf[0:P, q, :], ALU.add).then_inc(row_steps, 1)
            hold(pool, row_steps, n + 5)
            pool.tensor_copy(row[0:P, q, :], rowf[0:P, :]).then_inc(row_steps, 1)

        def scatter(b, q):
            hold(pool, row_steps, b * 6 + 7)
            hold(pool, a_done, aj(b + 1, A_SUM + 1) + 1)
            for t in range(T):
                pool.indirect_dma_start(agg, bass.IndirectOffsetOnAxis(ap=row[0:P, q, t:t + 1], axis=0),
                                        osum[0:P, t, :], None, compute_op=ALU.add).then_inc(scat, 16)
                hold(pool, scat, b * 64 + t * 16 + 16)
            pool.sem_inc(osum_free, 1)

        def iteration(b, q, more, more2):
            if more2:
                gather(b + 2, q)
            rows_of(b, q)
            if not (isinstance(b, int) and b == 0):
                scatter(b - 1, 1 - q)
            if more2:
                units(b + 2, q)

        pool.sem_inc(row_steps, 1)
        pool.sem_inc(osum_free, 1)
        gather(0, 0, first=True)
        units(0, 0, first=True)
        gather(1, 1, first=True)
        units(1, 1, second=True)
        sweep(pool, iteration)
        scatter(NB - 1, 1)

    @block.tensor
    def _(pe):
        def turn(o_, tiles, K, n_=P):
            for t in range(T):
                m = pe.transpose(o_[0:K, t * P:(t + 1) * P], tiles(t), ident[0:P, 0:P])
            m.then_inc(a_ready, 1)

        def abk(b, j):
            hold(pe, a_done, aj(b, j) - 3)
            return abank[j % 4]

        def dbk(b, j):
            hold(pe, d_done, dj(b, j) - 3)
            return dbank[j % 4]

        def inputs(b, q):
            i = b - 1
            hold(pe, gat[q], gathered(b, q))
            turn(abk(i, A_IN), lambda t: xg[0:P, q, t, 0:128], 128)
            turn(abk(i, A_IN + 1), lambda t: xg[0:P, q, t, 128:D], M1)
            hold(pe, ld[q], loaded(b, q))
            turn(abk(i, A_IN + 2), lambda t: ef[0:P, q, t, :], 64)
            hold(pe, idxf_ready, b + 1)
            turn(abk(i, A_IN + 3), lambda t: idxf[0:P, q, t:t + 1].to_broadcast([P, P]), P)
            hold(pe, rh_steps, b * 5 + 5)
            for s in range(3):
                turn(abk(i, A_IN + 4 + s), lambda t: rh3[0:P, t, s, :, :].rearrange("p k m -> p (k m)"), V3)
            bk = abk(i, A_FC1)
            hold(pe, a_done, aj(i, A_IN + 2) + 1)
            pe.matmul(bk[0:64, 0:W], fc1[:, :], efT[:, :], start=True, stop=True).then_inc(a_ready, 1)

        def node_y(b):
            i = b - 1
            pe.wait_ge(a_done, aj(i, A_IN + 1) + 1)
            for h in range(2):
                bk = dbk(i, D_Y + h)
                for j in range(2):
                    cols = slice((2 * h + j) * P, (2 * h + j + 1) * P)
                    oo = bk[0:P, j * D:(j + 1) * D]
                    pe.matmul(oo, xaT[:, cols], lin_a[:, :], start=True, stop=False)
                    m = pe.matmul(oo, xbT[:, cols], lin_b[:, :], start=False, stop=True)
                m.then_inc(d_ready, 1)

        def edge_w(b):
            i = b - 1
            pe.wait_ge(a_done, aj(i, A_FC1) + 1)
            for j in range(4):
                bk = abk(i, A_W + j)
                wt, K = (fc2a[:, :], 128) if j == 0 else (fc2e[:, j - 1, :, :].rearrange("p k m -> p (k m)"), V3)
                pe.matmul(bk[0:K, 0:W], wt, hT[:, :], start=True, stop=True).then_inc(a_ready, 1)

        def sums(b, q):
            hold(pe, o_steps, b * 6 + 6)
            hold(pe, eq_ready, b + 1)
            for h in range(2):
                bk = abk(b + 1, A_SUM + h)
                for j in range(2):
                    t = 2 * h + j
                    m = pe.matmul(bk[0:P, j * G:(j + 1) * G], eq[0:P, q, t, :], o[0:P, t, :], start=True, stop=True)
                m.then_inc(a_ready, 1)

        def iteration(b, q, more, more2):
            if isinstance(b, int) and b == 0:
                pe.wait_ge(a_ready, aj(0, 0))
                pe.sem_inc(a_ready, 2)
            else:
                sums(b - 1, 1 - q)
            hold(pe, x1n_ready, b * 4 + 4)
            turn(abk(b, A_XT), lambda t: x1n[0:P, t, 0:M0], M0)
            turn(abk(b, A_XT + 1), lambda t: x1n[0:P, t, M0:D], V3)
            if more:
                inputs(b + 1, 1 - q)
            pe.wait_ge(a_done, aj(b, A_XT + 1) + 1)
            bk = dbk(b, D_V)
            pe.matmul(bk[:, 0:W], nl0d[:, :], n0T[:, :], start=True, stop=True).then_inc(d_ready, 1)
            for s in range(3):
                bk = dbk(b, D_V + 1 + s)
                pe.matmul(bk[0:V3, 0:W], nl1e[:, s, :], n1T[:, :], start=True, stop=True).then_inc(d_ready, 1)
            if more:
                node_y(b + 1)
                edge_w(b + 1)
            else:
                pe.wait_ge(d_ready, dj(b, D_Y))
                pe.sem_inc(d_ready, 2)
            pe.wait_ge(prods, b * 4 + 4)
            for h in range(2):
                bk = dbk(b, D_OUT + h)
                for j in range(2):
                    cols = slice((2 * h + j) * P, (2 * h + j + 1) * P)
                    oo = bk[0:P, j * 224:(j + 1) * 224]
                    pe.matmul(oo[:, 0:128], tA[:, cols], wo_a[:, :], start=True, stop=False)
                    pe.matmul(oo[:, 32:128], t3[:, cols], wo_s[:, :], start=False, stop=True)
                    pe.matmul(oo[:, 128:224], t2[:, cols], wo_v[:, 0, :, :].rearrange("p w k -> p (w k)"),
                              start=True, stop=False, skip_group_check=True)
                    m = pe.matmul(oo[:, 128:224], t4[:, cols], wo_v[:, 1, :, :].rearrange("p w k -> p (w k)"),
                                  start=False, stop=True, skip_group_check=True)
                m.then_inc(d_ready, 1)

        pe.sem_inc(a_ready, 4)
        pe.sem_inc(d_ready, 4)
        inputs(0, 0)
        node_y(0)
        edge_w(0)
        pe.wait_ge(d_ready, 6)
        pe.sem_inc(d_ready, 2)
        sweep(pe, iteration)
        pe.wait_ge(a_ready, aj(NB - 1, A_IN))
        pe.sem_inc(a_ready, 12)
        sums(NB - 1, 1)

    @block.scalar
    def _(act):
        def out(b, j, to, K, cols=W, func=ACT.Copy):
            act.wait_ge(a_ready, aj(b, j) + 1)
            act.activation(to, abank[j % 4][0:K, 0:cols], func).then_inc(a_done, 1)

        def inputs(b, q, first=False, second=False):
            i = b - 1
            out(i, A_IN, xaT[:, :], 128)
            out(i, A_IN + 1, xbT[:, :], M1)
            out(i, A_IN + 2, efT[:, :], 64)
            if not first:
                act.wait_ge(eq_ready, b)
            out(i, A_IN + 3, idxrow[0:P, :, :].rearrange("p t e -> p (t e)"), P)
            if not (first or second):
                act.wait_ge(prods, (b - 1) * 4)
            for s in range(3):
                out(i, A_IN + 4 + s, shT[:, q, s, :], V3)
            out(i, A_FC1, hT[:, :], 64, func=ACT.Relu)

        def edge_w(b, q):
            out(b - 1, A_W, w01T[:, q, :], 128)
            for j in range(3):
                out(b - 1, A_W + 1 + j, w234T[:, q, j, :], V3)

        def deviation(b):
            act.wait_ge(ln_steps, b * 9 + 8)
            act.activation(std[0:P, :], mv[0:P, :, 1], ACT.Sqrt, bias=eps[0:P, :]).then_inc(std_ready, 1)

        def sums(b):
            act.wait_ge(osum_free, b + 1)
            for h in range(2):
                out(b + 1, A_SUM + h, osum[0:P, 2 * h:2 * h + 2, :].rearrange("p t f -> p (t f)"), P, 2 * G)

        def count(b):
            act.wait_ge(row_steps, b * 6 + 2)
            for t in range(T):
                if t:
                    act.wait_ge(cnt_ready, b * T + t)
                act.activation(junk[0:P, :], dup[0:P, t, :], ACT.Copy, accum_out=cnt[0:P, t:t + 1]).then_inc(cnt_ready, 1)

        def iteration(b, q, more, more2):
            if isinstance(b, int) and b == 0:
                act.wait_ge(a_done, aj(0, 0))
                act.sem_inc(a_done, 2)
            else:
                sums(b - 1)
            out(b, A_XT, n0T[:, :], M0)
            out(b, A_XT + 1, n1T[:, :], V3)
            if more:
                inputs(b + 1, 1 - q, second=isinstance(b, int) and b == 0)
            count(b)
            if more:
                edge_w(b + 1, 1 - q)
                deviation(b + 1)

        act.sem_inc(a_done, 4)
        inputs(0, 0, first=True)
        edge_w(0, 0)
        deviation(0)
        sweep(act, iteration)
        act.wait_ge(a_done, aj(NB - 1, A_IN))
        act.sem_inc(a_done, 12)
        sums(NB - 1)

    @block.vector
    def _(dve):
        def index(b, q):
            dve.wait_ge(ld[q], loaded(b, q))
            dve.wait_ge(row_steps, b * 6 - 5)
            dve.tensor_copy(idxf[0:P, q, :], isrc[0:P, q, :]).then_inc(idxf_ready, 1)

        def equal(b, q):
            dve.wait_ge(a_done, aj(b - 1, A_IN + 3) + 1)
            if not (isinstance(b, int) and b <= 1):
                dve.wait_ge(a_ready, aj(b - 1, A_SUM + 1) + 1)
                dve.wait_ge(row_steps, b * 6 - 5)
            dve.tensor_tensor(eq[0:P, q, :, :], idxrow[0:P, :, :], idxf[0:P, q, :].unsqueeze(2).to_broadcast([P, T, P]),
                              ALU.is_equal).then_inc(eq_ready, 1)

        def products(b, q):
            dve.wait_ge(a_done, aj(b - 1, A_W + 3) + 1)
            bk = dbank
            dve.wait_ge(d_ready, dj(b, D_V) + 1)
            dve.tensor_tensor(tA[:, :], bk[0][:, 0:W], w01T[:, q, :], ALU.mult).then_inc(d_done, 1)
            dve.wait_ge(d_ready, dj(b, D_V + 1) + 1)
            dve.tensor_tensor(t2[:, :], bk[1][0:V3, 0:W], w234T[:, q, 0, :], ALU.mult).then_inc(prods, 1)
            dve.tensor_tensor(b3[:, :], bk[1][0:V3, 0:W], shT[:, q, 0, :], ALU.mult).then_inc(d_done, 1)
            dve.wait_ge(d_ready, dj(b, D_V + 2) + 1)
            dve.tensor_tensor(c1_[:, :], bk[2][0:V3, 0:W], shT[:, q, 2, :], ALU.mult).then_inc(d_done, 1)
            dve.wait_ge(d_ready, dj(b, D_V + 3) + 1)
            dve.tensor_tensor(c2_[:, :], bk[3][0:V3, 0:W], shT[:, q, 1, :], ALU.mult).then_inc(d_done, 1)
            dve.wait_ge(d_done, dj(b, D_V + 1) + 1)
            dve.tensor_tensor(t3[:, :], b3[:, :], w234T[:, q, 1, :], ALU.mult).then_inc(prods, 1)
            dve.wait_ge(d_done, dj(b, D_V + 3) + 1)
            dve.tensor_tensor(c3_[:, :], c1_[:, :], c2_[:, :], ALU.subtract).then_inc(prods, 1)
            dve.wait_ge(prods, b * 4 + 3)
            dve.tensor_tensor(t4[:, :], c3_[:, :], w234T[:, q, 2, :], ALU.mult).then_inc(prods, 1)

        def moments(b, q):
            dve.wait_ge(gat[q], gathered(b, q))
            for h in range(2):
                dve.wait_ge(d_ready, dj(b - 1, D_Y + h) + 1)
                dve.tensor_tensor(y[0:P, 2 * h:2 * h + 2, :].rearrange("p t f -> p (t f)"), dbank[D_Y % 4 + h][0:P, 0:2 * D],
                                  ug[0:P, q, 2 * h:2 * h + 2, :].rearrange("p t f -> p (t f)"), ALU.add).then_inc(d_done, 1)
            for t in range(T):
                dve.wait_ge(d_done, dj(b - 1, D_Y + t // 2) + 1)
                dve.bn_stats(st[0:P, t, :], y[0:P, t, :]).then_inc(ln_steps, 1)
            for t in range(T):
                hold(dve, ln_steps, b * 9 + t + 1)
                dve.bn_aggr(mv[0:P, t, :], st[0:P, t, :]).then_inc(ln_steps, 1)

        def normed(b):
            dve.wait_ge(std_ready, b + 1)
            dve.reciprocal(rstd[0:P, :], std[0:P, :]).then_inc(ln_steps, 1)
            dve.wait_ge(ln_steps, b * 9 + 9)
            if not (isinstance(b, int) and b == 0):
                dve.wait_ge(a_ready, aj(b - 1, A_XT + 1) + 1)
            for t in range(T):
                dve.tensor_scalar(x1n[0:P, t, :], y[0:P, t, :], mv[0:P, t, 0:1], rstd[0:P, t:t + 1], ALU.subtract,
                                  ALU.mult).then_inc(x1n_ready, 1)

        def outputs(b, q):
            if not (isinstance(b, int) and b == 0):
                dve.wait_ge(a_ready, aj(b, A_SUM + 1) + 1)
            for h in range(2):
                dve.wait_ge(d_ready, dj(b, D_OUT + h) + 1)
                g = dbank[D_OUT % 4 + h][0:P, 0:448].rearrange("p (t c) -> p t c", t=2)
                ts = slice(2 * h, 2 * h + 2)
                dve.tensor_copy(o[0:P, ts, 0:V3], g[:, :, 32:128]).then_inc(o_steps, 1)
                dve.tensor_tensor(qr[0:P, ts, :, :], g[:, :, 0:32].unsqueeze(3).to_broadcast([P, 2, M1, 3]),
                                  rh6[0:P, q, ts, 0:3].unsqueeze(2).to_broadcast([P, 2, M1, 3]), ALU.mult).then_inc(o_steps, 1)
                dve.wait_ge(o_steps, b * 6 + h * 3 + 2)
                dve.tensor_tensor(o[0:P, ts, V3:G], g[:, :, 128:224], qr[0:P, ts, :, :].rearrange("p t w k -> p t (w k)"),
                                  ALU.add).then_inc(o_steps, 1)
                dve.wait_ge(o_steps, b * 6 + h * 3 + 3)
                dve.sem_inc(d_done, 1)

        def iteration(b, q, more, more2):
            if more:
                index(b + 1, 1 - q)
            equal(b, q)
            products(b, q)
            if more:
                moments(b + 1, 1 - q)
            else:
                dve.wait_ge(d_done, dj(b, D_Y))
                dve.sem_inc(d_done, 2)
            outputs(b, q)
            if more:
                normed(b + 1)

        dve.sem_inc(d_done, 4)
        dve.wait_ge(ld[0], loaded(0, 0))
        dve.tensor_copy(idxf[0:P, 0, :], isrc[0:P, 0, :]).then_inc(idxf_ready, 1)
        moments(0, 0)
        normed(0)
        dve.wait_ge(d_done, 6)
        dve.sem_inc(d_done, 2)
        sweep(dve, iteration)

    ctx.close()


def nodes(nc, tools, x_v, upd_v, agg_v, out_v, NBN, ident, lin_a, lin_b, skip0, skip1):
    ctx = ExitStack()
    sb, bank, sem = tools(ctx)
    G = 2 * V3
    xn = sb("xn", [128, 2, T, D])
    un = sb("un", [128, 2, T, D])
    gn = sb("gn", [128, 2, T, G])
    xaT = sb("xaT2", [128, W])
    xbT = sb("xbT2", [M1, W])
    y = sb("y2", [128, T, D])
    st = sb("st2", [128, T, 6])
    mv = sb("mv2", [128, T, 2])
    ve = sb("ve2", [128, T])
    rs = sb("rs2", [128, T])
    half = sb("half", [128, T])
    x1n = sb("x1n2", [128, 2, T, D])
    n0T = sb("n0T2", [M0, W])
    n1T = sb("n1T2", [V3, W])
    a = sb("a2", [128, T, G])
    sg = sb("sg", [128, T, V3])
    f = sb("f2", [128, T, D])
    z = sb("z2", [128, T, D])
    st_z = sb("st_z", [128, T, 6])
    mv_z = sb("mv_z", [128, T, 2])
    ve_z = sb("ve_z", [128, T])
    rs_z = sb("rs_z", [128, T])
    ob = sb("ob", [128, 2, T, D])

    abank = [bank(f"nabank{i}") for i in range(4)]
    dbank = [bank(f"ndbank{i}") for i in range(4)]

    ld = [sem("ld2_even"), sem("ld2_odd")]
    a_ready = sem("a_ready2")
    a_done = sem("a_done2")
    d_ready = sem("d_ready2")
    d_done = sem("d_done2")
    half_ready = sem("half_ready")
    ln_y = sem("ln_y")
    rs_y = sem("rs_y")
    x1n_ready = sem("x1n_ready2")
    sg_ready = sem("sg_ready")
    f_ready = sem("f_ready")
    z_ready = sem("z_ready")
    ln_z = sem("ln_z")
    rs_zr = sem("rs_zr")
    ob_ready = sem("ob_ready")
    stored = [sem("stored_even"), sem("stored_odd")]

    A_XT, A_IN = 0, 2
    D_Y, D_SK = 0, 2

    def aj(b, j):
        return (b + 1) * 4 + j

    dj = aj

    def loaded(b, q):
        return (b - q) * 24 + 48

    def sweep(eng, iteration):
        iteration(0, 0, True, True)
        with eng.Fori(0, (NBN - 4) // 2) as i:
            iteration(2 * i + 1, 1, True, True)
            iteration(2 * i + 2, 0, True, True)
        iteration(NBN - 3, 1, True, True)
        iteration(NBN - 2, 0, True, False)
        iteration(NBN - 1, 1, False, False)

    def early(b, n):
        return isinstance(b, int) and b < n

    block = ctx.enter_context(nc.Block())

    @block.sync
    def _(sp):
        def load(b, q):
            for to, of, n in ((xn, x_v, T * D), (un, upd_v, T * D), (gn, agg_v, T * G)):
                sp.dma_start(to[0:P, q, :, :].rearrange("p t f -> p (t f)"), of[:, ds(b * n, n)]).then_inc(ld[q], 16)

        def iteration(b, q, more, more2):
            if more2:
                sp.wait_ge(d_done, dj(b, D_SK + 1) + 1)
                load(b + 2, q)
            sp.wait_ge(ob_ready, b * 4 + 4)
            sp.dma_start(out_v[:, ds(b * T * D, T * D)], ob[0:P, q, :, :].rearrange("p t f -> p (t f)")).then_inc(stored[q], 16)

        load(0, 0)
        load(1, 1)
        sweep(sp, iteration)
        sp.wait_ge(stored[0], NBN // 2 * 16)
        sp.wait_ge(stored[1], NBN // 2 * 16)

    @block.tensor
    def _(pe):
        def turn(o_, tiles, K):
            for t in range(T):
                m = pe.transpose(o_[0:K, t * P:(t + 1) * P], tiles(t), ident[0:P, 0:P])
            m.then_inc(a_ready, 1)

        def abk(b, j):
            if not (isinstance(b, int) and b < 0):
                hold(pe, a_done, aj(b, j) - 3)
            return abank[j % 4]

        def dbk(b, j):
            if not (isinstance(b, int) and b < 0):
                hold(pe, d_done, dj(b, j) - 3)
            return dbank[j % 4]

        def inputs(b, q):
            hold(pe, ld[q], loaded(b, q))
            turn(abk(b - 1, A_IN), lambda t: xn[0:P, q, t, 0:128], 128)
            turn(abk(b - 1, A_IN + 1), lambda t: xn[0:P, q, t, 128:D], M1)

        def node_y(b):
            pe.wait_ge(a_done, aj(b - 1, A_IN + 1) + 1)
            for h in range(2):
                bk = dbk(b - 1, D_Y + h)
                for j in range(2):
                    cols = slice((2 * h + j) * P, (2 * h + j + 1) * P)
                    oo = bk[0:P, j * D:(j + 1) * D]
                    pe.matmul(oo, xaT[:, cols], lin_a[:, :], start=True, stop=False)
                    m = pe.matmul(oo, xbT[:, cols], lin_b[:, :], start=False, stop=True)
                m.then_inc(d_ready, 1)

        def iteration(b, q, more, more2):
            hold(pe, x1n_ready, b * 4 + 4)
            turn(abk(b, A_XT), lambda t: x1n[0:P, q, t, 0:M0], M0)
            turn(abk(b, A_XT + 1), lambda t: x1n[0:P, q, t, M0:D], V3)
            if more:
                inputs(b + 1, 1 - q)
                node_y(b + 1)
            else:
                pe.wait_ge(d_ready, dj(b, 0))
                pe.sem_inc(d_ready, 2)
            pe.wait_ge(a_done, aj(b, A_XT + 1) + 1)
            for h in range(2):
                bk = dbk(b, D_SK + h)
                for j in range(2):
                    cols = slice((2 * h + j) * P, (2 * h + j + 1) * P)
                    oo = bk[0:P, j * G:(j + 1) * G]
                    pe.matmul(oo[:, 0:V3], n0T[:, cols], skip0[:, :], start=True, stop=True)
                    m = pe.matmul(oo[:, V3:G], n1T[:, cols], skip1[:, :, :].rearrange("p w k -> p (w k)"), start=True, stop=True)
                m.then_inc(d_ready, 1)

        pe.sem_inc(a_ready, 2)
        inputs(0, 0)
        node_y(0)
        pe.wait_ge(d_ready, 2)
        pe.sem_inc(d_ready, 2)
        sweep(pe, iteration)

    @block.scalar
    def _(act):
        def out(b, j, to, K):
            act.wait_ge(a_ready, aj(b, j) + 1)
            act.activation(to, abank[j % 4][0:K, 0:W], ACT.Copy).then_inc(a_done, 1)

        def inputs(b):
            out(b - 1, A_IN, xaT[:, :], 128)
            out(b - 1, A_IN + 1, xbT[:, :], M1)

        def iteration(b, q, more, more2):
            out(b, A_XT, n0T[:, :], M0)
            out(b, A_XT + 1, n1T[:, :], V3)
            if more:
                inputs(b + 1)
            act.wait_ge(d_done, dj(b, D_SK + 1) + 1)
            if not early(b, 1):
                act.wait_ge(f_ready, b * 2)
            act.activation(sg[0:P, :, :], a[0:P, :, 0:V3], ACT.Sigmoid).then_inc(sg_ready, 1)

        act.sem_inc(a_done, 2)
        inputs(0)
        sweep(act, iteration)

    @block.gpsimd
    def _(pool):
        def power(b, moments, mv_, ve_, rs_, done):
            hold(pool, moments, b * 8 + 8)
            pool.tensor_scalar(ve_[0:P, :], mv_[0:P, :, 1], EPS, None, ALU.add).then_inc(done, 1)
            hold(pool, done, b * 2 + 1)
            pool.tensor_tensor(rs_[0:P, :], ve_[0:P, :], half[0:P, :], ALU.pow).then_inc(done, 1)

        def iteration(b, q, more, more2):
            if more:
                power(b + 1, ln_y, mv, ve, rs, rs_y)
            hold(pool, sg_ready, b + 1)
            if not early(b, 1):
                hold(pool, z_ready, b)
            pool.tensor_tensor(f[0:P, :, 0:M0], a[0:P, :, 0:M0], sg[0:P, :, 0:M0], ALU.mult).then_inc(f_ready, 1)
            pool.tensor_tensor(f[0:P, :, M0:D].rearrange("p t (w k) -> p t w k", k=3),
                               a[0:P, :, V3:G].rearrange("p t (w k) -> p t w k", k=3),
                               sg[0:P, :, M0:V3].unsqueeze(3).to_broadcast([P, T, M1, 3]), ALU.mult).then_inc(f_ready, 1)
            power(b, ln_z, mv_z, ve_z, rs_z, rs_zr)

        pool.memset(half[:, :], -0.5).then_inc(half_ready, 1)
        pool.wait_ge(half_ready, 1)
        power(0, ln_y, mv, ve, rs, rs_y)
        sweep(pool, iteration)

    @block.vector
    def _(dve):
        def moments_of(v, st_, mv_, b, steps):
            for t in range(T):
                dve.bn_stats(st_[0:P, t, :], v[0:P, t, :]).then_inc(steps, 1)
            for t in range(T):
                hold(dve, steps, b * 8 + t + 1)
                dve.bn_aggr(mv_[0:P, t, :], st_[0:P, t, :]).then_inc(steps, 1)

        def moments(b, q):
            dve.wait_ge(ld[q], loaded(b, q))
            for h in range(2):
                dve.wait_ge(d_ready, dj(b - 1, D_Y + h) + 1)
                dve.tensor_tensor(y[0:P, 2 * h:2 * h + 2, :].rearrange("p t f -> p (t f)"), dbank[D_Y + h][0:P, 0:2 * D],
                                  un[0:P, q, 2 * h:2 * h + 2, :].rearrange("p t f -> p (t f)"), ALU.add).then_inc(d_done, 1)
            dve.wait_ge(d_done, dj(b - 1, D_Y + 1) + 1)
            moments_of(y, st, mv, b, ln_y)

        def scaled(to, v, mv_, rs_, done):
            for t in range(T):
                dve.tensor_scalar(to[:, t, :], v[0:P, t, :], mv_[0:P, t, 0:1], rs_[0:P, t:t + 1], ALU.subtract,
                                  ALU.mult).then_inc(done, 1)

        def normed(b, q):
            dve.wait_ge(rs_y, b * 2 + 2)
            scaled(x1n[0:P, q], y, mv, rs, x1n_ready)

        def iteration(b, q, more, more2):
            if more:
                moments(b + 1, 1 - q)
            else:
                dve.wait_ge(d_done, dj(b, 0))
                dve.sem_inc(d_done, 2)
            if not early(b, 1):
                dve.wait_ge(f_ready, b * 2)
            for h in range(2):
                dve.wait_ge(d_ready, dj(b, D_SK + h) + 1)
                dve.tensor_tensor(a[0:P, 2 * h:2 * h + 2, :].rearrange("p t f -> p (t f)"), dbank[D_SK + h][0:P, 0:2 * G],
                                  gn[0:P, q, 2 * h:2 * h + 2, :].rearrange("p t f -> p (t f)"), ALU.add).then_inc(d_done, 1)
            if more:
                normed(b + 1, 1 - q)
            dve.wait_ge(f_ready, b * 2 + 2)
            dve.tensor_tensor(z[0:P, :, :], f[0:P, :, :], x1n[0:P, q, :, :], ALU.add).then_inc(z_ready, 1)
            dve.wait_ge(z_ready, b + 1)
            moments_of(z, st_z, mv_z, b, ln_z)
            dve.wait_ge(rs_zr, b * 2 + 2)
            if not early(b, 2):
                dve.wait_ge(stored[q], (b - q) * 8)
            scaled(ob[0:P, q], z, mv_z, rs_z, ob_ready)

        moments(0, 0)
        normed(0, 0)
        dve.wait_ge(d_done, 2)
        dve.sem_inc(d_done, 2)
        sweep(dve, iteration)

    ctx.close()


_INS = ['x', 'src', 'dst', 'edge_attr_3', 'edge_attr_4', 'edge_attr_64', 'L0_gnn_wm000', 'L0_gnn_wm011',
        'L0_gnn_wm101', 'L0_gnn_wm110', 'L0_gnn_lm0', 'L0_gnn_lm1', 'L0_gnn_wu000', 'L0_gnn_wu011', 'L0_gnn_wu101',
        'L0_gnn_wu110', 'L0_gnn_lu0', 'L0_gnn_lu1', 'L1_gnn_W_skip0', 'L1_gnn_W_skip1', 'L1_gnn_W_nl0',
        'L1_gnn_W_nl1', 'L1_gnn_W_fc1', 'L1_gnn_W_fc2', 'L1_gnn_W_out_s', 'L1_gnn_W_out_v']


def kernel(**inputs):
    import numpy as _np
    import concourse.bacc as _bacc
    from concourse import mybir as _mybir
    from concourse.bass_utils import run_bass_kernel_spmd as _run

    nc = _bacc.Bacc("TRN2", target_bir_lowering=False, num_devices=1)
    arrays, args = {}, []
    for name in _INS:
        a = _np.ascontiguousarray(inputs[name])
        arrays[f"in_{name}_dram"] = a
        args.append(nc.dram_tensor(f"in_{name}_dram", a.shape, _mybir.dt.from_np(a.dtype), kind="ExternalInput").ap())
    shape = inputs['x'].shape
    args.append(nc.dram_tensor("out_0_dram", shape, _mybir.dt.from_np(_np.dtype('float32')), kind="ExternalOutput").ap())
    build(nc, *args)
    r = _run(nc, [arrays], core_ids=[0])
    return r.results[0]["out_0_dram"]
```

```python
from contextlib import ExitStack

import numpy as np

import concourse.bass as bass
from concourse import mybir

F32 = mybir.dt.float32
F32R = mybir.dt.float32r
BF16 = mybir.dt.bfloat16
I32 = mybir.dt.int32
ALU = mybir.AluOpType
ACT = mybir.ActivationFunctionType
AX = mybir.AxisListType

P = 125
T = 4
W = P * T
M0, M1, D = 64, 32, 160
V3 = 3 * M1
EPS = 1e-5

SOURCES, DVE_OPS, POOL_OPS, HIGHS, UNITS = [], [], [], [], []
GROUPS = 8
NG = 9
for _g in range(GROUPS):
    _s, _o, _n, _q = NG * _g, 11 * (_g % 2), len(DVE_OPS), 2 * (_g % 2)
    SOURCES += [("z011", _g), ("x0", 4 * _g), ("z101", _g), ("x0", 4 * _g + 1), ("x1", 0, _g),
                ("x0", 4 * _g + 2), ("x1", 1, _g), ("x1", 2, _g), ("x0", 4 * _g + 3)]
    _h = len(HIGHS)
    HIGHS += [(22, _q, _n + 1, _s + 1), (23, _q + 1, _n + 3, _s + 3)]
    DVE_OPS += [("z", _s, _o, "a1"), ("mul", _s + 1, 22, "a0", 0), ("z", _s + 2, _o + 3, "x1"),
                ("mul", _s + 3, 23, "a0", 0), ("low", 22, _h),
                ("mul", _s + 4, _o + 6, "a1", 0), ("mul", _s + 5, _o + 7, "a0", 0), ("mul", _s + 6, _o + 8, "a1", 1),
                ("add", _o + 6, _o + 8), ("mul", _s + 7, _o + 9, "a1", 2), ("mul", _s + 8, _o + 10, "a0", 0),
                ("add", _o + 6, _o + 9)]
    UNITS += [("hl", 2 * _g, 0, _q, _s + 6, ("dve", _n + 4), _h),
              ("w", 3 * _g, 0, _o + 7, _s + 8, ("dve", _n + 6), None),
              ("hl", 2 * _g + 1, 0, _q + 1, _s + 11, ("pool", len(POOL_OPS) + 1), _h + 1),
              ("w", 3 * _g + 1, 0, _o + 10, _s + 11, ("dve", _n + 10), None),
              ("w", 3 * _g + 2, 0, _o + 6, _s + 11, ("dve", _n + 11), None)]
    UNITS += [("sel", _g, _k, _o + _k, _s + 14 + _k, ("pool", len(POOL_OPS) + (0, 2, 3)[_k]), None) for _k in range(3)]
    POOL_OPS += [("add", _o + _k, _o + 3 + _k, _n + 2) for _k in range(3)]
    POOL_OPS[-2:-2] = [("low", 23, _h + 1)]
FIRST_UNIT = 9
UNITS = sorted(((k_, n_, c_, sl_, max(at_, FIRST_UNIT), nd_, h_) for k_, n_, c_, sl_, at_, nd_, h_ in UNITS), key=lambda u: u[4])
NS, NO, NPO, NH, NU = len(SOURCES), len(DVE_OPS), len(POOL_OPS), len(HIGHS), len(UNITS)
LAST = {op[1]: n for n, op in enumerate(DVE_OPS) if op[0] in ("z", "mul")}
RING = 4
SLOTS = 24


def group_of(slot_unit):
    kind, n = slot_unit[0:2]
    return {"hl": n // 2, "w": n // 3, "sel": n}[kind]


LAST_UNIT = [max(u for u in range(NU) if group_of(UNITS[u]) == g) for g in range(GROUPS)]

J_IDX, J_STK, J_X0, J_XE, J_S, J_X1, J_A0, J_A1 = 0, 1, 6, 7, 11, 12, 15, 16
NPREP = 19
NSUM = 4
NJOB = NPREP + NSUM
SUM_AT = [10, 12, 14, 16]
LOW_AT = [4 * 12, 6 * 12]
PREP_AT = [18] + [20 + 2 * j for j in range(NPREP - 1)]


PASSED = []


def ds(start, size):
    return bass.DynSlice(start, size)


def hold(eng, sem, value):
    eng.wait_ge(sem, value)
    eng.sem_inc(PASSED[0], 1)


def build(nc, x, src, dst, edge_attr_3, edge_attr_4, edge_attr_64, wm000, wm011, wm101, wm110, lm0, lm1,
          wu000, wu011, wu101, wu110, lu0, lu1, w_skip0, w_skip1, w_nl0, w_nl1, w_fc1, w_fc2,
          w_out_s, w_out_v, out):
    N, E = x.shape[0], src.shape[0]
    RN, RE = N // P, E // P
    NBN, NB = RN // T, RE // T
    assert N == P * T * NBN and E == P * T * NB and NB % 2 == 0 and NB >= 4 and NBN % 2 == 0

    upd = nc.dram_tensor("upd", (N + P, D), F32, kind="Internal").ap()
    agg = nc.dram_tensor("agg", (N + P, 2 * V3), F32, kind="Internal").ap()

    src_v = src.rearrange("(p c) -> p c", p=P)
    dst_v = dst.rearrange("(p c) -> p c", p=P)
    ea4_v = edge_attr_4.rearrange("(p c) f -> p (c f)", p=P)
    ea3_v = edge_attr_3.rearrange("(p c) f -> p (c f)", p=P)
    ef_v = edge_attr_64.rearrange("(p c) f -> p (c f)", p=P)
    x_v = x.rearrange("(p c) f -> p (c f)", p=P)
    out_v = out.rearrange("(p c) f -> p (c f)", p=P)
    upd_v = upd[0:N, :].rearrange("(p c) f -> p (c f)", p=P)
    agg_v = agg[0:N, :].rearrange("(p c) f -> p (c f)", p=P)

    top = ExitStack()

    def tools(ctx):
        def sb(name, shape, dt=F32):
            return ctx.enter_context(nc.sbuf_tensor(name, shape, dt))

        def bank(name, dt=F32):
            return ctx.enter_context(nc.psum_tensor(name, [128, 2048 // (4 if dt == F32 else 2)], dt))

        def sem(name):
            return ctx.enter_context(nc.semaphore(name))
        return sb, bank, sem

    with top:
        sb, bank, sem = tools(top)
        PASSED[:] = [sem("passed")]
        ident = sb("ident", [128, 128])
        identb = sb("identb", [128, 128], BF16)
        lower = sb("lower", [128, P])
        spare = sb("spare", [128, 1])
        zero = sb("zero", [128, 4 * V3])
        lin_a = sb("lin_a", [128, D])
        lin_b = sb("lin_b", [32, D])
        nl0d = sb("nl0d", [M0, 128])
        nl1e = sb("nl1e", [V3, 3, V3])
        fc1 = sb("fc1", [M0, 64])
        fc2a = sb("fc2a", [64, 128])
        fc2e = sb("fc2e", [64, 3, 3, M1])
        wo_a = sb("wo_a", [128, 128])
        wo_s = sb("wo_s", [V3, V3])
        wo_v = sb("wo_v", [V3, 2, M1, 3])
        skip0 = sb("skip0", [M0, V3])
        skip1 = sb("skip1", [V3, M1, 3])

        with ExitStack() as c0:
            sb0, _, sem0 = tools(c0)
            k_in = sb0("k_in", [V3, 6])
            k_out = sb0("k_out", [V3, 3])
            lu0_s = sb0("lu0_s", [M0, M0])
            lu1_r = sb0("lu1_r", [V3, M1])
            nl1_r = sb0("nl1_r", [V3, M1])
            sk1_r = sb0("sk1_r", [V3, M1])
            wov_r = sb0("wov_r", [V3, 2, M1])
            lin1e = sb0("lin1e", [V3, M1, 3])
            raw_s = sb0("raw_s", [V3, V3])
            raw_a = sb0("raw_a", [128, 128])
            w_in = sem0("w_in")
            w_on = sem0("w_on")
            c_pool = sem0("c_pool")
            c_vec = sem0("c_vec")
            c_done = sem0("c_done")
            w_mov = sem0("w_mov")
            block = c0.enter_context(nc.Block())

            @block.sync
            def _(sp):
                rows = [(lu0_s[:, :], lu0), (nl0d[:, 0:M0], w_nl0), (nl0d[:, M0:128], w_nl0), (fc1[:, :], w_fc1),
                        (fc2a[:, :], w_fc2[:, 0:128]), (skip0[:, :], w_skip0),
                        (raw_s[0:32, :], w_out_s[64:96, :])]
                rows += [(raw_s[32 * k:32 * k + 32, :], w_out_s[64:96, :]) for k in range(1, 3)]
                rows += [(fc2e[:, j, k, :], w_fc2[:, 128 + 32 * j:160 + 32 * j]) for j in range(3) for k in range(3)]
                for to, of in rows:
                    sp.dma_start(to, of).then_inc(w_in, 16)
                for k in range(3):
                    for j in range(2):
                        sp.dma_start(wov_r[32 * k:32 * k + 32, j, :],
                                     w_out_v[64 + 32 * j:96 + 32 * j, :]).then_inc(w_in, 16)
                    for tile, of in ((lu1_r, lu1), (nl1_r, w_nl1), (sk1_r, w_skip1)):
                        sp.dma_start(tile[k:k + 3 * (M1 - 1) + 1:3, :], of).then_inc(w_in, 16)
                sp.wait_ge(c_pool, 3)
                sp.dma_start(raw_a[64:128, 0:32], w_out_v[0:64, :]).then_inc(w_in, 16)
                sp.dma_start(raw_a[0:64, 32:128], w_out_s[0:64, :]).then_inc(w_in, 16)
                sp.wait_ge(c_done, 2)
                sp.dma_start(lin_a[64:128, 64:160], lin1e[0:64, :, :].rearrange("p m k -> p (m k)")).then_inc(w_mov, 16)
                sp.dma_start(lin_b[:, 64:160], lin1e[64:96, :, :].rearrange("p m k -> p (m k)")).then_inc(w_mov, 16)
                sp.wait_ge(w_mov, 32)

            n_in = 16 * (7 + 2 + 9 + 3 * 5 + 2)

            @block.gpsimd
            def _(pool):
                pool.memset(ident[:, :], 0.0).then_inc(c_pool, 1)
                pool.memset(lower[:, :], 1.0).then_inc(c_pool, 1)
                pool.memset(raw_a[:, :], 0.0).then_inc(c_pool, 1)
                pool.memset(zero[:, :], 0.0).then_inc(c_pool, 1)
                pool.memset(lin_b[:, :], 0.0).then_inc(c_pool, 1)
                pool.wait_ge(c_pool, 5)
                pool.affine_select(out=ident[:, :], in_=ident[:, :], compare_op=ALU.not_equal, fill=1.0, base=0,
                                   pattern=[[-1, 128]], channel_multiplier=1).then_inc(c_pool, 1)
                pool.affine_select(out=lower[:, :], in_=lower[:, :], compare_op=ALU.is_gt, fill=0.0, base=0,
                                   pattern=[[-1, P]], channel_multiplier=1).then_inc(c_pool, 1)
                pool.iota(spare[:, :], pattern=[[0, 1]], base=N, channel_multiplier=1,
                          allow_small_or_imprecise_dtypes=True).then_inc(c_pool, 1)
                pool.wait_ge(c_pool, 8)

            @block.vector
            def _(dve):
                n = [0]

                def step(ins):
                    n[0] += 1
                    ins.then_inc(c_vec, 1)
                    dve.wait_ge(c_vec, n[0])

                dve.wait_ge(c_pool, 8)
                step(dve.tensor_copy(identb[:, :], ident[:, :]))
                step(dve.tensor_reduce(k_in[:, 0:3], ident[0:V3, 0:V3].rearrange("p (m k) -> p k m", k=3), AX.X, ALU.add))
                step(dve.tensor_reduce(k_out[:, :], ident[0:V3, 0:V3].rearrange("p (k m) -> p k m", k=3), AX.X, ALU.add))
                step(dve.tensor_copy(k_in[:, 3:6], k_in[:, 0:3]))
                dve.wait_ge(w_in, n_in)

                def spread(to, rows, mask):
                    return dve.tensor_tensor(to, rows.unsqueeze(2).to_broadcast([V3, M1, 3]),
                                             mask.unsqueeze(1).to_broadcast([V3, M1, 3]), ALU.mult)

                step(spread(lin1e[:, :, :], lu1_r[:, :], k_in[:, 0:3]))
                step(spread(skip1[:, :, :], sk1_r[:, :], k_in[:, 0:3]))
                for j in range(2):
                    step(spread(wo_v[:, j, :, :], wov_r[:, j, :], k_out[:, :]))
                for s in range(3):
                    step(dve.tensor_tensor(nl1e[:, s, :].rearrange("p (k m) -> p k m", k=3),
                                           nl1_r[:, :].unsqueeze(1).to_broadcast([V3, 3, M1]),
                                           k_in[:, s:s + 3].unsqueeze(2).to_broadcast([V3, 3, M1]), ALU.mult))
                step(dve.tensor_scalar(wo_v[:, 0, :, :], wo_v[:, 0, :, :], 1 / 32, None, ALU.mult))
                step(dve.tensor_scalar(wo_v[:, 1, :, :], wo_v[:, 1, :, :], float(np.sqrt(1.5) / 32), None, ALU.mult))
                step(dve.tensor_scalar(wo_s[:, :], raw_s[:, :], 1 / 32, None, ALU.mult))
                step(dve.tensor_scalar(wo_a[:, 32:128], raw_a[:, 32:128], 1 / 32, None, ALU.mult))
                step(dve.tensor_scalar(wo_a[:, 0:32], raw_a[:, 0:32], float(np.sqrt(3.0) / 32), None, ALU.mult))
                step(dve.tensor_scalar(lin1e[:, :, :], lin1e[:, :, :], float(1 / np.sqrt(M1)), None, ALU.mult))
                step(dve.scalar_tensor_tensor(out=lin1e[:, :, :], in0=ident[0:V3, 0:V3].rearrange("p (m k) -> p m k", k=3),
                                              scalar=2.0, in1=lin1e[:, :, :], op0=ALU.mult, op1=ALU.add))
                step(dve.memset(lin_a[:, :], 0.0))
                step(dve.tensor_scalar(lu0_s[:, :], lu0_s[:, :], float(1 / np.sqrt(M0)), None, ALU.mult))
                dve.scalar_tensor_tensor(out=lin_a[0:M0, 0:M0], in0=ident[0:M0, 0:M0], scalar=2.0, in1=lu0_s[:, :],
                                         op0=ALU.mult, op1=ALU.add).then_inc(c_done, 2)

        layer0_edges(nc, tools, x, upd, agg, upd_v, agg_v, src_v, dst_v, ea4_v, N, NB, RN,
                     ident, identb, lower, spare, zero,
                     (wm000, wm011, wm101, wm110, lm0, lm1, wu000, wu011, wu101, wu110))
        layer1_edges(nc, tools, x, upd, agg, src_v, dst_v, ea3_v, ef_v, N, NB, ident, lower, spare,
                     (lin_a, lin_b, nl0d, nl1e, fc1, fc2a, fc2e, wo_a, wo_s, wo_v))
        nodes(nc, tools, x_v, upd_v, agg_v, out_v, NBN, ident, lin_a, lin_b, skip0, skip1)


def layer0_edges(nc, tools, x, upd, agg, upd_v, agg_v, src_v, dst_v, ea4_v, N, NB, RN,
                 ident, identb, lower, spare, zero, weights):
    wm000, wm011, wm101, wm110, lm0, lm1, wu000, wu011, wu101, wu110 = weights
    ctx = ExitStack()
    sb, bank, sem = tools(ctx)
    s_tp0 = float(1 / np.sqrt(M0 * M0 + M1 * M1))
    s_tp1 = float(1 / np.sqrt(2 * M0 * M1))
    s_msg = float(1 / np.sqrt(M0 + M1))
    i3 = float(1 / np.sqrt(3.0))

    w_hl = sb("w_hl", [128, 16, 128], F32R)
    w_dir = sb("w_dir", [128, 24, M0])
    w011 = sb("w011", [128, 2, M1, M1], F32R)
    w101 = sb("w101", [128, 2, M1, M1], F32R)
    sel_x0 = sb("sel_x0", [V3, 2 * M1 // 4 * 128], BF16)
    sel_x1 = sb("sel_x1", [V3, 8 * 128], BF16)
    sel_rep = sb("sel_rep", [V3, 128], BF16)
    sel_dup = sb("sel_dup", [V3, 2, 128], BF16)
    fold = sb("fold", [128, M0])
    sel_w = sb("sel_w", [128, 2 * V3])
    msg_a = sb("msg_a", [128, 128])
    msg_s = sb("msg_s", [M1, 128])
    msg_k = sb("msg_k", [128, 128])

    with ExitStack() as c1:
        sb1, _, sem1 = tools(c1)
        raw = sb1("raw_w", [128, 40, M0])
        t011 = sb1("t011", [128, M1, M1])
        t101 = sb1("t101", [128, M1, M1])
        w_in = sem1("w_in0")
        done = sem1("w_made0")
        blk = c1.enter_context(nc.Block())

        @blk.sync
        def _(sp):
            sp.dma_start(raw[:, 0:32, :], wu000.rearrange("(c u) v w -> (u v) c w", u=2)).then_inc(w_in, 16)
            sp.dma_start(raw[:, 32:40, :], wu110.rearrange("(c u) v w -> (u v) c w", u=4)).then_inc(w_in, 16)
            for j in range(2):
                rows = slice(64 * j, 64 * j + 64)
                sp.dma_start(t011[rows, :, :], wu011).then_inc(w_in, 16)
                sp.dma_start(t101[rows, :, :], wu101.rearrange("u v w -> v u w")).then_inc(w_in, 16)
            for j in range(2):
                c = slice(64 * j, 64 * j + 64)
                sp.dma_start(msg_a[0:64, c], wm000[:, 0, :]).then_inc(w_in, 16)
                sp.dma_start(msg_a[64:128, c], lm0).then_inc(w_in, 16)
                sp.dma_start(msg_s[:, c], wm110[:, 0, :]).then_inc(w_in, 16)
            for j in range(4):
                c = slice(32 * j, 32 * j + 32)
                sp.dma_start(msg_k[0:64, c], wm011[:, 0, :]).then_inc(w_in, 16)
                sp.dma_start(msg_k[64:96, c], wm101[:, 0, :]).then_inc(w_in, 16)
                sp.dma_start(msg_k[96:128, c], lm1).then_inc(w_in, 16)

        @blk.vector
        def _(dve):
            n = [0]

            def step(ins):
                n[0] += 1
                ins.then_inc(done, 1)
                dve.wait_ge(done, n[0])

            for r in range(3):
                rows = slice(32 * r, 32 * r + 32)
                one = identb[rows, rows]
                step(dve.tensor_copy(sel_x0[rows, :].rearrange("p (u v) -> p u v", v=64),
                                     one.unsqueeze(2).to_broadcast([32, 32, 64])))
                step(dve.tensor_copy(sel_x1[rows, :].rearrange("p (u v) -> p u v", v=32),
                                     one.unsqueeze(2).to_broadcast([32, 32, 32])))
                step(dve.tensor_copy(sel_rep[rows, :].rearrange("p (j u) -> p j u", u=32),
                                     one.unsqueeze(1).to_broadcast([32, 4, 32])))
            step(dve.memset(sel_dup[:, :, :], 0.0))
            for r in range(3):
                rows = slice(32 * r, 32 * r + 32)
                for c in range(4):
                    step(dve.tensor_copy(sel_dup[rows, c % 2, 32 * c:32 * c + 32], identb[rows, rows]))
            for j in range(2):
                rows = slice(64 * j, 64 * j + 64)
                step(dve.tensor_copy(fold[rows, :], ident[rows, rows]))
            step(dve.memset(sel_w[:, :], 0.0))
            step(dve.tensor_reduce(sel_w[:, V3:V3 + 4], ident[:, :].rearrange("p (j v) -> p j v", v=32), AX.X, ALU.add))
            step(dve.tensor_scalar(sel_w[:, V3:V3 + 4], sel_w[:, V3:V3 + 4], s_tp1, None, ALU.mult))
            dve.wait_ge(w_in, 16 * (6 + 6 + 12))
            step(dve.tensor_scalar(raw[:, 0:32, :], raw[:, 0:32, :], s_tp0, None, ALU.mult))
            step(dve.tensor_scalar(raw[:, 32:40, :], raw[:, 32:40, :], s_tp0 * i3, None, ALU.mult))
            by_group = raw[:, 0:32, :].rearrange("p (g c) w -> p g c w", c=4)
            hl = w_hl[:, :, :].rearrange("p (g c) w -> p g c w", c=2)
            step(dve.tensor_copy(hl[:, :, :, 0:M0], by_group[:, :, 0:2, :]))
            step(dve.tensor_tensor(hl[:, :, :, M0:128], by_group[:, :, 0:2, :], hl[:, :, :, 0:M0], ALU.subtract))
            direct = w_dir[:, :, :].rearrange("p (g c) w -> p g c w", c=3)
            step(dve.tensor_copy(direct[:, :, 0:2, :], by_group[:, :, 2:4, :]))
            step(dve.tensor_copy(direct[:, :, 2, :], raw[:, 32:40, :]))
            for to, of in ((w011, t011[:, :, :].rearrange("u v w -> u w v")), (w101, t101[:, :, :].rearrange("v u w -> v w u"))):
                step(dve.tensor_copy(to[:, 0, :, :], of))
                step(dve.tensor_tensor(to[:, 1, :, :], of, to[:, 0, :, :], ALU.subtract))
            step(dve.tensor_scalar(msg_a[0:64, :], msg_a[0:64, :], s_msg, None, ALU.mult))
            step(dve.tensor_scalar(msg_a[64:128, :], msg_a[64:128, :], float(1 / np.sqrt(M0)), None, ALU.mult))
            step(dve.tensor_scalar(msg_s[:, :], msg_s[:, :], s_msg * i3, None, ALU.mult))
            step(dve.tensor_scalar(msg_k[0:96, :], msg_k[0:96, :], s_msg, None, ALU.mult))
            step(dve.tensor_scalar(msg_k[96:128, :], msg_k[96:128, :], float(1 / np.sqrt(M1)), None, ALU.mult))

    isrc = sb("isrc", [128, 2, T], I32)
    idst = sb("idst", [128, 2, T], I32)
    ea4 = sb("ea4", [128, 2, T, 4])
    xs = sb("xs", [128, T, D])
    xd = sb("xd", [128, T, D])
    xe = sb("xe", [128, T, 4, 128])
    xpe = sb("xpe", [128, T, M1, 3])
    xsum = sb("xsum", [128, T, M1])
    parts = sb("parts", [128, T, 5, 3, M1], BF16)
    rest = sb("rest", [128, T, 5, M1])
    idxf = sb("idxf", [128, 2, T])
    idxrow = sb("idxrow", [128, T, P])
    eq = sb("eq", [128, 2, T, P])
    dup = sb("dup", [128, T, P])
    cnt = sb("cnt", [128, T])
    later = sb("later", [128, T])
    junk = sb("junk", [128, P])
    gap = sb("gap", [128, T])
    move = sb("move", [128, T])
    rowf = sb("rowf", [128, T])
    row = sb("row", [128, 2, T], I32)
    xeT = sb("xeT", [128, 4, W])
    xsumT = sb("xsumT", [M1, W])
    stk = sb("stk", [V3, 2, 5, W], BF16)
    x0T = sb("x0T", [128, W])
    x0hl = sb("x0hl", [128, 2, W], F32R)
    a0hl = sb("a0hl", [128, 2, W], F32R)
    a0T = sb("a0T", [128, 2, W])
    a1T = sb("a1T", [128, 2, 3, W])
    x1T = sb("x1T", [128, 2, 3, W])
    prod = sb("prod", [128, SLOTS, W])
    high = sb("high", [128, 4, W], F32R)
    low = sb("low", [128, 4, W], F32R)
    acc0T = sb("acc0T", [128, W])
    acc1T = sb("acc1T", [V3, W])
    accs = sb("accs", [128, T, D])
    osum = sb("osum", [128, T, D])

    ring = [bank(f"ring{i}") for i in range(RING)]
    acc = ctx.enter_context(nc.psum_tensor("acc", [128, 2, 512], F32))
    small = [bank(f"small{i}") for i in range(2)]

    ld = [sem("ld0_even"), sem("ld0_odd")]
    gat = [sem("gat0_even"), sem("gat0_odd")]
    op_steps = sem("op_steps")
    casts = sem("casts")
    row_steps = sem("row_steps")
    cnt_ready = sem("cnt_ready")
    idxf_ready = sem("idxf_ready")
    eq_ready = sem("eq_ready")
    job_ready = sem("job_ready")
    job_done = sem("job_done")
    src_ready = sem("src_ready")
    op_done = sem("op_done")
    pool_done = sem("pool_done")
    high_ready = sem("high_ready")
    in_high = sem("in_high")
    in_low = sem("in_low")
    unit_done = sem("unit_done")
    acc_out = sem("acc_out")
    zeroed = sem("zeroed")
    zeroed_agg = sem("zeroed_agg")
    scat = sem("scat0")
    osum_free = sem("osum_free0")

    def loaded(b, q):
        return (b - q) * 24 + 48

    def gathered(b, q):
        return (b - q) * 64 + 128

    def job_no(b, j):
        return b * NJOB + j

    def sum_no(b, h):
        return (b + 2) * NJOB - NSUM + h

    def made(b, o):
        return (b + 1) * NO + o + 1

    def used(b, u):
        return (b + 1) * NU + u + 1

    block = ctx.enter_context(nc.Block())

    def sweep(eng, main, **last):
        with eng.Fori(0, (NB - 4) // 2) as i:
            main(2 * i + 1, 1)
            main(2 * i + 2, 0)
        main(NB - 3, 1)
        main(NB - 2, 0, **last)

    @block.sync
    def _(sp):
        def load(b, q):
            sp.dma_start(isrc[0:P, q, :], src_v[:, ds(b * T, T)]).then_inc(ld[q], 16)
            sp.dma_start(idst[0:P, q, :], dst_v[:, ds(b * T, T)]).then_inc(ld[q], 16)
            sp.dma_start(ea4[0:P, q, :, :].rearrange("p t f -> p (t f)"), ea4_v[:, ds(b * 16, 16)]).then_inc(ld[q], 16)

        load(0, 0)
        load(1, 1)
        sp.dma_start(upd_v.rearrange("p (r f) -> p r f", f=2 * D),
                     zero[0:P, 0:2 * D].unsqueeze(1).to_broadcast([P, RN // 2, 2 * D])).then_inc(zeroed, 16)
        sp.dma_start(upd[N:N + P, :], zero[0:P, 0:D]).then_inc(zeroed, 16)
        sp.dma_start(agg_v.rearrange("p (r f) -> p r f", f=2 * 2 * V3),
                     zero[0:P, 0:4 * V3].unsqueeze(1).to_broadcast([P, RN // 2, 4 * V3])).then_inc(zeroed_agg, 16)
        sp.dma_start(agg[N:N + P, :], zero[0:P, 0:2 * V3]).then_inc(zeroed_agg, 16)

        with sp.Fori(0, (NB - 2) // 2) as i:
            for q in range(2):
                b = 2 * i + q
                hold(sp, op_steps, b * 11 + 11)
                hold(sp, idxf_ready, b + 1)
                load(b + 2, q)
        sp.wait_ge(zeroed_agg, 32)

    @block.gpsimd
    def _(pool):
        def gather(b, q, tiles):
            for t in tiles:
                pool.indirect_dma_start(xs[0:P, t, :], None, x,
                                        bass.IndirectOffsetOnAxis(ap=isrc[0:P, q, t:t + 1], axis=0)).then_inc(gat[q], 16)
                pool.indirect_dma_start(xd[0:P, t, :], None, x,
                                        bass.IndirectOffsetOnAxis(ap=idst[0:P, q, t:t + 1], axis=0)).then_inc(gat[q], 16)

        def split_x(b, q, first=False):
            hold(pool, gat[q], gathered(b, q))
            if not first:
                hold(pool, job_ready, job_no(b - 1, J_S) + 1)
            s0 = xs[0:P, :, 0:M0].rearrange("p t (s u) -> p t s u", u=M1)
            s1 = xs[0:P, :, M0:D].rearrange("p t (u k) -> p t k u", k=3)
            hold(pool, casts, b * 5 + 2)
            pool.tensor_tensor(rest[0:P, :, 0:2, :], s0, parts[0:P, :, 0:2, 0, :], ALU.subtract).then_inc(op_steps, 1)
            pool.tensor_tensor(rest[0:P, :, 2:5, :], s1, parts[0:P, :, 2:5, 0, :], ALU.subtract).then_inc(op_steps, 1)

        def split_rest(b, q):
            hold(pool, casts, b * 5 + 3)
            pool.tensor_tensor(parts[0:P, :, :, 2, :], rest[0:P, :, :, :], parts[0:P, :, :, 1, :],
                               ALU.subtract).then_inc(op_steps, 1)

        d0 = xd[0:P, :, 0:M0]
        d1k = xd[0:P, :, M0:D].rearrange("p t (u k) -> p t k u", k=3)

        def edge_scalars(b, q):
            e0 = ea4[0:P, q, :, 3:4]
            pool.tensor_tensor(xpe[0:P, :, :, :], xd[0:P, :, M0:D].rearrange("p t (u k) -> p t u k", k=3),
                               ea4[0:P, q, :, 0:3].unsqueeze(2).to_broadcast([P, T, M1, 3]), ALU.mult).then_inc(op_steps, 1)
            pool.tensor_tensor(xe[0:P, :, 0, 0:64], d0, e0.to_broadcast([P, T, M0]), ALU.mult).then_inc(op_steps, 1)

        def edge_vectors(b, q):
            for k in range(3):
                pool.tensor_tensor(xe[0:P, :, 1 + k, 0:64], d0, ea4[0:P, q, :, k:k + 1].to_broadcast([P, T, M0]),
                                   ALU.mult).then_inc(op_steps, 1)

        def edge_rest(b, q):
            pool.tensor_tensor(xe[0:P, :, 1:4, 64:96], d1k, ea4[0:P, q, :, 3:4].unsqueeze(3).to_broadcast([P, T, 3, M1]),
                               ALU.mult).then_inc(op_steps, 1)

        def edge_sum(b, q):
            hold(pool, op_steps, b * 11 + 9)
            pool.tensor_tensor(xsum[0:P, :, :], xpe[0:P, :, :, 0], xpe[0:P, :, :, 1], ALU.add).then_inc(op_steps, 1)
            hold(pool, op_steps, b * 11 + 10)
            pool.tensor_tensor(xsum[0:P, :, :], xsum[0:P, :, :], xpe[0:P, :, :, 2], ALU.add).then_inc(op_steps, 1)

        def duplicates(b, q):
            hold(pool, eq_ready, b + 1)
            pool.tensor_tensor(dup[0:P, :, :], eq[0:P, q, :, :], lower[0:P, :].unsqueeze(1).to_broadcast([P, T, P]),
                               ALU.mult).then_inc(row_steps, 1)
            pool.tensor_tensor(gap[0:P, :], spare[0:P, :].to_broadcast([P, T]), idxf[0:P, q, :],
                               ALU.subtract).then_inc(row_steps, 1)

        def rows_of(b, q):
            n = b * 6 + 1
            hold(pool, row_steps, n + 2)
            hold(pool, cnt_ready, b * T + T)
            pool.tensor_scalar(later[0:P, :], cnt[0:P, :], 1.0, None, ALU.min).then_inc(row_steps, 1)
            hold(pool, row_steps, n + 3)
            pool.tensor_tensor(move[0:P, :], later[0:P, :], gap[0:P, :], ALU.mult).then_inc(row_steps, 1)
            hold(pool, row_steps, n + 4)
            pool.tensor_tensor(rowf[0:P, :], move[0:P, :], idxf[0:P, q, :], ALU.add).then_inc(row_steps, 1)
            hold(pool, row_steps, n + 5)
            pool.tensor_copy(row[0:P, q, :], rowf[0:P, :]).then_inc(row_steps, 1)

        def scatter(b, q, t):
            if t == 0:
                hold(pool, row_steps, b * 6 + 7)
                hold(pool, job_done, sum_no(b, 3) + 1)
            else:
                hold(pool, scat, b * 64 + t * 16)
            pool.indirect_dma_start(upd, bass.IndirectOffsetOnAxis(ap=row[0:P, q, t:t + 1], axis=0),
                                    osum[0:P, t, :], None, compute_op=ALU.add).then_inc(scat, 16)

        def scattered(b):
            hold(pool, scat, b * 64 + 64)
            pool.sem_inc(osum_free, 1)

        def main(b, q, before=True, more=True, more2=True):
            between = {13: [lambda: duplicates(b, q)], 16: [lambda: rows_of(b, q)]}
            if more:
                n, r = b + 1, 1 - q
                between.update({
                    1: [lambda: split_x(n, r)], 5: [lambda: split_rest(n, r)], 6: [lambda: edge_scalars(n, r)],
                    8: [lambda: edge_vectors(n, r)], 10: [lambda: edge_rest(n, r)], 11: [lambda: edge_sum(n, r)]})
            if more2:
                def start():
                    hold(pool, ld[q], loaded(b + 2, q))
                    hold(pool, op_steps, b * 11 + 22)
                    hold(pool, casts, b * 5 + 10)
                between[19] = [start] + [lambda: gather(b + 2, q, (0,))]
                for t in range(1, T):
                    between[19 + 3 * t] = [lambda t=t: gather(b + 2, q, (t,))]
            if before:
                for t in range(T):
                    between[17 + 3 * t] = [lambda t=t: scatter(b - 1, 1 - q, t)]
                between[30] = [lambda: scattered(b - 1)]
            for n_, op in enumerate(POOL_OPS):
                for do in between.get(n_, []):
                    do()
                if op[0] == "add":
                    hold(pool, op_done, made(b, op[3]))
                    pool.tensor_tensor(prod[:, op[1], :], prod[:, op[1], :], prod[:, op[2], :], ALU.add).then_inc(pool_done, 1)
                else:
                    hold(pool, high_ready, b * NH + op[2] + 1)
                    pool.tensor_tensor(low[:, HIGHS[op[2]][1], :], prod[:, op[1], :], high[:, HIGHS[op[2]][1], :],
                                       ALU.subtract).then_inc(pool_done, 1)

        pool.sem_inc(row_steps, 1)
        pool.sem_inc(osum_free, 1)
        pool.sem_inc(pool_done, NPO)
        hold(pool, ld[0], loaded(0, 0))
        gather(0, 0, range(T))
        split_x(0, 0, first=True)
        split_rest(0, 0)
        edge_scalars(0, 0)
        edge_vectors(0, 0)
        edge_rest(0, 0)
        edge_sum(0, 0)
        hold(pool, ld[1], loaded(1, 1))
        hold(pool, casts, 5)
        hold(pool, op_steps, 11)
        gather(1, 1, range(T))
        main(0, 0, before=False)
        pool.wait_ge(zeroed, 32)
        sweep(pool, main, more2=False)
        main(NB - 1, 1, more=False, more2=False)
        for t in range(T):
            scatter(NB - 1, 1, t)
        scattered(NB - 1)

    @block.tensor
    def _(pe):
        def job_bank(b, q, j):
            return small[(q + j) % 2]

        def free(n):
            hold(pe, job_done, n - 1)

        def turn(bank_, srcs, K, ops, is_bf16=False):
            out_ = bank_[0:K, 0:512] if not is_bf16 else bank_[0:K, 0:256].bitcast(BF16)
            step = 128 if is_bf16 else P
            for t in range(T):
                m = pe.transpose(out_[:, t * step:t * step + P], srcs(t), ops[0:P, 0:P])
            return m

        def prep(b, q, j, first=False):
            bk = job_bank(b, q, j)
            n = job_no(b, j)
            if not (first and j < 2):
                free(n)
            if j == J_IDX:
                hold(pe, idxf_ready, b + 1)
                m = turn(bk, lambda t: idxf[0:P, q, t:t + 1].to_broadcast([P, P]), P, ident)
            elif j == J_X0:
                hold(pe, job_done, job_no(b, J_STK + 1) + 1)
                pe.matmul(bk[:, 0:W], sel_dup[:, 0, :], stk[:, q, 0, :], start=True, stop=False)
                m = pe.matmul(bk[:, 0:W], sel_dup[:, 1, :], stk[:, q, 1, :], start=False, stop=True)
            elif J_STK <= j < J_STK + 5:
                hold(pe, op_steps, b * 11 + 3)
                m = turn(bk, lambda t: parts[0:P, t, j - J_STK, :, :].rearrange("p a u -> p (a u)"), V3, identb, True)
            elif J_XE <= j < J_XE + 4:
                hold(pe, op_steps, b * 11 + 11)
                hold(pe, casts, b * 5 + 5)
                m = turn(bk, lambda t: xe[0:P, t, j - J_XE, :], 128, ident)
            elif j == J_S:
                m = turn(bk, lambda t: xsum[0:P, t, :], M1, ident)
            elif J_X1 <= j < J_X1 + 3:
                k = j - J_X1
                hold(pe, job_done, job_no(b, J_STK + 4) + 1)
                m = pe.matmul(bk[:, 0:W], sel_rep[:, :], stk[:, q, 2 + k, :], start=True, stop=True)
            elif j == J_A0:
                hold(pe, job_done, job_no(b, J_S) + 1)
                pe.matmul(bk[:, 0:W], msg_a[:, :], xeT[:, 0, :], start=True, stop=False)
                m = pe.matmul(bk[:, 0:W], msg_s[:, :], xsumT[:, :], start=False, stop=True)
            else:
                m = pe.matmul(bk[:, 0:W], msg_k[:, :], xeT[:, 1 + j - J_A1, :], start=True, stop=True)
            m.then_inc(job_ready, 1)

        def sums(b, q, h):
            free(sum_no(b, h))
            bk = small[(q + h) % 2]
            if h < 2:
                hold(pe, acc_out, b * 2 + 4)
            else:
                hold(pe, job_done, sum_no(b, 1) + 1)
                hold(pe, eq_ready, b + 1)
            for i in range(2):
                t = 2 * (h % 2) + i
                o = bk[0:P, i * D:(i + 1) * D]
                if h < 2:
                    pe.matmul(o[:, 0:M0], acc0T[:, t * P:(t + 1) * P], fold[:, :], start=True, stop=True)
                    m = pe.transpose(o[:, M0:D].rearrange("p (w k) -> p k w", k=3), acc1T[:, t * P:(t + 1) * P],
                                     ident[0:V3, 0:V3])
                else:
                    m = pe.matmul(o, eq[0:P, q, t, :], accs[0:P, t, :], start=True, stop=True)
            m.then_inc(job_ready, 1)

        def source(b, q, s):
            src = SOURCES[s]
            last = LAST[s - RING] if s >= RING else LAST[s - RING + NS] - NO
            pe.wait_ge(op_done, made(b, last))
            o = ring[s % RING][:, 0:W]
            if src[0] == "x0":
                c = src[1]
                m = pe.matmul(o, sel_x0[:, (c % 16) * 128:(c % 16 + 1) * 128], stk[:, q, c // 16, :], start=True, stop=True)
            elif src[0] == "x1":
                m = pe.matmul(o, sel_x1[:, src[2] * 128:(src[2] + 1) * 128], stk[:, q, 2 + src[1], :], start=True, stop=True)
            else:
                wt, hl, i = (w011, x0hl, 0) if src[0] == "z011" else (w101, a0hl, 1)
                if src[1] == 0:
                    pe.wait_ge(in_low, b * 2 + i + 1)
                for part in range(2):
                    m = pe.matmul(o, wt[:, part, 4 * src[1]:4 * src[1] + 4, :].rearrange("u w v -> u (w v)"), hl[:, q, :],
                                  start=(part == 0), stop=(part == 1))
            m.then_inc(src_ready, 1)

        first, last = {}, {}
        for u in range(NU):
            half = UNITS[u][0] == "sel"
            first.setdefault(half, u)
            last[half] = u
        assert UNITS[first[False]][0] == "hl"

        def contract(b, u):
            kind, n, k, slot, _, (by, op), h = UNITS[u]
            a, z = u == first[kind == "sel"], u == last[kind == "sel"]
            if kind == "hl":
                pe.wait_ge(high_ready, b * NH + h + 1)
                pe.matmul(acc[:, 0, 0:W], w_hl[:, n, :], high[:, HIGHS[h][1], :], start=a, stop=False, skip_group_check=True)
            if by == "dve":
                pe.wait_ge(op_done, made(b, op))
            else:
                pe.wait_ge(pool_done, (b + 1) * NPO + op + 1)
            if kind == "hl":
                m = pe.matmul(acc[:, 0, 0:W], w_hl[:, n, :], low[:, slot, :], start=False, stop=z,
                              skip_group_check=True)
            elif kind == "sel":
                at = V3 - (32 * k + 4 * n)
                m = pe.matmul(acc[0:V3, 1, 0:W], sel_w[:, at:at + V3], prod[:, slot, :], start=a, stop=z)
            else:
                m = pe.matmul(acc[0:M0, 0, 0:W], w_dir[:, n, :], prod[:, slot, :], start=a, stop=z, skip_group_check=True)
            m.then_inc(unit_done, 1)

        def main(b, q, before=True, more=True):
            jobs = {}
            if before:
                for h in range(NSUM):
                    jobs[SUM_AT[h]] = lambda h=h: sums(b - 1, 1 - q, h)
            if more:
                for j in range(NPREP):
                    jobs[PREP_AT[j]] = lambda j=j: prep(b + 1, 1 - q, j)
            for s in range(NS):
                source(b, q, s)
                if before:
                    for u in range(NU):
                        if UNITS[u][4] - NS == s:
                            contract(b - 1, u)
                if s == FIRST_UNIT:
                    pe.wait_ge(acc_out, b * 2 + 2)
                for u in range(NU):
                    if UNITS[u][4] == s:
                        contract(b, u)
                if s in jobs:
                    jobs[s]()

        pe.sem_inc(unit_done, NU)
        for j in range(NPREP):
            prep(0, 0, j, first=True)
        pe.wait_ge(job_ready, NPREP)
        pe.sem_inc(job_ready, NSUM)
        main(0, 0, before=False)
        sweep(pe, main)
        main(NB - 1, 1, more=False)
        for u in range(NU):
            if UNITS[u][4] >= NS:
                contract(NB - 1, u)
        pe.wait_ge(job_ready, NB * NJOB)
        pe.sem_inc(job_ready, NPREP)
        for h in range(NSUM):
            sums(NB - 1, 1, h)

    @block.vector
    def _(dve):
        def index(b, q):
            dve.wait_ge(ld[q], loaded(b, q))
            dve.tensor_copy(idxf[0:P, q, :], isrc[0:P, q, :]).then_inc(idxf_ready, 1)

        def equal(b, q, first=False):
            dve.wait_ge(job_done, job_no(b, J_IDX) + 1)
            if not first:
                dve.wait_ge(job_ready, sum_no(b - 2, 3) + 1)
                dve.wait_ge(row_steps, (b - 1) * 6 + 1)
            dve.tensor_tensor(eq[0:P, q, :, :], idxrow[0:P, :, :], idxf[0:P, q, :].unsqueeze(2).to_broadcast([P, T, P]),
                              ALU.is_equal).then_inc(eq_ready, 1)

        def input_low(b, q, i):
            dve.wait_ge(in_high, b * 2 + i + 1)
            whole, parts_ = ((x0T[64:128, :], x0hl), (a0T[64:128, q, :], a0hl))[i]
            dve.tensor_tensor(parts_[64:128, q, :], whole, parts_[64:128, q, :], ALU.subtract).then_inc(in_low, 1)

        def main(b, q, first=False, more=True):
            dve.wait_ge(job_done, job_no(b, NPREP - 1) + 1)
            for n, op in enumerate(DVE_OPS):
                g, i = n // (NO // GROUPS), n % (NO // GROUPS)
                if i == 0:
                    dve.wait_ge(unit_done, used(b, LAST_UNIT[g - 2] if g >= 2 else LAST_UNIT[g - 2] - NU))
                if op[0] == "add":
                    dve.wait_ge(op_done, made(b, n - 1))
                    dve.tensor_tensor(prod[:, op[1], :], prod[:, op[1], :], prod[:, op[2], :], ALU.add).then_inc(op_done, 1)
                elif op[0] == "low":
                    dve.wait_ge(high_ready, b * NH + op[2] + 1)
                    dve.tensor_tensor(low[:, HIGHS[op[2]][1], :], prod[:, op[1], :], high[:, HIGHS[op[2]][1], :],
                                      ALU.subtract).then_inc(op_done, 1)
                else:
                    dve.wait_ge(src_ready, b * NS + op[1] + 1)
                    source = ring[op[1] % RING][:, 0:W]
                    if op[0] == "z":
                        by = {"a1": a1T, "x1": x1T}[op[3]][:, q, :, :]
                        dve.tensor_tensor(prod[:, op[2]:op[2] + 3, :], source.unsqueeze(1).to_broadcast([128, 3, W]), by,
                                          ALU.mult).then_inc(op_done, 1)
                    else:
                        if op[2] == 22:
                            dve.wait_ge(op_done, made(b, n + 3 - NO // GROUPS))
                        if op[2] == 23:
                            dve.wait_ge(pool_done, (b + 1) * NPO + 4 * g - 2)
                        by = a0T[:, q, :] if op[3] == "a0" else a1T[:, q, op[4], :]
                        dve.tensor_tensor(prod[:, op[2], :], source, by, ALU.mult).then_inc(op_done, 1)
                if n == 5 and not first:
                    equal(b, q)
                if n == 10 and more:
                    dve.wait_ge(row_steps, b * 6 + 1)
                    index(b + 1, 1 - q)
                if n in LOW_AT and more:
                    input_low(b + 1, 1 - q, LOW_AT.index(n))

        dve.sem_inc(op_done, NO)
        index(0, 0)
        equal(0, 0, first=True)
        input_low(0, 0, 0)
        input_low(0, 0, 1)
        main(0, 0, first=True)
        sweep(dve, main)
        main(NB - 1, 1, more=False)

    @block.scalar
    def _(act):
        def prep(b, q, j, first=False):
            act.wait_ge(job_ready, job_no(b, j) + 1)
            bk = small[(q + j) % 2]
            if j == J_IDX:
                if not first:
                    act.wait_ge(eq_ready, b)
                to, of = idxrow[0:P, :, :].rearrange("p t e -> p (t e)"), bk[0:P, 0:W]
            elif j == J_X0:
                if not first:
                    act.wait_ge(op_done, made(b - 2, NO - 1))
                    act.wait_ge(in_low, b * 2 - 1)
                to, of = x0T[:, :], bk[:, 0:W]
            elif J_STK <= j < J_STK + 5:
                to = stk[:, q, j - J_STK, :].rearrange("p (t e) -> p t e", t=T)
                of = bk[0:V3, 0:256].bitcast(BF16).rearrange("p (t e) -> p t e", t=T)[:, :, 0:P]
            elif J_XE <= j < J_XE + 4:
                to, of = xeT[:, j - J_XE, :], bk[:, 0:W]
            elif j == J_S:
                to, of = xsumT[:, :], bk[0:M1, 0:W]
            elif J_X1 <= j < J_X1 + 3:
                to, of = x1T[:, q, j - J_X1, :], bk[:, 0:W]
            elif j == J_A0:
                to, of = a0T[:, q, :], bk[:, 0:W]
            else:
                to, of = a1T[:, q, j - J_A1, :], bk[:, 0:W]
            act.activation(to, of, ACT.Copy).then_inc(job_done, 1)
            if j in (J_X0, J_A0):
                act.wait_ge(job_done, job_no(b, j) + 1)
                act.activation((x0hl if j == J_X0 else a0hl)[:, q, :], to, ACT.Copy).then_inc(in_high, 1)

        def part_0(b, q):
            act.wait_ge(gat[q], gathered(b, q))
            act.activation(parts[0:P, :, 0:2, 0, :], xs[0:P, :, 0:M0].rearrange("p t (s u) -> p t s u", u=M1),
                           ACT.Copy).then_inc(casts, 1)
            act.activation(parts[0:P, :, 2:5, 0, :], xs[0:P, :, M0:D].rearrange("p t (u k) -> p t k u", k=3),
                           ACT.Copy).then_inc(casts, 1)

        def part_1(b):
            act.wait_ge(op_steps, b * 11 + 2)
            act.activation(parts[0:P, :, :, 1, :], rest[0:P, :, :, :], ACT.Copy).then_inc(casts, 1)

        def edge_copies(b):
            act.activation(xe[0:P, :, 0, 64:128], xd[0:P, :, 0:M0], ACT.Copy).then_inc(casts, 1)
            act.activation(xe[0:P, :, 1:4, 96:128], xd[0:P, :, M0:D].rearrange("p t (u k) -> p t k u", k=3),
                           ACT.Copy).then_inc(casts, 1)

        def high_part(b, h):
            slot, to, op, _ = HIGHS[h]
            u = next(u for u in range(NU) if UNITS[u][6] == (h - 4) % NH)
            act.wait_ge(op_done, made(b, op))
            act.wait_ge(unit_done, used(b, u if h >= 4 else u - NU))
            act.activation(high[:, to, :], prod[:, slot, :], ACT.Copy).then_inc(high_ready, 1)

        def updates(b):
            act.wait_ge(unit_done, used(b, NU - 1))
            act.activation(acc0T[:, :], acc[:, 0, 0:W], ACT.Copy).then_inc(acc_out, 1)
            act.activation(acc1T[:, :], acc[0:V3, 1, 0:W], ACT.Copy).then_inc(acc_out, 1)

        def sums(b, q, h):
            if h == 0:
                act.wait_ge(osum_free, b + 1)
            act.wait_ge(job_ready, sum_no(b, h) + 1)
            to, t = accs if h < 2 else osum, 2 * (h % 2)
            act.activation(to[0:P, t:t + 2, :].rearrange("p t f -> p (t f)"),
                           small[(q + h) % 2][0:P, 0:2 * D], ACT.Copy).then_inc(job_done, 1)

        def count(b):
            act.wait_ge(row_steps, b * 6 + 2)
            for t in range(T):
                if t:
                    act.wait_ge(cnt_ready, b * T + t)
                act.activation(junk[0:P, :], dup[0:P, t, :], ACT.Copy, accum_out=cnt[0:P, t:t + 1]).then_inc(cnt_ready, 1)

        def main(b, q, before=True, more=True):
            work = [(HIGHS[h][3] + 0.5, lambda h=h: high_part(b, h)) for h in range(NH)] + [(31.2, lambda: count(b))]
            if before:
                work += [(FIRST_UNIT - 0.6, lambda: updates(b - 1))]
                work += [(SUM_AT[h] + 0.2, lambda h=h: sums(b - 1, 1 - q, h)) for h in range(NSUM)]
            if more:
                work += [(PREP_AT[j] + 0.2, lambda j=j: prep(b + 1, 1 - q, j)) for j in range(NPREP)]
                work += [(2, lambda: part_0(b + 1, 1 - q)), (7, lambda: part_1(b + 1)), (13, lambda: edge_copies(b + 1))]
            for _, do in sorted(work, key=lambda w: w[0]):
                do()

        act.sem_inc(acc_out, 2)
        part_0(0, 0)
        part_1(0)
        edge_copies(0)
        for j in range(NPREP):
            prep(0, 0, j, first=True)
        act.wait_ge(job_done, NPREP)
        act.sem_inc(job_done, NSUM)
        main(0, 0, before=False)
        sweep(act, main)
        main(NB - 1, 1, more=False)
        act.wait_ge(job_done, NB * NJOB)
        act.sem_inc(job_done, NPREP)
        updates(NB - 1)
        for h in range(NSUM):
            sums(NB - 1, 1, h)

    ctx.close()


def layer1_edges(nc, tools, x, upd, agg, src_v, dst_v, ea3_v, ef_v, N, NB, ident, lower, spare, weights):
    lin_a, lin_b, nl0d, nl1e, fc1, fc2a, fc2e, wo_a, wo_s, wo_v = weights
    ctx = ExitStack()
    sb, bank, sem = tools(ctx)
    RE = NB * T
    G = 2 * V3

    rhat = sb("rhat", [128, RE, 3])
    eps = sb("eps1", [128, 1])

    with ExitStack() as c1:
        sb1, _, sem1 = tools(c1)
        ea3 = sb1("ea3", [128, RE, 3])
        sq = sb1("sq", [128, RE, 3])
        nrm = sb1("nrm", [128, RE])
        inv = sb1("inv", [128, RE])
        a_in = sem1("a_in")
        r_steps = sem1("r_steps")
        blk = c1.enter_context(nc.Block())

        @blk.sync
        def _(sp):
            sp.dma_start(ea3[0:P, :, :].rearrange("p c f -> p (c f)"), ea3_v).then_inc(a_in, 16)

        @blk.scalar
        def _(act):
            act.wait_ge(r_steps, 3)
            act.activation(nrm[0:P, :], nrm[0:P, :], ACT.Sqrt).then_inc(r_steps, 1)

        @blk.vector
        def _(dve):
            dve.memset(eps[:, :], EPS).then_inc(r_steps, 1)
            dve.wait_ge(a_in, 16)
            dve.tensor_tensor(sq[0:P, :, :], ea3[0:P, :, :], ea3[0:P, :, :], ALU.mult).then_inc(r_steps, 1)
            dve.wait_ge(r_steps, 2)
            dve.tensor_reduce(nrm[0:P, :], sq[0:P, :, :], AX.X, ALU.add).then_inc(r_steps, 1)
            dve.wait_ge(r_steps, 4)
            dve.reciprocal(inv[0:P, :], nrm[0:P, :]).then_inc(r_steps, 1)
            dve.wait_ge(r_steps, 5)
            dve.tensor_tensor(rhat[0:P, :, :], ea3[0:P, :, :], inv[0:P, :].unsqueeze(2).to_broadcast([P, RE, 3]),
                              ALU.mult).then_inc(r_steps, 1)

    isrc = sb("isrc1", [128, 2, T], I32)
    idst = sb("idst1", [128, 2, T], I32)
    ef = sb("ef", [128, 2, T, 64])
    xg = sb("xg", [128, 2, T, D])
    ug = sb("ug", [128, 2, T, D])
    rh6 = sb("rh6", [128, 2, T, 6])
    rh3 = sb("rh3", [128, T, 3, 3, M1])
    idxf = sb("idxf1", [128, 2, T])
    idxrow = sb("idxrow1", [128, T, P])
    eq = sb("eq1", [128, 2, T, P])
    dup = sb("dup1", [128, T, P])
    cnt = sb("cnt1", [128, T])
    later = sb("later1", [128, T])
    junk = sb("junk1", [128, P])
    gap = sb("gap1", [128, T])
    move = sb("move1", [128, T])
    rowf = sb("rowf1", [128, T])
    row = sb("row1", [128, 2, T], I32)
    xaT = sb("xaT", [128, W])
    xbT = sb("xbT", [M1, W])
    efT = sb("efT", [64, W])
    hT = sb("hT", [64, W])
    shT = sb("shT", [V3, 2, 3, W])
    w01T = sb("w01T", [128, 2, W])
    w234T = sb("w234T", [V3, 2, 3, W])
    y = sb("y1", [128, T, D])
    st = sb("st1", [128, T, 6])
    mv = sb("mv1", [128, T, 2])
    std = sb("std1", [128, T])
    rstd = sb("rstd1", [128, T])
    x1n = sb("x1n1", [128, T, D])
    n0T = sb("n0T", [M0, W])
    n1T = sb("n1T", [V3, W])
    tA = sb("tA", [128, W])
    t2 = sb("t2", [V3, W])
    b3 = sb("b3", [V3, W])
    t3 = sb("t3", [V3, W])
    c1_ = sb("c1_", [V3, W])
    c2_ = sb("c2_", [V3, W])
    c3_ = sb("c3_", [V3, W])
    t4 = sb("t4", [V3, W])
    qr = sb("qr", [128, T, M1, 3])
    o = sb("o1", [128, T, G])
    osum = sb("osum1", [128, T, G])

    abank = [bank(f"abank{i}") for i in range(4)]
    dbank = [bank(f"dbank{i}") for i in range(4)]

    ld = [sem("ld1_even"), sem("ld1_odd")]
    gat = [sem("gat1_even"), sem("gat1_odd")]
    a_ready = sem("a_ready1")
    a_done = sem("a_done1")
    d_ready = sem("d_ready1")
    d_done = sem("d_done1")
    rh6_ready = sem("rh6_ready")
    rh3_ready = sem("rh3_ready")
    row_steps = sem("row_steps1")
    cnt_ready = sem("cnt_ready1")
    idxf_ready = sem("idxf_ready1")
    eq_ready = sem("eq_ready1")
    prods = sem("prods1")
    o_steps = sem("o_steps")
    ln_steps = sem("ln_steps1")
    std_ready = sem("std_ready1")
    x1n_ready = sem("x1n_ready1")
    scat = sem("scat1")
    osum_free = sem("osum_free1")

    A_SUM, A_XT, A_IN, A_FC1, A_W = 0, 2, 4, 11, 12
    D_V, D_Y, D_OUT = 0, 4, 6

    def aj(b, j):
        return (b + 1) * 16 + j

    def dj(b, j):
        return (b + 1) * 8 + j

    def loaded(b, q):
        return (b - q) * 24 + 48

    def gathered(b, q):
        return (b - q) * 64 + 128

    def sweep(eng, iteration):
        iteration(0, 0, True, True)
        with eng.Fori(0, (NB - 4) // 2) as i:
            iteration(2 * i + 1, 1, True, True)
            iteration(2 * i + 2, 0, True, True)
        iteration(NB - 3, 1, True, True)
        iteration(NB - 2, 0, True, False)
        iteration(NB - 1, 1, False, False)

    block = ctx.enter_context(nc.Block())

    @block.sync
    def _(sp):
        def load(b, q):
            sp.dma_start(isrc[0:P, q, :], src_v[:, ds(b * T, T)]).then_inc(ld[q], 16)
            sp.dma_start(idst[0:P, q, :], dst_v[:, ds(b * T, T)]).then_inc(ld[q], 16)
            sp.dma_start(ef[0:P, q, :, :].rearrange("p t f -> p (t f)"), ef_v[:, ds(b * T * 64, T * 64)]).then_inc(ld[q], 16)

        def iteration(b, q, more, more2):
            if more2:
                sp.wait_ge(idxf_ready, b + 1)
                sp.wait_ge(a_ready, aj(b - 1, A_IN + 2) + 1)
                load(b + 2, q)

        load(0, 0)
        load(1, 1)
        sweep(sp, iteration)

    @block.gpsimd
    def _(pool):
        def gather(b, q, t):
            at = bass.IndirectOffsetOnAxis(ap=idst[0:P, q, t:t + 1], axis=0)
            pool.indirect_dma_start(xg[0:P, q, t, :], None, x, at).then_inc(gat[q], 16)
            pool.indirect_dma_start(ug[0:P, q, t, :], None, upd, at).then_inc(gat[q], 16)

        def units(b, q, first=False):
            if not first:
                hold(pool, d_done, dj(b - 2, D_OUT + 1) + 1)
            for j in range(2):
                pool.tensor_copy(rh6[0:P, q, :, 3 * j:3 * j + 3], rhat[0:P, ds(b * T, T), :]).then_inc(rh6_ready, 1)

        def rows_of(b, q):
            hold(pool, eq_ready, b + 1)
            n = b * 6 + 1
            pool.tensor_tensor(dup[0:P, :, :], eq[0:P, q, :, :], lower[0:P, :].unsqueeze(1).to_broadcast([P, T, P]),
                               ALU.mult).then_inc(row_steps, 1)
            pool.tensor_tensor(gap[0:P, :], spare[0:P, :].to_broadcast([P, T]), idxf[0:P, q, :],
                               ALU.subtract).then_inc(row_steps, 1)
            hold(pool, row_steps, n + 2)
            hold(pool, cnt_ready, b * T + T)
            pool.tensor_scalar(later[0:P, :], cnt[0:P, :], 1.0, None, ALU.min).then_inc(row_steps, 1)
            hold(pool, row_steps, n + 3)
            pool.tensor_tensor(move[0:P, :], later[0:P, :], gap[0:P, :], ALU.mult).then_inc(row_steps, 1)
            hold(pool, row_steps, n + 4)
            pool.tensor_tensor(rowf[0:P, :], move[0:P, :], idxf[0:P, q, :], ALU.add).then_inc(row_steps, 1)
            hold(pool, row_steps, n + 5)
            pool.tensor_copy(row[0:P, q, :], rowf[0:P, :]).then_inc(row_steps, 1)

        def scatter(b, q, t):
            if t:
                hold(pool, scat, b * 64 + t * 16)
            pool.indirect_dma_start(agg, bass.IndirectOffsetOnAxis(ap=row[0:P, q, t:t + 1], axis=0),
                                    osum[0:P, t, :], None, compute_op=ALU.add).then_inc(scat, 16)

        def scatter_ready(b):
            hold(pool, row_steps, b * 6 + 7)
            hold(pool, a_done, aj(b + 1, A_SUM + 1) + 1)

        def scattered(b):
            hold(pool, scat, b * 64 + 64)
            pool.sem_inc(osum_free, 1)

        def iteration(b, q, more, more2):
            before = not (isinstance(b, int) and b == 0)
            if before:
                scatter_ready(b - 1)
            if more2:
                hold(pool, ld[q], loaded(b + 2, q))
                hold(pool, a_ready, aj(b - 1, A_IN + 1) + 1)
                hold(pool, d_done, dj(b - 1, D_Y + 1) + 1)
            for t in range(T):
                if before:
                    scatter(b - 1, 1 - q, t)
                if more2:
                    gather(b + 2, q, t)
            if before:
                scattered(b - 1)
            rows_of(b, q)
            if more2:
                units(b + 2, q)

        pool.sem_inc(row_steps, 1)
        pool.sem_inc(osum_free, 1)
        for b in range(2):
            hold(pool, ld[b], loaded(b, b))
            for t in range(T):
                gather(b, b, t)
            units(b, b, first=True)
        sweep(pool, iteration)
        scatter_ready(NB - 1)
        for t in range(T):
            scatter(NB - 1, 1, t)
        scattered(NB - 1)

    @block.tensor
    def _(pe):
        def turn(o_, tiles, K, n_=P):
            for t in range(T):
                m = pe.transpose(o_[0:K, t * P:(t + 1) * P], tiles(t), ident[0:P, 0:P])
            m.then_inc(a_ready, 1)

        def abk(b, j):
            hold(pe, a_done, aj(b, j) - 3)
            return abank[j % 4]

        def dbk(b, j):
            hold(pe, d_done, dj(b, j) - 3)
            return dbank[j % 4]

        def inputs(b, q):
            i = b - 1
            hold(pe, gat[q], gathered(b, q))
            turn(abk(i, A_IN), lambda t: xg[0:P, q, t, 0:128], 128)
            turn(abk(i, A_IN + 1), lambda t: xg[0:P, q, t, 128:D], M1)
            hold(pe, ld[q], loaded(b, q))
            turn(abk(i, A_IN + 2), lambda t: ef[0:P, q, t, :], 64)
            hold(pe, idxf_ready, b + 1)
            turn(abk(i, A_IN + 3), lambda t: idxf[0:P, q, t:t + 1].to_broadcast([P, P]), P)
            hold(pe, rh3_ready, b * 3 + 3)
            for s in range(3):
                turn(abk(i, A_IN + 4 + s), lambda t: rh3[0:P, t, s, :, :].rearrange("p k m -> p (k m)"), V3)
            bk = abk(i, A_FC1)
            hold(pe, a_done, aj(i, A_IN + 2) + 1)
            pe.matmul(bk[0:64, 0:W], fc1[:, :], efT[:, :], start=True, stop=True).then_inc(a_ready, 1)

        def node_y(b):
            i = b - 1
            pe.wait_ge(a_done, aj(i, A_IN + 1) + 1)
            for h in range(2):
                bk = dbk(i, D_Y + h)
                for j in range(2):
                    cols = slice((2 * h + j) * P, (2 * h + j + 1) * P)
                    oo = bk[0:P, j * D:(j + 1) * D]
                    pe.matmul(oo, xaT[:, cols], lin_a[:, :], start=True, stop=False)
                    m = pe.matmul(oo, xbT[:, cols], lin_b[:, :], start=False, stop=True)
                m.then_inc(d_ready, 1)

        def edge_w(b):
            i = b - 1
            pe.wait_ge(a_done, aj(i, A_FC1) + 1)
            for j in range(4):
                bk = abk(i, A_W + j)
                wt, K = (fc2a[:, :], 128) if j == 0 else (fc2e[:, j - 1, :, :].rearrange("p k m -> p (k m)"), V3)
                pe.matmul(bk[0:K, 0:W], wt, hT[:, :], start=True, stop=True).then_inc(a_ready, 1)

        def sums(b, q):
            hold(pe, o_steps, b * 6 + 6)
            hold(pe, eq_ready, b + 1)
            for h in range(2):
                bk = abk(b + 1, A_SUM + h)
                for j in range(2):
                    t = 2 * h + j
                    m = pe.matmul(bk[0:P, j * G:(j + 1) * G], eq[0:P, q, t, :], o[0:P, t, :], start=True, stop=True)
                m.then_inc(a_ready, 1)

        def iteration(b, q, more, more2):
            if isinstance(b, int) and b == 0:
                pe.wait_ge(a_ready, aj(0, 0))
                pe.sem_inc(a_ready, 2)
            else:
                sums(b - 1, 1 - q)
            hold(pe, x1n_ready, b * 4 + 4)
            turn(abk(b, A_XT), lambda t: x1n[0:P, t, 0:M0], M0)
            turn(abk(b, A_XT + 1), lambda t: x1n[0:P, t, M0:D], V3)
            if more:
                inputs(b + 1, 1 - q)
            pe.wait_ge(a_done, aj(b, A_XT + 1) + 1)
            bk = dbk(b, D_V)
            pe.matmul(bk[:, 0:W], nl0d[:, :], n0T[:, :], start=True, stop=True).then_inc(d_ready, 1)
            for s in range(3):
                bk = dbk(b, D_V + 1 + s)
                pe.matmul(bk[0:V3, 0:W], nl1e[:, s, :], n1T[:, :], start=True, stop=True).then_inc(d_ready, 1)
            if more:
                node_y(b + 1)
                edge_w(b + 1)
            else:
                pe.wait_ge(d_ready, dj(b, D_Y))
                pe.sem_inc(d_ready, 2)
            pe.wait_ge(prods, b * 4 + 4)
            for h in range(2):
                bk = dbk(b, D_OUT + h)
                for j in range(2):
                    cols = slice((2 * h + j) * P, (2 * h + j + 1) * P)
                    oo = bk[0:P, j * 224:(j + 1) * 224]
                    pe.matmul(oo[:, 0:128], tA[:, cols], wo_a[:, :], start=True, stop=False)
                    pe.matmul(oo[:, 32:128], t3[:, cols], wo_s[:, :], start=False, stop=True)
                    pe.matmul(oo[:, 128:224], t2[:, cols], wo_v[:, 0, :, :].rearrange("p w k -> p (w k)"),
                              start=True, stop=False, skip_group_check=True)
                    m = pe.matmul(oo[:, 128:224], t4[:, cols], wo_v[:, 1, :, :].rearrange("p w k -> p (w k)"),
                                  start=False, stop=True, skip_group_check=True)
                m.then_inc(d_ready, 1)

        pe.sem_inc(a_ready, 4)
        pe.sem_inc(d_ready, 4)
        inputs(0, 0)
        node_y(0)
        edge_w(0)
        pe.wait_ge(d_ready, 6)
        pe.sem_inc(d_ready, 2)
        sweep(pe, iteration)
        pe.wait_ge(a_ready, aj(NB - 1, A_IN))
        pe.sem_inc(a_ready, 12)
        sums(NB - 1, 1)

    @block.scalar
    def _(act):
        def out(b, j, to, K, cols=W, func=ACT.Copy):
            act.wait_ge(a_ready, aj(b, j) + 1)
            act.activation(to, abank[j % 4][0:K, 0:cols], func).then_inc(a_done, 1)

        def inputs(b, q, first=False, second=False):
            i = b - 1
            out(i, A_IN, xaT[:, :], 128)
            out(i, A_IN + 1, xbT[:, :], M1)
            out(i, A_IN + 2, efT[:, :], 64)
            if not first:
                act.wait_ge(eq_ready, b)
            out(i, A_IN + 3, idxrow[0:P, :, :].rearrange("p t e -> p (t e)"), P)
            if not (first or second):
                act.wait_ge(prods, (b - 1) * 4)
            for s in range(3):
                out(i, A_IN + 4 + s, shT[:, q, s, :], V3)
            out(i, A_FC1, hT[:, :], 64, func=ACT.Relu)

        def edge_w(b, q):
            out(b - 1, A_W, w01T[:, q, :], 128)
            for j in range(3):
                out(b - 1, A_W + 1 + j, w234T[:, q, j, :], V3)

        def deviation(b):
            act.wait_ge(ln_steps, b * 9 + 8)
            act.activation(std[0:P, :], mv[0:P, :, 1], ACT.Sqrt, bias=eps[0:P, :]).then_inc(std_ready, 1)

        def sums(b):
            act.wait_ge(osum_free, b + 1)
            for h in range(2):
                out(b + 1, A_SUM + h, osum[0:P, 2 * h:2 * h + 2, :].rearrange("p t f -> p (t f)"), P, 2 * G)

        def count(b):
            act.wait_ge(row_steps, b * 6 + 2)
            for t in range(T):
                if t:
                    act.wait_ge(cnt_ready, b * T + t)
                act.activation(junk[0:P, :], dup[0:P, t, :], ACT.Copy, accum_out=cnt[0:P, t:t + 1]).then_inc(cnt_ready, 1)

        def unit_rows(b, q):
            act.wait_ge(rh6_ready, b * 2 + 2)
            for s in range(3):
                act.activation(rh3[0:P, :, s, :, :], rh6[0:P, q, :, s:s + 3].unsqueeze(3).to_broadcast([P, T, 3, M1]),
                               ACT.Copy).then_inc(rh3_ready, 1)

        def iteration(b, q, more, more2):
            if isinstance(b, int) and b == 0:
                act.wait_ge(a_done, aj(0, 0))
                act.sem_inc(a_done, 2)
            else:
                sums(b - 1)
            out(b, A_XT, n0T[:, :], M0)
            out(b, A_XT + 1, n1T[:, :], V3)
            if more:
                inputs(b + 1, 1 - q, second=isinstance(b, int) and b == 0)
            count(b)
            if more:
                edge_w(b + 1, 1 - q)
                deviation(b + 1)
            if more2:
                unit_rows(b + 2, q)

        unit_rows(0, 0)
        act.sem_inc(a_done, 4)
        inputs(0, 0, first=True)
        edge_w(0, 0)
        deviation(0)
        unit_rows(1, 1)
        sweep(act, iteration)
        act.wait_ge(a_done, aj(NB - 1, A_IN))
        act.sem_inc(a_done, 12)
        sums(NB - 1)

    @block.vector
    def _(dve):
        def index(b, q):
            dve.wait_ge(ld[q], loaded(b, q))
            dve.wait_ge(row_steps, b * 6 - 5)
            dve.tensor_copy(idxf[0:P, q, :], isrc[0:P, q, :]).then_inc(idxf_ready, 1)

        def equal(b, q):
            dve.wait_ge(a_done, aj(b - 1, A_IN + 3) + 1)
            if not (isinstance(b, int) and b <= 1):
                dve.wait_ge(a_ready, aj(b - 1, A_SUM + 1) + 1)
                dve.wait_ge(row_steps, b * 6 - 5)
            dve.tensor_tensor(eq[0:P, q, :, :], idxrow[0:P, :, :], idxf[0:P, q, :].unsqueeze(2).to_broadcast([P, T, P]),
                              ALU.is_equal).then_inc(eq_ready, 1)

        def products(b, q):
            dve.wait_ge(a_done, aj(b - 1, A_W + 3) + 1)
            bk = dbank
            dve.wait_ge(d_ready, dj(b, D_V) + 1)
            dve.tensor_tensor(tA[:, :], bk[0][:, 0:W], w01T[:, q, :], ALU.mult).then_inc(d_done, 1)
            dve.wait_ge(d_ready, dj(b, D_V + 1) + 1)
            dve.tensor_tensor(t2[:, :], bk[1][0:V3, 0:W], w234T[:, q, 0, :], ALU.mult).then_inc(prods, 1)
            dve.tensor_tensor(b3[:, :], bk[1][0:V3, 0:W], shT[:, q, 0, :], ALU.mult).then_inc(d_done, 1)
            dve.wait_ge(d_ready, dj(b, D_V + 2) + 1)
            dve.tensor_tensor(c1_[:, :], bk[2][0:V3, 0:W], shT[:, q, 2, :], ALU.mult).then_inc(d_done, 1)
            dve.wait_ge(d_ready, dj(b, D_V + 3) + 1)
            dve.tensor_tensor(c2_[:, :], bk[3][0:V3, 0:W], shT[:, q, 1, :], ALU.mult).then_inc(d_done, 1)
            dve.wait_ge(d_done, dj(b, D_V + 1) + 1)
            dve.tensor_tensor(t3[:, :], b3[:, :], w234T[:, q, 1, :], ALU.mult).then_inc(prods, 1)
            dve.wait_ge(d_done, dj(b, D_V + 3) + 1)
            dve.tensor_tensor(c3_[:, :], c1_[:, :], c2_[:, :], ALU.subtract).then_inc(prods, 1)
            dve.wait_ge(prods, b * 4 + 3)
            dve.tensor_tensor(t4[:, :], c3_[:, :], w234T[:, q, 2, :], ALU.mult).then_inc(prods, 1)

        def moments(b, q):
            dve.wait_ge(gat[q], gathered(b, q))
            for h in range(2):
                dve.wait_ge(d_ready, dj(b - 1, D_Y + h) + 1)
                dve.tensor_tensor(y[0:P, 2 * h:2 * h + 2, :].rearrange("p t f -> p (t f)"), dbank[D_Y % 4 + h][0:P, 0:2 * D],
                                  ug[0:P, q, 2 * h:2 * h + 2, :].rearrange("p t f -> p (t f)"), ALU.add).then_inc(d_done, 1)
            for t in range(T):
                dve.wait_ge(d_done, dj(b - 1, D_Y + t // 2) + 1)
                dve.bn_stats(st[0:P, t, :], y[0:P, t, :]).then_inc(ln_steps, 1)
            for t in range(T):
                hold(dve, ln_steps, b * 9 + t + 1)
                dve.bn_aggr(mv[0:P, t, :], st[0:P, t, :]).then_inc(ln_steps, 1)

        def normed(b):
            dve.wait_ge(std_ready, b + 1)
            dve.reciprocal(rstd[0:P, :], std[0:P, :]).then_inc(ln_steps, 1)
            dve.wait_ge(ln_steps, b * 9 + 9)
            if not (isinstance(b, int) and b == 0):
                dve.wait_ge(a_ready, aj(b - 1, A_XT + 1) + 1)
            for t in range(T):
                dve.tensor_scalar(x1n[0:P, t, :], y[0:P, t, :], mv[0:P, t, 0:1], rstd[0:P, t:t + 1], ALU.subtract,
                                  ALU.mult).then_inc(x1n_ready, 1)

        def outputs(b, q):
            if not (isinstance(b, int) and b == 0):
                dve.wait_ge(a_ready, aj(b, A_SUM + 1) + 1)
            for h in range(2):
                dve.wait_ge(d_ready, dj(b, D_OUT + h) + 1)
                g = dbank[D_OUT % 4 + h][0:P, 0:448].rearrange("p (t c) -> p t c", t=2)
                ts = slice(2 * h, 2 * h + 2)
                dve.tensor_copy(o[0:P, ts, 0:V3], g[:, :, 32:128]).then_inc(o_steps, 1)
                dve.tensor_tensor(qr[0:P, ts, :, :], g[:, :, 0:32].unsqueeze(3).to_broadcast([P, 2, M1, 3]),
                                  rh6[0:P, q, ts, 0:3].unsqueeze(2).to_broadcast([P, 2, M1, 3]), ALU.mult).then_inc(o_steps, 1)
                dve.wait_ge(o_steps, b * 6 + h * 3 + 2)
                dve.tensor_tensor(o[0:P, ts, V3:G], g[:, :, 128:224], qr[0:P, ts, :, :].rearrange("p t w k -> p t (w k)"),
                                  ALU.add).then_inc(o_steps, 1)
                dve.wait_ge(o_steps, b * 6 + h * 3 + 3)
                dve.sem_inc(d_done, 1)

        def iteration(b, q, more, more2):
            if more:
                index(b + 1, 1 - q)
            equal(b, q)
            products(b, q)
            if more:
                moments(b + 1, 1 - q)
            else:
                dve.wait_ge(d_done, dj(b, D_Y))
                dve.sem_inc(d_done, 2)
            outputs(b, q)
            if more:
                normed(b + 1)

        dve.sem_inc(d_done, 4)
        dve.wait_ge(ld[0], loaded(0, 0))
        dve.tensor_copy(idxf[0:P, 0, :], isrc[0:P, 0, :]).then_inc(idxf_ready, 1)
        moments(0, 0)
        normed(0)
        dve.wait_ge(d_done, 6)
        dve.sem_inc(d_done, 2)
        sweep(dve, iteration)

    ctx.close()


def nodes(nc, tools, x_v, upd_v, agg_v, out_v, NBN, ident, lin_a, lin_b, skip0, skip1):
    ctx = ExitStack()
    sb, bank, sem = tools(ctx)
    G = 2 * V3
    xn = sb("xn", [128, 2, T, D])
    un = sb("un", [128, 2, T, D])
    gn = sb("gn", [128, 2, T, G])
    xaT = sb("xaT2", [128, W])
    xbT = sb("xbT2", [M1, W])
    y = sb("y2", [128, T, D])
    st = sb("st2", [128, T, 6])
    mv = sb("mv2", [128, T, 2])
    ve = sb("ve2", [128, T])
    rs = sb("rs2", [128, T])
    half = sb("half", [128, T])
    x1n = sb("x1n2", [128, 2, T, D])
    n0T = sb("n0T2", [M0, W])
    n1T = sb("n1T2", [V3, W])
    a = sb("a2", [128, T, G])
    sg = sb("sg", [128, T, V3])
    f = sb("f2", [128, T, D])
    z = sb("z2", [128, T, D])
    st_z = sb("st_z", [128, T, 6])
    mv_z = sb("mv_z", [128, T, 2])
    ve_z = sb("ve_z", [128, T])
    rs_z = sb("rs_z", [128, T])
    ob = sb("ob", [128, 2, T, D])

    abank = [bank(f"nabank{i}") for i in range(4)]
    dbank = [bank(f"ndbank{i}") for i in range(4)]

    ld_x = [sem("ld_x_even"), sem("ld_x_odd")]
    ld_u = [sem("ld_u_even"), sem("ld_u_odd")]
    ld_g = [sem("ld_g_even"), sem("ld_g_odd")]
    a_ready = sem("a_ready2")
    a_done = sem("a_done2")
    d_ready = sem("d_ready2")
    d_done = sem("d_done2")
    half_ready = sem("half_ready")
    ln_y = sem("ln_y")
    rs_y = sem("rs_y")
    x1n_ready = sem("x1n_ready2")
    sg_ready = sem("sg_ready")
    f_ready = sem("f_ready")
    z_ready = sem("z_ready")
    ln_z = sem("ln_z")
    rs_zr = sem("rs_zr")
    ob_ready = sem("ob_ready")
    stored = [sem("stored_even"), sem("stored_odd")]

    A_XT, A_IN = 0, 2
    D_SK, D_Y = 0, 2

    def aj(b, j):
        return (b + 2) * 4 + j

    dj = aj

    def loaded(b, q):
        return (b - q) * 8 + 16

    def sweep(eng, iteration):
        iteration(0, 0, 3)
        with eng.Fori(0, (NBN - 4) // 2) as i:
            iteration(2 * i + 1, 1, 3)
            iteration(2 * i + 2, 0, 3)
        iteration(NBN - 3, 1, 2)
        iteration(NBN - 2, 0, 1)
        iteration(NBN - 1, 1, 0)

    def early(b, n):
        return isinstance(b, int) and b < n

    block = ctx.enter_context(nc.Block())

    @block.sync
    def _(sp):
        def load(b, q, to, of, n, arrived):
            sp.dma_start(to[0:P, q, :, :].rearrange("p t f -> p (t f)"), of[:, ds(b * n, n)]).then_inc(arrived[q], 16)

        def load_x(b, q):
            load(b, q, xn, x_v, T * D, ld_x)

        def load_ug(b, q):
            load(b, q, un, upd_v, T * D, ld_u)
            load(b, q, gn, agg_v, T * G, ld_g)

        def iteration(b, q, left):
            if left >= 3:
                sp.wait_ge(a_ready, aj(b - 1, A_IN + 1) + 1)
                load_x(b + 3, 1 - q)
            if left >= 2:
                sp.wait_ge(d_done, dj(b, D_SK + 1) + 1)
                load_ug(b + 2, q)
            if not early(b, 1):
                sp.wait_ge(ob_ready, b * 4)
                store(b - 1, 1 - q)

        def store(b, q):
            sp.dma_start(out_v[:, ds(b * T * D, T * D)], ob[0:P, q, :, :].rearrange("p t f -> p (t f)")).then_inc(stored[q], 16)

        load_x(0, 0)
        load_x(1, 1)
        load_ug(0, 0)
        load_ug(1, 1)
        sp.wait_ge(a_ready, aj(-2, A_IN + 1) + 1)
        load_x(2, 0)
        sweep(sp, iteration)
        sp.wait_ge(ob_ready, NBN * 4)
        store(NBN - 1, 1)
        sp.wait_ge(stored[0], NBN // 2 * 16)
        sp.wait_ge(stored[1], NBN // 2 * 16)

    @block.tensor
    def _(pe):
        def turn(o_, tiles, K):
            for t in range(T):
                m = pe.transpose(o_[0:K, t * P:(t + 1) * P], tiles(t), ident[0:P, 0:P])
            m.then_inc(a_ready, 1)

        def abk(b, j):
            if not early(b, -1):
                hold(pe, a_done, aj(b, j) - 3)
            return abank[j % 4]

        def dbk(b, j):
            if not early(b, -1):
                hold(pe, d_done, dj(b, j) - 3)
            return dbank[j % 4]

        def inputs(b, q):
            hold(pe, ld_x[q], loaded(b, q))
            turn(abk(b - 2, A_IN), lambda t: xn[0:P, q, t, 0:128], 128)
            turn(abk(b - 2, A_IN + 1), lambda t: xn[0:P, q, t, 128:D], M1)

        def node_y(b):
            pe.wait_ge(a_done, aj(b - 2, A_IN + 1) + 1)
            for h in range(2):
                bk = dbk(b - 2, D_Y + h)
                for j in range(2):
                    cols = slice((2 * h + j) * P, (2 * h + j + 1) * P)
                    oo = bk[0:P, j * D:(j + 1) * D]
                    pe.matmul(oo, xaT[:, cols], lin_a[:, :], start=True, stop=False)
                    m = pe.matmul(oo, xbT[:, cols], lin_b[:, :], start=False, stop=True)
                m.then_inc(d_ready, 1)

        def iteration(b, q, left):
            hold(pe, x1n_ready, b * 4 + 4)
            turn(abk(b, A_XT), lambda t: x1n[0:P, q, t, 0:M0], M0)
            turn(abk(b, A_XT + 1), lambda t: x1n[0:P, q, t, M0:D], V3)
            if left >= 2:
                inputs(b + 2, q)
            else:
                pe.wait_ge(a_ready, aj(b, A_IN))
                pe.sem_inc(a_ready, 2)
            pe.wait_ge(a_done, aj(b, A_XT + 1) + 1)
            for h in range(2):
                bk = dbk(b, D_SK + h)
                for j in range(2):
                    cols = slice((2 * h + j) * P, (2 * h + j + 1) * P)
                    oo = bk[0:P, j * G:(j + 1) * G]
                    pe.matmul(oo[:, 0:V3], n0T[:, cols], skip0[:, :], start=True, stop=True)
                    m = pe.matmul(oo[:, V3:G], n1T[:, cols], skip1[:, :, :].rearrange("p w k -> p (w k)"), start=True, stop=True)
                m.then_inc(d_ready, 1)
            if left >= 2:
                node_y(b + 2)
            else:
                pe.wait_ge(d_ready, dj(b, D_Y))
                pe.sem_inc(d_ready, 2)

        for b in range(2):
            if b:
                pe.wait_ge(a_ready, aj(b - 2, 0))
                pe.wait_ge(d_ready, dj(b - 2, 0))
            pe.sem_inc(a_ready, 2)
            pe.sem_inc(d_ready, 2)
            inputs(b, b)
            node_y(b)
        sweep(pe, iteration)

    @block.scalar
    def _(act):
        def out(b, j, to, K):
            act.wait_ge(a_ready, aj(b, j) + 1)
            act.activation(to, abank[j % 4][0:K, 0:W], ACT.Copy).then_inc(a_done, 1)

        def inputs(b):
            out(b - 2, A_IN, xaT[:, :], 128)
            out(b - 2, A_IN + 1, xbT[:, :], M1)

        def iteration(b, q, left):
            out(b, A_XT, n0T[:, :], M0)
            out(b, A_XT + 1, n1T[:, :], V3)
            if left >= 2:
                inputs(b + 2)
            else:
                act.wait_ge(a_done, aj(b, A_IN))
                act.sem_inc(a_done, 2)
            act.wait_ge(d_done, dj(b, D_SK + 1) + 1)
            if not early(b, 1):
                act.wait_ge(f_ready, b * 2)
            act.activation(sg[0:P, :, :], a[0:P, :, 0:V3], ACT.Sigmoid).then_inc(sg_ready, 1)

        for b in range(2):
            if b:
                act.wait_ge(a_done, aj(b - 2, 0))
            act.sem_inc(a_done, 2)
            inputs(b)
        sweep(act, iteration)

    @block.gpsimd
    def _(pool):
        def power(b, moments, mv_, ve_, rs_, done):
            hold(pool, moments, b * 8 + 8)
            pool.tensor_scalar(ve_[0:P, :], mv_[0:P, :, 1], EPS, None, ALU.add).then_inc(done, 1)
            hold(pool, done, b * 2 + 1)
            pool.tensor_tensor(rs_[0:P, :], ve_[0:P, :], half[0:P, :], ALU.pow).then_inc(done, 1)

        def iteration(b, q, left):
            if left:
                power(b + 1, ln_y, mv, ve, rs, rs_y)
            if not early(b, 1):
                hold(pool, z_ready, b)
                power(b - 1, ln_z, mv_z, ve_z, rs_z, rs_zr)
            hold(pool, sg_ready, b + 1)
            pool.tensor_tensor(f[0:P, :, 0:M0], a[0:P, :, 0:M0], sg[0:P, :, 0:M0], ALU.mult).then_inc(f_ready, 1)
            pool.tensor_tensor(f[0:P, :, M0:D].rearrange("p t (w k) -> p t w k", k=3),
                               a[0:P, :, V3:G].rearrange("p t (w k) -> p t w k", k=3),
                               sg[0:P, :, M0:V3].unsqueeze(3).to_broadcast([P, T, M1, 3]), ALU.mult).then_inc(f_ready, 1)

        pool.memset(half[:, :], -0.5).then_inc(half_ready, 1)
        pool.wait_ge(half_ready, 1)
        power(0, ln_y, mv, ve, rs, rs_y)
        sweep(pool, iteration)
        power(NBN - 1, ln_z, mv_z, ve_z, rs_z, rs_zr)

    @block.vector
    def _(dve):
        def moments_of(v, st_, mv_, b, steps):
            for t in range(T):
                dve.bn_stats(st_[0:P, t, :], v[0:P, t, :]).then_inc(steps, 1)
            for t in range(T):
                hold(dve, steps, b * 8 + t + 1)
                dve.bn_aggr(mv_[0:P, t, :], st_[0:P, t, :]).then_inc(steps, 1)

        def moments(b, q):
            dve.wait_ge(ld_u[q], loaded(b, q))
            if not early(b, 1):
                dve.wait_ge(x1n_ready, b * 4)
            for h in range(2):
                dve.wait_ge(d_ready, dj(b - 2, D_Y + h) + 1)
                dve.tensor_tensor(y[0:P, 2 * h:2 * h + 2, :].rearrange("p t f -> p (t f)"), dbank[D_Y + h][0:P, 0:2 * D],
                                  un[0:P, q, 2 * h:2 * h + 2, :].rearrange("p t f -> p (t f)"), ALU.add).then_inc(d_done, 1)
            dve.wait_ge(d_done, dj(b - 2, D_Y + 1) + 1)
            moments_of(y, st, mv, b, ln_y)

        def scaled(to, v, mv_, rs_, done):
            for t in range(T):
                dve.tensor_scalar(to[:, t, :], v[0:P, t, :], mv_[0:P, t, 0:1], rs_[0:P, t:t + 1], ALU.subtract,
                                  ALU.mult).then_inc(done, 1)

        def normed(b, q):
            dve.wait_ge(rs_y, b * 2 + 2)
            if not early(b, 2):
                dve.wait_ge(z_ready, b - 1)
            scaled(x1n[0:P, q], y, mv, rs, x1n_ready)

        def summed(b, q):
            dve.wait_ge(f_ready, b * 2 + 2)
            if not early(b, 1):
                dve.wait_ge(ob_ready, b * 4)
            dve.tensor_tensor(z[0:P, :, :], f[0:P, :, :], x1n[0:P, q, :, :], ALU.add).then_inc(z_ready, 1)
            dve.wait_ge(z_ready, b + 1)
            moments_of(z, st_z, mv_z, b, ln_z)

        def result(b, q):
            dve.wait_ge(rs_zr, b * 2 + 2)
            if not early(b, 2):
                dve.wait_ge(stored[q], (b - q) * 8)
            scaled(ob[0:P, q], z, mv_z, rs_z, ob_ready)

        def iteration(b, q, left):
            if left:
                moments(b + 1, 1 - q)
            else:
                dve.wait_ge(d_done, dj(b - 1, D_Y))
                dve.sem_inc(d_done, 2)
            if not early(b, 1):
                summed(b - 1, 1 - q)
            dve.wait_ge(ld_g[q], loaded(b, q))
            for h in range(2):
                dve.wait_ge(d_ready, dj(b, D_SK + h) + 1)
                dve.tensor_tensor(a[0:P, 2 * h:2 * h + 2, :].rearrange("p t f -> p (t f)"), dbank[D_SK + h][0:P, 0:2 * G],
                                  gn[0:P, q, 2 * h:2 * h + 2, :].rearrange("p t f -> p (t f)"), ALU.add).then_inc(d_done, 1)
            if left:
                normed(b + 1, 1 - q)
            if not early(b, 1):
                result(b - 1, 1 - q)

        dve.sem_inc(d_done, 2)
        moments(0, 0)
        normed(0, 0)
        dve.wait_ge(d_done, dj(-1, 0))
        dve.sem_inc(d_done, 2)
        sweep(dve, iteration)
        summed(NBN - 1, 1)
        result(NBN - 1, 1)

    ctx.close()


_INS = ['x', 'src', 'dst', 'edge_attr_3', 'edge_attr_4', 'edge_attr_64', 'L0_gnn_wm000', 'L0_gnn_wm011',
        'L0_gnn_wm101', 'L0_gnn_wm110', 'L0_gnn_lm0', 'L0_gnn_lm1', 'L0_gnn_wu000', 'L0_gnn_wu011', 'L0_gnn_wu101',
        'L0_gnn_wu110', 'L0_gnn_lu0', 'L0_gnn_lu1', 'L1_gnn_W_skip0', 'L1_gnn_W_skip1', 'L1_gnn_W_nl0',
        'L1_gnn_W_nl1', 'L1_gnn_W_fc1', 'L1_gnn_W_fc2', 'L1_gnn_W_out_s', 'L1_gnn_W_out_v']


def kernel(**inputs):
    import numpy as _np
    import concourse.bacc as _bacc
    from concourse import mybir as _mybir
    from concourse.bass_utils import run_bass_kernel_spmd as _run

    nc = _bacc.Bacc("TRN2", target_bir_lowering=False, num_devices=1)
    arrays, args = {}, []
    for name in _INS:
        a = _np.ascontiguousarray(inputs[name])
        arrays[f"in_{name}_dram"] = a
        args.append(nc.dram_tensor(f"in_{name}_dram", a.shape, _mybir.dt.from_np(a.dtype), kind="ExternalInput").ap())
    shape = inputs['x'].shape
    args.append(nc.dram_tensor("out_0_dram", shape, _mybir.dt.from_np(_np.dtype('float32')), kind="ExternalOutput").ap())
    build(nc, *args)
    r = _run(nc, [arrays], core_ids=[0])
    return r.results[0]["out_0_dram"]
```

```python
from contextlib import ExitStack

import numpy as np

import concourse.bass as bass
from concourse import mybir

F32 = mybir.dt.float32
F32R = mybir.dt.float32r
BF16 = mybir.dt.bfloat16
I32 = mybir.dt.int32
ALU = mybir.AluOpType
ACT = mybir.ActivationFunctionType
AX = mybir.AxisListType

P = 125
T = 4
W = P * T
M0, M1, D = 64, 32, 160
V3 = 3 * M1
EPS = 1e-5

SOURCES, DVE_OPS, POOL_OPS, HIGHS, UNITS = [], [], [], [], []
GROUPS = 8
NG = 9
for _g in range(GROUPS):
    _s, _o, _n, _q = NG * _g, 11 * (_g % 2), len(DVE_OPS), _g % 2
    SOURCES += [("z011", _g), ("x0", 4 * _g), ("z101", _g), ("x0", 4 * _g + 1), ("x1", 0, _g),
                ("x0", 4 * _g + 2), ("x1", 1, _g), ("x1", 2, _g), ("x0", 4 * _g + 3)]
    _h = len(HIGHS)
    HIGHS += [(22, _q, _n + 3, _s + 3), (23, 2, _n + 5, _s + 5)]
    DVE_OPS += [("z", _s, _o, "a1"), ("mul", _s + 1, _o + 10, "a0", 0), ("z", _s + 2, _o + 3, "x1"),
                ("mul", _s + 3, 22, "a0", 0), ("mul", _s + 4, _o + 6, "a1", 0), ("mul", _s + 5, 23, "a0", 0),
                ("mul", _s + 6, _o + 7, "a1", 1), ("add", _o + 6, _o + 7), ("mul", _s + 7, _o + 8, "a1", 2),
                ("mul", _s + 8, _o + 9, "a0", 0), ("add", _o + 6, _o + 8)]
    UNITS += [("w", 3 * _g + 1, 0, _o + 9, _s + 10 + 2 * (_g == 0), ("dve", _n + 9), None),
              ("hl", 2 * _g, 0, _q, _s + 11, ("pool", len(POOL_OPS) + 1), _h),
              ("w", 3 * _g, 0, _o + 10, _s + 8 + 4 * (_g == 0), ("dve", _n + 1), None),
              ("w", 3 * _g + 2, 0, _o + 6, _s + 12, ("dve", _n + 10), None),
              ("hl", 2 * _g + 1, 0, 2, _s + 13, ("pool", len(POOL_OPS) + 4), _h + 1)]
    UNITS += [("sel", _g, _k, _o + _k, _s + 14 + _k, ("pool", len(POOL_OPS) + (0, 2, 3)[_k]), None) for _k in range(3)]
    POOL_OPS += [("add", _o, _o + 3, _n + 2), ("low", 22, _h), ("add", _o + 1, _o + 4, _n + 2),
                 ("add", _o + 2, _o + 5, _n + 2), ("low", 23, _h + 1)]
FIRST_UNIT = 9
UNITS = sorted((u[0:4] + (max(u[4], FIRST_UNIT),) + u[5:7] for u in UNITS), key=lambda u: u[4])
NS, NO, NPO, NH, NU = len(SOURCES), len(DVE_OPS), len(POOL_OPS), len(HIGHS), len(UNITS)
LAST = {op[1]: n for n, op in enumerate(DVE_OPS) if op[0] in ("z", "mul")}
RING = 4
SLOTS = 24


def group_of(unit):
    kind, n = unit[0:2]
    return {"hl": n // 2, "w": n // 3, "sel": n}[kind]


LAST_UNIT = [max(u for u in range(NU) if group_of(UNITS[u]) == g) for g in range(GROUPS)]

J_IDX, J_STK, J_X0, J_XE, J_S, J_X1, J_A0, J_A1 = 0, 1, 6, 7, 11, 12, 15, 16
NPREP = 19
NSUM = 4
NJOB = NPREP + NSUM
SUM_AT = [10, 12, 14, 16]
PREP_AT = [18] + [20 + 2 * j for j in range(NPREP - 1)]
LOW_AT = [4 * NO // GROUPS, 6 * NO // GROUPS]


PASSED = []


def ds(start, size):
    return bass.DynSlice(start, size)


def hold(eng, sem, value):
    eng.wait_ge(sem, value)
    eng.sem_inc(PASSED[0], 1)


def build(nc, x, src, dst, edge_attr_3, edge_attr_4, edge_attr_64, wm000, wm011, wm101, wm110, lm0, lm1,
          wu000, wu011, wu101, wu110, lu0, lu1, w_skip0, w_skip1, w_nl0, w_nl1, w_fc1, w_fc2,
          w_out_s, w_out_v, out):
    N, E = x.shape[0], src.shape[0]
    RN, RE = N // P, E // P
    NBN, NB = RN // T, RE // T
    assert N == P * T * NBN and E == P * T * NB and NB % 2 == 0 and NB >= 4 and NBN % 2 == 0

    upd = nc.dram_tensor("upd", (N + P, D), F32, kind="Internal").ap()
    agg = nc.dram_tensor("agg", (N + P, 2 * V3), F32, kind="Internal").ap()

    src_v = src.rearrange("(p c) -> p c", p=P)
    dst_v = dst.rearrange("(p c) -> p c", p=P)
    ea4_v = edge_attr_4.rearrange("(p c) f -> p (c f)", p=P)
    ea3_v = edge_attr_3.rearrange("(p c) f -> p (c f)", p=P)
    ef_v = edge_attr_64.rearrange("(p c) f -> p (c f)", p=P)
    x_v = x.rearrange("(p c) f -> p (c f)", p=P)
    out_v = out.rearrange("(p c) f -> p (c f)", p=P)
    upd_v = upd[0:N, :].rearrange("(p c) f -> p (c f)", p=P)
    agg_v = agg[0:N, :].rearrange("(p c) f -> p (c f)", p=P)
    upd_r = upd[0:N, :].rearrange("(p c) f -> p c f", p=P)
    agg_r = agg[0:N, :].rearrange("(p c) f -> p c f", p=P)

    top = ExitStack()

    def tools(ctx):
        def sb(name, shape, dt=F32):
            return ctx.enter_context(nc.sbuf_tensor(name, shape, dt))

        def bank(name, dt=F32):
            return ctx.enter_context(nc.psum_tensor(name, [128, 2048 // (4 if dt == F32 else 2)], dt))

        def sem(name):
            return ctx.enter_context(nc.semaphore(name))
        return sb, bank, sem

    with top:
        sb, bank, sem = tools(top)
        PASSED[:] = [sem("passed")]
        ident = sb("ident", [128, 128])
        identb = sb("identb", [128, 128], BF16)
        lower = sb("lower", [128, P])
        spare = sb("spare", [128, 1])
        zero = sb("zero", [128, 4 * 2 * V3])
        lin0 = sb("lin0", [M0, M0])
        lin1 = sb("lin1", [V3, M1, 3])
        nl0d = sb("nl0d", [M0, 128])
        nl1e = sb("nl1e", [V3, 3, V3])
        fc1 = sb("fc1", [M0, 128])
        fc2a = sb("fc2a", [128, 128])
        fc2e = sb("fc2e", [128, 3, 3, M1])
        wo_a = sb("wo_a", [128, 128])
        wo_s = sb("wo_s", [V3, V3])
        wo_v = sb("wo_v", [V3, 2, M1, 3])
        skip0 = sb("skip0", [M0, V3])
        skip1 = sb("skip1", [V3, M1, 3])

        with ExitStack() as c0:
            sb0, _, sem0 = tools(c0)
            k_in = sb0("k_in", [V3, 6])
            k_out = sb0("k_out", [V3, 3])
            lu0_s = sb0("lu0_s", [M0, M0])
            lu1_r = sb0("lu1_r", [V3, M1])
            nl1_r = sb0("nl1_r", [V3, M1])
            sk1_r = sb0("sk1_r", [V3, M1])
            wov_r = sb0("wov_r", [V3, 2, M1])
            raw_s = sb0("raw_s", [V3, V3])
            raw_a = sb0("raw_a", [128, 128])
            w_in = sem0("w_in")
            c_pool = sem0("c_pool")
            c_vec = sem0("c_vec")
            block = c0.enter_context(nc.Block())

            @block.sync
            def _(sp):
                rows = [(lu0_s[:, :], lu0), (nl0d[:, 0:M0], w_nl0), (nl0d[:, M0:128], w_nl0), (fc1[:, 0:64], w_fc1),
                        (fc1[:, 64:128], w_fc1), (fc2a[0:64, :], w_fc2[:, 0:128]), (fc2a[64:128, :], w_fc2[:, 0:128]),
                        (skip0[:, :], w_skip0),
                        (raw_s[0:32, :], w_out_s[64:96, :])]
                rows += [(raw_s[32 * k:32 * k + 32, :], w_out_s[64:96, :]) for k in range(1, 3)]
                rows += [(fc2e[h:h + 64, j, k, :], w_fc2[:, 128 + 32 * j:160 + 32 * j])
                         for j in range(3) for k in range(3) for h in (0, 64)]
                for to, of in rows:
                    sp.dma_start(to, of).then_inc(w_in, 16)
                for k in range(3):
                    for j in range(2):
                        sp.dma_start(wov_r[32 * k:32 * k + 32, j, :],
                                     w_out_v[64 + 32 * j:96 + 32 * j, :]).then_inc(w_in, 16)
                    for tile, of in ((lu1_r, lu1), (nl1_r, w_nl1), (sk1_r, w_skip1)):
                        sp.dma_start(tile[k:k + 3 * (M1 - 1) + 1:3, :], of).then_inc(w_in, 16)
                sp.wait_ge(c_pool, 3)
                sp.dma_start(raw_a[64:128, 0:32], w_out_v[0:64, :]).then_inc(w_in, 16)
                sp.dma_start(raw_a[0:64, 32:128], w_out_s[0:64, :]).then_inc(w_in, 16)

            n_in = 16 * (9 + 2 + 18 + 3 * 5 + 2)

            @block.gpsimd
            def _(pool):
                pool.memset(ident[:, :], 0.0).then_inc(c_pool, 1)
                pool.memset(lower[:, :], 1.0).then_inc(c_pool, 1)
                pool.memset(raw_a[:, :], 0.0).then_inc(c_pool, 1)
                pool.memset(zero[:, :], 0.0).then_inc(c_pool, 1)
                pool.wait_ge(c_pool, 4)
                pool.affine_select(out=ident[:, :], in_=ident[:, :], compare_op=ALU.not_equal, fill=1.0, base=0,
                                   pattern=[[-1, 128]], channel_multiplier=1).then_inc(c_pool, 1)
                pool.affine_select(out=lower[:, :], in_=lower[:, :], compare_op=ALU.is_gt, fill=0.0, base=0,
                                   pattern=[[-1, P]], channel_multiplier=1).then_inc(c_pool, 1)
                pool.iota(spare[:, :], pattern=[[0, 1]], base=N, channel_multiplier=1,
                          allow_small_or_imprecise_dtypes=True).then_inc(c_pool, 1)
                pool.wait_ge(c_pool, 7)

            @block.vector
            def _(dve):
                n = [0]

                def step(ins):
                    n[0] += 1
                    ins.then_inc(c_vec, 1)
                    dve.wait_ge(c_vec, n[0])

                dve.wait_ge(c_pool, 7)
                step(dve.tensor_copy(identb[:, :], ident[:, :]))
                step(dve.tensor_reduce(k_in[:, 0:3], ident[0:V3, 0:V3].rearrange("p (m k) -> p k m", k=3), AX.X, ALU.add))
                step(dve.tensor_reduce(k_out[:, :], ident[0:V3, 0:V3].rearrange("p (k m) -> p k m", k=3), AX.X, ALU.add))
                step(dve.tensor_copy(k_in[:, 3:6], k_in[:, 0:3]))
                dve.wait_ge(w_in, n_in)

                def spread(to, rows, mask):
                    return dve.tensor_tensor(to, rows.unsqueeze(2).to_broadcast([V3, M1, 3]),
                                             mask.unsqueeze(1).to_broadcast([V3, M1, 3]), ALU.mult)

                step(spread(lin1[:, :, :], lu1_r[:, :], k_in[:, 0:3]))
                step(spread(skip1[:, :, :], sk1_r[:, :], k_in[:, 0:3]))
                for j in range(2):
                    step(spread(wo_v[:, j, :, :], wov_r[:, j, :], k_out[:, :]))
                for s in range(3):
                    step(dve.tensor_tensor(nl1e[:, s, :].rearrange("p (k m) -> p k m", k=3),
                                           nl1_r[:, :].unsqueeze(1).to_broadcast([V3, 3, M1]),
                                           k_in[:, s:s + 3].unsqueeze(2).to_broadcast([V3, 3, M1]), ALU.mult))
                step(dve.tensor_scalar(wo_v[:, 0, :, :], wo_v[:, 0, :, :], 1 / 32, None, ALU.mult))
                step(dve.tensor_scalar(wo_v[:, 1, :, :], wo_v[:, 1, :, :], float(np.sqrt(1.5) / 32), None, ALU.mult))
                step(dve.tensor_scalar(wo_s[:, :], raw_s[:, :], 1 / 32, None, ALU.mult))
                step(dve.tensor_scalar(wo_a[:, 32:128], raw_a[:, 32:128], 1 / 32, None, ALU.mult))
                step(dve.tensor_scalar(wo_a[:, 0:32], raw_a[:, 0:32], float(np.sqrt(3.0) / 32), None, ALU.mult))
                step(dve.tensor_scalar(lin1[:, :, :], lin1[:, :, :], float(1 / np.sqrt(M1)), None, ALU.mult))
                step(dve.scalar_tensor_tensor(out=lin1[:, :, :], in0=ident[0:V3, 0:V3].rearrange("p (m k) -> p m k", k=3),
                                              scalar=2.0, in1=lin1[:, :, :], op0=ALU.mult, op1=ALU.add))
                step(dve.tensor_scalar(lu0_s[:, :], lu0_s[:, :], float(1 / np.sqrt(M0)), None, ALU.mult))
                step(dve.scalar_tensor_tensor(out=lin0[:, :], in0=ident[0:M0, 0:M0], scalar=2.0, in1=lu0_s[:, :],
                                              op0=ALU.mult, op1=ALU.add))

        layer0_edges(nc, tools, x, upd, agg, upd_r, agg_r, src_v, dst_v, ea4_v, N, NB, RN,
                     ident, identb, lower, spare, zero,
                     (wm000, wm011, wm101, wm110, lm0, lm1, wu000, wu011, wu101, wu110))
        layer1_edges(nc, tools, x, upd, agg, src_v, dst_v, ea3_v, ef_v, N, NB, ident, lower, spare,
                     (lin0, lin1, nl0d, nl1e, fc1, fc2a, fc2e, wo_a, wo_s, wo_v))
        nodes(nc, tools, x_v, upd_v, agg_v, out_v, NBN, ident, lin0, lin1, skip0, skip1)


def layer0_edges(nc, tools, x, upd, agg, upd_r, agg_r, src_v, dst_v, ea4_v, N, NB, RN,
                 ident, identb, lower, spare, zero, weights):
    wm000, wm011, wm101, wm110, lm0, lm1, wu000, wu011, wu101, wu110 = weights
    ctx = ExitStack()
    sb, bank, sem = tools(ctx)
    s_tp0 = float(1 / np.sqrt(M0 * M0 + M1 * M1))
    s_tp1 = float(1 / np.sqrt(2 * M0 * M1))
    s_msg = float(1 / np.sqrt(M0 + M1))
    i3 = float(1 / np.sqrt(3.0))

    w_hl = sb("w_hl", [128, 16, 128], F32R)
    w_dir = sb("w_dir", [128, 24, M0])
    w011 = sb("w011", [128, 2, M1, M1], F32R)
    w101 = sb("w101", [128, 2, M1, M1], F32R)
    sel_x0 = sb("sel_x0", [V3, 2 * M1 // 4 * 128], BF16)
    sel_x1 = sb("sel_x1", [V3, 8 * 128], BF16)
    sel_rep = sb("sel_rep", [V3, 128], BF16)
    sel_dup = sb("sel_dup", [V3, 2, 128], BF16)
    fold = sb("fold", [128, M0])
    sel_w = sb("sel_w", [128, 2 * V3])
    msg_a = sb("msg_a", [128, 128])
    msg_s = sb("msg_s", [M1, 128])
    msg_k = sb("msg_k", [128, 128])

    with ExitStack() as c1:
        sb1, _, sem1 = tools(c1)
        raw = sb1("raw_w", [128, 40, M0])
        t011 = sb1("t011", [128, M1, M1])
        t101 = sb1("t101", [128, M1, M1])
        w_in = sem1("w_in0")
        done = sem1("w_made0")
        blk = c1.enter_context(nc.Block())

        @blk.sync
        def _(sp):
            sp.dma_start(raw[:, 0:32, :], wu000.rearrange("(c u) v w -> (u v) c w", u=2)).then_inc(w_in, 16)
            sp.dma_start(raw[:, 32:40, :], wu110.rearrange("(c u) v w -> (u v) c w", u=4)).then_inc(w_in, 16)
            for j in range(2):
                rows = slice(64 * j, 64 * j + 64)
                sp.dma_start(t011[rows, :, :], wu011).then_inc(w_in, 16)
                sp.dma_start(t101[rows, :, :], wu101.rearrange("u v w -> v u w")).then_inc(w_in, 16)
            for j in range(2):
                c = slice(64 * j, 64 * j + 64)
                sp.dma_start(msg_a[0:64, c], wm000[:, 0, :]).then_inc(w_in, 16)
                sp.dma_start(msg_a[64:128, c], lm0).then_inc(w_in, 16)
                sp.dma_start(msg_s[:, c], wm110[:, 0, :]).then_inc(w_in, 16)
            for j in range(4):
                c = slice(32 * j, 32 * j + 32)
                sp.dma_start(msg_k[0:64, c], wm011[:, 0, :]).then_inc(w_in, 16)
                sp.dma_start(msg_k[64:96, c], wm101[:, 0, :]).then_inc(w_in, 16)
                sp.dma_start(msg_k[96:128, c], lm1).then_inc(w_in, 16)

        @blk.vector
        def _(dve):
            n = [0]

            def step(ins):
                n[0] += 1
                ins.then_inc(done, 1)
                dve.wait_ge(done, n[0])

            for r in range(3):
                rows = slice(32 * r, 32 * r + 32)
                one = identb[rows, rows]
                step(dve.tensor_copy(sel_x0[rows, :].rearrange("p (u v) -> p u v", v=64),
                                     one.unsqueeze(2).to_broadcast([32, 32, 64])))
                step(dve.tensor_copy(sel_x1[rows, :].rearrange("p (u v) -> p u v", v=32),
                                     one.unsqueeze(2).to_broadcast([32, 32, 32])))
                step(dve.tensor_copy(sel_rep[rows, :].rearrange("p (j u) -> p j u", u=32),
                                     one.unsqueeze(1).to_broadcast([32, 4, 32])))
            step(dve.memset(sel_dup[:, :, :], 0.0))
            for r in range(3):
                rows = slice(32 * r, 32 * r + 32)
                for c in range(4):
                    step(dve.tensor_copy(sel_dup[rows, c % 2, 32 * c:32 * c + 32], identb[rows, rows]))
            for j in range(2):
                rows = slice(64 * j, 64 * j + 64)
                step(dve.tensor_copy(fold[rows, :], ident[rows, rows]))
            step(dve.memset(sel_w[:, :], 0.0))
            step(dve.tensor_reduce(sel_w[:, V3:V3 + 4], ident[:, :].rearrange("p (j v) -> p j v", v=32), AX.X, ALU.add))
            step(dve.tensor_scalar(sel_w[:, V3:V3 + 4], sel_w[:, V3:V3 + 4], s_tp1, None, ALU.mult))
            dve.wait_ge(w_in, 16 * (6 + 6 + 12))
            step(dve.tensor_scalar(raw[:, 0:32, :], raw[:, 0:32, :], s_tp0, None, ALU.mult))
            step(dve.tensor_scalar(raw[:, 32:40, :], raw[:, 32:40, :], s_tp0 * i3, None, ALU.mult))
            by_group = raw[:, 0:32, :].rearrange("p (g c) w -> p g c w", c=4)
            hl = w_hl[:, :, :].rearrange("p (g c) w -> p g c w", c=2)
            step(dve.tensor_copy(hl[:, :, :, 0:M0], by_group[:, :, 1:3, :]))
            step(dve.tensor_tensor(hl[:, :, :, M0:128], by_group[:, :, 1:3, :], hl[:, :, :, 0:M0], ALU.subtract))
            direct = w_dir[:, :, :].rearrange("p (g c) w -> p g c w", c=3)
            for c, of in ((0, by_group[:, :, 0, :]), (1, by_group[:, :, 3, :]), (2, raw[:, 32:40, :])):
                step(dve.tensor_copy(direct[:, :, c, :], of))
            for to, of in ((w011, t011[:, :, :].rearrange("u v w -> u w v")), (w101, t101[:, :, :].rearrange("v u w -> v w u"))):
                step(dve.tensor_copy(to[:, 0, :, :], of))
                step(dve.tensor_tensor(to[:, 1, :, :], of, to[:, 0, :, :], ALU.subtract))
            step(dve.tensor_scalar(msg_a[0:64, :], msg_a[0:64, :], s_msg, None, ALU.mult))
            step(dve.tensor_scalar(msg_a[64:128, :], msg_a[64:128, :], float(1 / np.sqrt(M0)), None, ALU.mult))
            step(dve.tensor_scalar(msg_s[:, :], msg_s[:, :], s_msg * i3, None, ALU.mult))
            step(dve.tensor_scalar(msg_k[0:96, :], msg_k[0:96, :], s_msg, None, ALU.mult))
            step(dve.tensor_scalar(msg_k[96:128, :], msg_k[96:128, :], float(1 / np.sqrt(M1)), None, ALU.mult))

    isrc = sb("isrc", [128, 2, T], I32)
    idst = sb("idst", [128, 2, T], I32)
    ea4 = sb("ea4", [128, 2, T, 4])
    xs = sb("xs", [128, T, D])
    xd = sb("xd", [128, T, D])
    xe = sb("xe", [128, T, 4, 128])
    xsum = sb("xsum", [128, T, M1])
    parts = sb("parts", [128, T, 5, 3, M1], BF16)
    rest = sb("rest", [128, T, 5, M1])
    xpe = rest[:, :, 0:3, :]
    idxf = sb("idxf", [128, 2, T])
    idxrow = sb("idxrow", [128, T, P])
    eq = sb("eq", [128, 2, T, P])
    dup = sb("dup", [128, T, P])
    cnt = sb("cnt", [128, T])
    later = sb("later", [128, T])
    junk = sb("junk", [128, P])
    gap = sb("gap", [128, T])
    move = sb("move", [128, T])
    rowf = sb("rowf", [128, T])
    row = sb("row", [128, 2, T], I32)
    xeT = sb("xeT", [128, 4, W])
    xsumT = sb("xsumT", [M1, W])
    stk = sb("stk", [V3, 2, 5, W], BF16)
    x0hl = sb("x0hl", [128, 2, W], F32R)
    a0hl = sb("a0hl", [128, 2, W], F32R)
    a0T = sb("a0T", [128, 2, W])
    a1T = sb("a1T", [128, 2, 3, W])
    x1T = sb("x1T", [128, 2, 3, W])
    prod = sb("prod", [128, SLOTS, W])
    high = sb("high", [128, 3, W], F32R)
    low = sb("low", [128, 3, W], F32R)
    acc0T = sb("acc0T", [128, W])
    x0T = acc0T
    acc1T = sb("acc1T", [V3, W])
    accs = sb("accs", [128, T, D])
    osum = sb("osum", [128, T, D])

    ring = [bank(f"ring{i}") for i in range(RING)]
    acc = ctx.enter_context(nc.psum_tensor("acc", [128, 2, 512], F32))
    small = [bank(f"small{i}") for i in range(2)]

    ld = [sem("ld0_even"), sem("ld0_odd")]
    gat = [sem("gat0_even"), sem("gat0_odd")]
    op_steps = sem("op_steps")
    casts = sem("casts")
    row_steps = sem("row_steps")
    cnt_ready = sem("cnt_ready")
    idxf_ready = sem("idxf_ready")
    eq_ready = sem("eq_ready")
    job_ready = sem("job_ready")
    job_done = sem("job_done")
    src_ready = sem("src_ready")
    op_done = sem("op_done")
    pool_done = sem("pool_done")
    high_ready = sem("high_ready")
    in_high = sem("in_high")
    in_low = sem("in_low")
    unit_done = sem("unit_done")
    acc_out = sem("acc_out")
    zeroed = sem("zeroed")
    zeroed_agg = sem("zeroed_agg")
    scat = sem("scat0")
    osum_free = sem("osum_free0")

    def loaded(b, q):
        return (b - q) * 24 + 48

    def gathered(b, q):
        return (b - q) * 64 + 128

    def job_no(b, j):
        return b * NJOB + j

    def sum_no(b, h):
        return (b + 2) * NJOB - NSUM + h

    def made(b, o):
        return (b + 1) * NO + o + 1

    def used(b, u):
        return (b + 1) * NU + u + 1

    block = ctx.enter_context(nc.Block())

    def sweep(eng, main, **last):
        with eng.Fori(0, (NB - 4) // 2) as i:
            main(2 * i + 1, 1)
            main(2 * i + 2, 0)
        main(NB - 3, 1)
        main(NB - 2, 0, **last)

    @block.sync
    def _(sp):
        def load(b, q):
            sp.dma_start(isrc[0:P, q, :], src_v[:, ds(b * T, T)]).then_inc(ld[q], 16)
            sp.dma_start(idst[0:P, q, :], dst_v[:, ds(b * T, T)]).then_inc(ld[q], 16)
            sp.dma_start(ea4[0:P, q, :, :].rearrange("p t f -> p (t f)"), ea4_v[:, ds(b * 16, 16)]).then_inc(ld[q], 16)

        def clear(rows_v, c, n, f, done):
            m = max(k for k in (1, 2, 4) if n % k == 0)
            sp.dma_start(rows_v[:, ds(c, n), :].rearrange("p (r m) f -> p r (m f)", m=m),
                         zero[0:P, 0:m * f].unsqueeze(1).to_broadcast([P, n // m, m * f])).then_inc(done, 16)

        def next_load(b, q):
            hold(sp, op_steps, b * 11 + 11)
            hold(sp, idxf_ready, b + 1)
            load(b + 2, q)

        n_upd, n_agg = RN // GROUPS, RN // (NB // 2)
        assert RN % GROUPS == 0 and RN % (NB // 2) == 0
        load(0, 0)
        load(1, 1)
        for g in range(GROUPS):
            sp.wait_ge(src_ready, g * NG + 1)
            clear(upd_r, g * n_upd, n_upd, D, zeroed)
            if g < 2:
                next_load(g, g)
        sp.dma_start(upd[N:N + P, :], zero[0:P, 0:D]).then_inc(zeroed, 16)
        sp.dma_start(agg[N:N + P, :], zero[0:P, 0:2 * V3]).then_inc(zeroed_agg, 16)
        for c in range(2):
            clear(agg_r, c * n_agg, n_agg, 2 * V3, zeroed_agg)
        with sp.Fori(0, (NB - 4) // 2) as i:
            for q in range(2):
                next_load(2 * i + 2 + q, q)
            clear(agg_r, (i + 2) * n_agg, n_agg, 2 * V3, zeroed_agg)
        sp.wait_ge(zeroed_agg, (NB // 2 + 1) * 16)

    @block.gpsimd
    def _(pool):
        def gather(b, q, tiles):
            for t in tiles:
                pool.indirect_dma_start(xs[0:P, t, :], None, x,
                                        bass.IndirectOffsetOnAxis(ap=isrc[0:P, q, t:t + 1], axis=0)).then_inc(gat[q], 16)
                pool.indirect_dma_start(xd[0:P, t, :], None, x,
                                        bass.IndirectOffsetOnAxis(ap=idst[0:P, q, t:t + 1], axis=0)).then_inc(gat[q], 16)

        def split_x(b, q, first=False):
            hold(pool, gat[q], gathered(b, q))
            if not first:
                hold(pool, job_ready, job_no(b - 1, J_S) + 1)
            s0 = xs[0:P, :, 0:M0].rearrange("p t (s u) -> p t s u", u=M1)
            s1 = xs[0:P, :, M0:D].rearrange("p t (u k) -> p t k u", k=3)
            hold(pool, casts, b * 5 + 2)
            pool.tensor_tensor(rest[0:P, :, 0:2, :], s0, parts[0:P, :, 0:2, 0, :], ALU.subtract).then_inc(op_steps, 1)
            pool.tensor_tensor(rest[0:P, :, 2:5, :], s1, parts[0:P, :, 2:5, 0, :], ALU.subtract).then_inc(op_steps, 1)

        def split_rest(b, q):
            hold(pool, casts, b * 5 + 3)
            pool.tensor_tensor(parts[0:P, :, :, 2, :], rest[0:P, :, :, :], parts[0:P, :, :, 1, :],
                               ALU.subtract).then_inc(op_steps, 1)

        d0 = xd[0:P, :, 0:M0]
        d1k = xd[0:P, :, M0:D].rearrange("p t (u k) -> p t k u", k=3)

        def edge_scalars(b, q):
            e0 = ea4[0:P, q, :, 3:4]
            hold(pool, op_steps, b * 11 + 3)
            pool.tensor_tensor(xpe[0:P], d1k, ea4[0:P, q, :, 0:3].unsqueeze(3).to_broadcast([P, T, 3, M1]),
                               ALU.mult).then_inc(op_steps, 1)
            pool.tensor_tensor(xe[0:P, :, 0, 0:64], d0, e0.to_broadcast([P, T, M0]), ALU.mult).then_inc(op_steps, 1)

        def edge_vectors(b, q):
            for k in range(3):
                pool.tensor_tensor(xe[0:P, :, 1 + k, 0:64], d0, ea4[0:P, q, :, k:k + 1].to_broadcast([P, T, M0]),
                                   ALU.mult).then_inc(op_steps, 1)

        def edge_rest(b, q):
            pool.tensor_tensor(xe[0:P, :, 1:4, 64:96], d1k, ea4[0:P, q, :, 3:4].unsqueeze(3).to_broadcast([P, T, 3, M1]),
                               ALU.mult).then_inc(op_steps, 1)

        def edge_sum(b, q):
            hold(pool, op_steps, b * 11 + 9)
            pool.tensor_tensor(xsum[0:P, :, :], xpe[0:P, :, 0, :], xpe[0:P, :, 1, :], ALU.add).then_inc(op_steps, 1)
            hold(pool, op_steps, b * 11 + 10)
            pool.tensor_tensor(xsum[0:P, :, :], xsum[0:P, :, :], xpe[0:P, :, 2, :], ALU.add).then_inc(op_steps, 1)

        def duplicates(b, q):
            hold(pool, eq_ready, b + 1)
            pool.tensor_tensor(dup[0:P, :, :], eq[0:P, q, :, :], lower[0:P, :].unsqueeze(1).to_broadcast([P, T, P]),
                               ALU.mult).then_inc(row_steps, 1)
            pool.tensor_tensor(gap[0:P, :], spare[0:P, :].to_broadcast([P, T]), idxf[0:P, q, :],
                               ALU.subtract).then_inc(row_steps, 1)

        def rows_of(b, q):
            n = b * 6 + 1
            hold(pool, row_steps, n + 2)
            hold(pool, cnt_ready, b * T + T)
            pool.tensor_scalar(later[0:P, :], cnt[0:P, :], 1.0, None, ALU.min).then_inc(row_steps, 1)
            hold(pool, row_steps, n + 3)
            pool.tensor_tensor(move[0:P, :], later[0:P, :], gap[0:P, :], ALU.mult).then_inc(row_steps, 1)
            hold(pool, row_steps, n + 4)
            pool.tensor_tensor(rowf[0:P, :], move[0:P, :], idxf[0:P, q, :], ALU.add).then_inc(row_steps, 1)
            hold(pool, row_steps, n + 5)
            pool.tensor_copy(row[0:P, q, :], rowf[0:P, :]).then_inc(row_steps, 1)

        def scatter(b, q, t):
            if t == 0:
                hold(pool, row_steps, b * 6 + 7)
                hold(pool, job_done, sum_no(b, 3) + 1)
            else:
                hold(pool, scat, b * 64 + t * 16)
            pool.indirect_dma_start(upd, bass.IndirectOffsetOnAxis(ap=row[0:P, q, t:t + 1], axis=0),
                                    osum[0:P, t, :], None, compute_op=ALU.add).then_inc(scat, 16)

        def scattered(b):
            hold(pool, scat, b * 64 + 64)
            pool.sem_inc(osum_free, 1)

        def main(b, q, before=True, more=True, more2=True):
            n, r = b + 1, 1 - q
            for i, op in enumerate(POOL_OPS):
                if more and i == 1:
                    split_x(n, r)
                if more and i == 6:
                    split_rest(n, r)
                if more and i == 7:
                    edge_scalars(n, r)
                if more and i == 10:
                    edge_vectors(n, r)
                if more and i == 12:
                    edge_rest(n, r)
                if more and i == 13:
                    edge_sum(n, r)
                if i == 16:
                    duplicates(b, q)
                if i == 20:
                    rows_of(b, q)
                if before and i in (21, 25, 29, 33):
                    scatter(b - 1, r, (i - 21) // 4)
                if more2 and i == 23:
                    hold(pool, ld[q], loaded(b + 2, q))
                    hold(pool, op_steps, b * 11 + 22)
                    hold(pool, casts, b * 5 + 10)
                if more2 and i in (23, 27, 31, 35):
                    gather(b + 2, q, ((i - 23) // 4,))
                if before and i == 37:
                    scattered(b - 1)
                if op[0] == "add":
                    hold(pool, op_done, made(b, op[3]))
                    pool.tensor_tensor(prod[:, op[1], :], prod[:, op[1], :], prod[:, op[2], :], ALU.add).then_inc(pool_done, 1)
                else:
                    hold(pool, high_ready, b * NH + op[2] + 1)
                    pool.tensor_tensor(low[:, HIGHS[op[2]][1], :], prod[:, op[1], :], high[:, HIGHS[op[2]][1], :],
                                       ALU.subtract).then_inc(pool_done, 1)

        pool.sem_inc(row_steps, 1)
        pool.sem_inc(osum_free, 1)
        pool.sem_inc(pool_done, NPO)
        hold(pool, ld[0], loaded(0, 0))
        gather(0, 0, range(T))
        split_x(0, 0, first=True)
        split_rest(0, 0)
        edge_scalars(0, 0)
        edge_vectors(0, 0)
        edge_rest(0, 0)
        edge_sum(0, 0)
        hold(pool, ld[1], loaded(1, 1))
        hold(pool, casts, 5)
        hold(pool, op_steps, 11)
        gather(1, 1, range(T))
        main(0, 0, before=False)
        pool.wait_ge(zeroed, (GROUPS + 1) * 16)
        sweep(pool, main, more2=False)
        main(NB - 1, 1, more=False, more2=False)
        for t in range(T):
            scatter(NB - 1, 1, t)
        scattered(NB - 1)

    @block.tensor
    def _(pe):
        def job_bank(b, q, j):
            return small[(q + j) % 2]

        def free(n):
            hold(pe, job_done, n - 1)

        def turn(bank_, srcs, K, ops, is_bf16=False):
            out_ = bank_[0:K, 0:512] if not is_bf16 else bank_[0:K, 0:256].bitcast(BF16)
            step = 128 if is_bf16 else P
            for t in range(T):
                m = pe.transpose(out_[:, t * step:t * step + P], srcs(t), ops[0:P, 0:P])
            return m

        def prep(b, q, j, first=False):
            bk = job_bank(b, q, j)
            n = job_no(b, j)
            if not (first and j < 2):
                free(n)
            if j == J_IDX:
                hold(pe, idxf_ready, b + 1)
                m = turn(bk, lambda t: idxf[0:P, q, t:t + 1].to_broadcast([P, P]), P, ident)
            elif j == J_X0:
                hold(pe, job_done, job_no(b, J_STK + 1) + 1)
                pe.matmul(bk[:, 0:W], sel_dup[:, 0, :], stk[:, q, 0, :], start=True, stop=False)
                m = pe.matmul(bk[:, 0:W], sel_dup[:, 1, :], stk[:, q, 1, :], start=False, stop=True)
            elif J_STK <= j < J_STK + 5:
                hold(pe, op_steps, b * 11 + 3)
                m = turn(bk, lambda t: parts[0:P, t, j - J_STK, :, :].rearrange("p a u -> p (a u)"), V3, identb, True)
            elif J_XE <= j < J_XE + 4:
                hold(pe, op_steps, b * 11 + 11)
                hold(pe, casts, b * 5 + 5)
                m = turn(bk, lambda t: xe[0:P, t, j - J_XE, :], 128, ident)
            elif j == J_S:
                m = turn(bk, lambda t: xsum[0:P, t, :], M1, ident)
            elif J_X1 <= j < J_X1 + 3:
                k = j - J_X1
                hold(pe, job_done, job_no(b, J_STK + 4) + 1)
                m = pe.matmul(bk[:, 0:W], sel_rep[:, :], stk[:, q, 2 + k, :], start=True, stop=True)
            elif j == J_A0:
                hold(pe, job_done, job_no(b, J_S) + 1)
                pe.matmul(bk[:, 0:W], msg_a[:, :], xeT[:, 0, :], start=True, stop=False)
                m = pe.matmul(bk[:, 0:W], msg_s[:, :], xsumT[:, :], start=False, stop=True)
            else:
                m = pe.matmul(bk[:, 0:W], msg_k[:, :], xeT[:, 1 + j - J_A1, :], start=True, stop=True)
            m.then_inc(job_ready, 1)

        def sums(b, q, h):
            free(sum_no(b, h))
            bk = small[(q + h) % 2]
            if h < 2:
                hold(pe, acc_out, b * 2 + 4)
            else:
                hold(pe, job_done, sum_no(b, 1) + 1)
                hold(pe, eq_ready, b + 1)
            for i in range(2):
                t = 2 * (h % 2) + i
                o = bk[0:P, i * D:(i + 1) * D]
                if h < 2:
                    pe.matmul(o[:, 0:M0], acc0T[:, t * P:(t + 1) * P], fold[:, :], start=True, stop=True)
                    m = pe.transpose(o[:, M0:D].rearrange("p (w k) -> p k w", k=3), acc1T[:, t * P:(t + 1) * P],
                                     ident[0:V3, 0:V3])
                else:
                    m = pe.matmul(o, eq[0:P, q, t, :], accs[0:P, t, :], start=True, stop=True)
            m.then_inc(job_ready, 1)

        def source(b, q, s):
            src = SOURCES[s]
            last = LAST[s - RING] if s >= RING else LAST[s - RING + NS] - NO
            pe.wait_ge(op_done, made(b, last))
            o = ring[s % RING][:, 0:W]
            if src[0] == "x0":
                c = src[1]
                m = pe.matmul(o, sel_x0[:, (c % 16) * 128:(c % 16 + 1) * 128], stk[:, q, c // 16, :], start=True, stop=True)
            elif src[0] == "x1":
                m = pe.matmul(o, sel_x1[:, src[2] * 128:(src[2] + 1) * 128], stk[:, q, 2 + src[1], :], start=True, stop=True)
            else:
                wt, hl, i = (w011, x0hl, 0) if src[0] == "z011" else (w101, a0hl, 1)
                if src[1] == 0:
                    pe.wait_ge(in_low, b * 2 + i + 1)
                for part in range(2):
                    m = pe.matmul(o, wt[:, part, 4 * src[1]:4 * src[1] + 4, :].rearrange("u w v -> u (w v)"), hl[:, q, :],
                                  start=(part == 0), stop=(part == 1))
            m.then_inc(src_ready, 1)

        first, last = {}, {}
        for u in range(NU):
            half = UNITS[u][0] == "sel"
            first.setdefault(half, u)
            last[half] = u
        assert UNITS[first[False]][0] == "hl"

        def contract(b, u):
            kind, n, k, slot, _, (by, op), h = UNITS[u]
            a, z = u == first[kind == "sel"], u == last[kind == "sel"]
            if kind == "hl":
                pe.wait_ge(high_ready, b * NH + h + 1)
                pe.matmul(acc[:, 0, 0:W], w_hl[:, n, :], high[:, HIGHS[h][1], :], start=a, stop=False, skip_group_check=True)
            if by == "dve":
                pe.wait_ge(op_done, made(b, op))
            else:
                pe.wait_ge(pool_done, (b + 1) * NPO + op + 1)
            if kind == "hl":
                m = pe.matmul(acc[:, 0, 0:W], w_hl[:, n, :], low[:, slot, :], start=False, stop=z,
                              skip_group_check=True)
            elif kind == "sel":
                at = V3 - (32 * k + 4 * n)
                m = pe.matmul(acc[0:V3, 1, 0:W], sel_w[:, at:at + V3], prod[:, slot, :], start=a, stop=z)
            else:
                m = pe.matmul(acc[0:M0, 0, 0:W], w_dir[:, n, :], prod[:, slot, :], start=a, stop=z, skip_group_check=True)
            m.then_inc(unit_done, 1)

        def main(b, q, before=True, more=True):
            for s in range(NS):
                source(b, q, s)
                if before:
                    for u in range(NU):
                        if UNITS[u][4] - NS == s:
                            contract(b - 1, u)
                if s == FIRST_UNIT:
                    pe.wait_ge(acc_out, b * 2 + 2)
                for u in range(NU):
                    if UNITS[u][4] == s:
                        contract(b, u)
                if before and s in SUM_AT:
                    sums(b - 1, 1 - q, SUM_AT.index(s))
                if more and s in PREP_AT:
                    prep(b + 1, 1 - q, PREP_AT.index(s))

        pe.sem_inc(unit_done, NU)
        for j in range(NPREP):
            prep(0, 0, j, first=True)
        pe.wait_ge(job_ready, NPREP)
        pe.sem_inc(job_ready, NSUM)
        main(0, 0, before=False)
        sweep(pe, main)
        main(NB - 1, 1, more=False)
        for u in range(NU):
            if UNITS[u][4] >= NS:
                contract(NB - 1, u)
        pe.wait_ge(job_ready, NB * NJOB)
        pe.sem_inc(job_ready, NPREP)
        for h in range(NSUM):
            sums(NB - 1, 1, h)

    @block.vector
    def _(dve):
        def index(b, q):
            dve.wait_ge(ld[q], loaded(b, q))
            dve.tensor_copy(idxf[0:P, q, :], isrc[0:P, q, :]).then_inc(idxf_ready, 1)

        def equal(b, q, first=False):
            dve.wait_ge(job_done, job_no(b, J_IDX) + 1)
            if not first:
                dve.wait_ge(job_ready, sum_no(b - 2, 3) + 1)
                dve.wait_ge(row_steps, (b - 1) * 6 + 1)
            dve.tensor_tensor(eq[0:P, q, :, :], idxrow[0:P, :, :], idxf[0:P, q, :].unsqueeze(2).to_broadcast([P, T, P]),
                              ALU.is_equal).then_inc(eq_ready, 1)

        def input_low(b, q, i):
            dve.wait_ge(in_high, b * 2 + i + 1)
            whole, parts_ = ((x0T[64:128, :], x0hl), (a0T[64:128, q, :], a0hl))[i]
            dve.tensor_tensor(parts_[64:128, q, :], whole, parts_[64:128, q, :], ALU.subtract).then_inc(in_low, 1)

        def main(b, q, first=False, more=True):
            dve.wait_ge(job_done, job_no(b, NPREP - 1) + 1)
            for n, op in enumerate(DVE_OPS):
                g, i = n // (NO // GROUPS), n % (NO // GROUPS)
                if i == 0:
                    dve.wait_ge(unit_done, used(b, LAST_UNIT[g - 2] if g >= 2 else LAST_UNIT[g - 2] - NU))
                if op[0] == "add":
                    dve.wait_ge(op_done, made(b, n - 1))
                    dve.tensor_tensor(prod[:, op[1], :], prod[:, op[1], :], prod[:, op[2], :], ALU.add).then_inc(op_done, 1)
                else:
                    dve.wait_ge(src_ready, b * NS + op[1] + 1)
                    source = ring[op[1] % RING][:, 0:W]
                    if op[0] == "z":
                        by = {"a1": a1T, "x1": x1T}[op[3]][:, q, :, :]
                        dve.tensor_tensor(prod[:, op[2]:op[2] + 3, :], source.unsqueeze(1).to_broadcast([128, 3, W]), by,
                                          ALU.mult).then_inc(op_done, 1)
                    else:
                        if op[2] == 22:
                            dve.wait_ge(pool_done, (b + 1) * NPO + 5 * g - 3)
                        if op[2] == 23:
                            dve.wait_ge(pool_done, (b + 1) * NPO + 5 * g)
                        by = a0T[:, q, :] if op[3] == "a0" else a1T[:, q, op[4], :]
                        dve.tensor_tensor(prod[:, op[2], :], source, by, ALU.mult).then_inc(op_done, 1)
                if n == 5 and not first:
                    equal(b, q)
                if n == 10 and more:
                    dve.wait_ge(row_steps, b * 6 + 1)
                    index(b + 1, 1 - q)
                if n in LOW_AT and more:
                    input_low(b + 1, 1 - q, LOW_AT.index(n))

        dve.sem_inc(op_done, NO)
        index(0, 0)
        equal(0, 0, first=True)
        input_low(0, 0, 0)
        input_low(0, 0, 1)
        main(0, 0, first=True)
        sweep(dve, main)
        main(NB - 1, 1, more=False)

    @block.scalar
    def _(act):
        def prep(b, q, j, first=False):
            act.wait_ge(job_ready, job_no(b, j) + 1)
            bk = small[(q + j) % 2]
            if j == J_IDX:
                if not first:
                    act.wait_ge(eq_ready, b)
                to, of = idxrow[0:P, :, :].rearrange("p t e -> p (t e)"), bk[0:P, 0:W]
            elif j == J_X0:
                if not first:
                    act.wait_ge(op_done, made(b - 2, NO - 1))
                    act.wait_ge(in_low, b * 2 - 1)
                to, of = x0T[:, :], bk[:, 0:W]
            elif J_STK <= j < J_STK + 5:
                to = stk[:, q, j - J_STK, :].rearrange("p (t e) -> p t e", t=T)
                of = bk[0:V3, 0:256].bitcast(BF16).rearrange("p (t e) -> p t e", t=T)[:, :, 0:P]
            elif J_XE <= j < J_XE + 4:
                to, of = xeT[:, j - J_XE, :], bk[:, 0:W]
            elif j == J_S:
                to, of = xsumT[:, :], bk[0:M1, 0:W]
            elif J_X1 <= j < J_X1 + 3:
                to, of = x1T[:, q, j - J_X1, :], bk[:, 0:W]
            elif j == J_A0:
                to, of = a0T[:, q, :], bk[:, 0:W]
            else:
                to, of = a1T[:, q, j - J_A1, :], bk[:, 0:W]
            act.activation(to, of, ACT.Copy).then_inc(job_done, 1)
            if j in (J_X0, J_A0):
                act.wait_ge(job_done, job_no(b, j) + 1)
                act.activation((x0hl if j == J_X0 else a0hl)[:, q, :], to, ACT.Copy).then_inc(in_high, 1)

        def part_0(b, q):
            act.wait_ge(gat[q], gathered(b, q))
            act.activation(parts[0:P, :, 0:2, 0, :], xs[0:P, :, 0:M0].rearrange("p t (s u) -> p t s u", u=M1),
                           ACT.Copy).then_inc(casts, 1)
            act.activation(parts[0:P, :, 2:5, 0, :], xs[0:P, :, M0:D].rearrange("p t (u k) -> p t k u", k=3),
                           ACT.Copy).then_inc(casts, 1)

        def part_1(b):
            act.wait_ge(op_steps, b * 11 + 2)
            act.activation(parts[0:P, :, :, 1, :], rest[0:P, :, :, :], ACT.Copy).then_inc(casts, 1)

        def edge_copies(b):
            act.activation(xe[0:P, :, 0, 64:128], xd[0:P, :, 0:M0], ACT.Copy).then_inc(casts, 1)
            act.activation(xe[0:P, :, 1:4, 96:128], xd[0:P, :, M0:D].rearrange("p t (u k) -> p t k u", k=3),
                           ACT.Copy).then_inc(casts, 1)

        def high_part(b, h):
            slot, to, op, _ = HIGHS[h]
            back = 2 if to == 2 else 4
            u = next(u for u in range(NU) if UNITS[u][6] == (h - back) % NH)
            act.wait_ge(op_done, made(b, op))
            act.wait_ge(unit_done, used(b, u if h >= back else u - NU))
            act.activation(high[:, to, :], prod[:, slot, :], ACT.Copy).then_inc(high_ready, 1)

        def updates(b, last=False):
            act.wait_ge(unit_done, used(b, NU - 1))
            act.wait_ge(in_low, (b + 1) * 2 if last else b * 2 + 3)
            act.activation(acc0T[:, :], acc[:, 0, 0:W], ACT.Copy).then_inc(acc_out, 1)
            act.activation(acc1T[:, :], acc[0:V3, 1, 0:W], ACT.Copy).then_inc(acc_out, 1)

        def sums(b, q, h):
            if h == 0:
                act.wait_ge(osum_free, b + 1)
            act.wait_ge(job_ready, sum_no(b, h) + 1)
            to, t = accs if h < 2 else osum, 2 * (h % 2)
            act.activation(to[0:P, t:t + 2, :].rearrange("p t f -> p (t f)"),
                           small[(q + h) % 2][0:P, 0:2 * D], ACT.Copy).then_inc(job_done, 1)

        def count(b):
            act.wait_ge(row_steps, b * 6 + 2)
            for t in range(T):
                if t:
                    act.wait_ge(cnt_ready, b * T + t)
                act.activation(junk[0:P, :], dup[0:P, t, :], ACT.Copy, accum_out=cnt[0:P, t:t + 1]).then_inc(cnt_ready, 1)

        def main(b, q, before=True, more=True):
            for s in range(NS):
                if more and s == 2:
                    part_0(b + 1, 1 - q)
                if more and s == 7:
                    part_1(b + 1)
                if more and s == 13:
                    edge_copies(b + 1)
                if before and s == FIRST_UNIT - 1:
                    updates(b - 1)
                if before and s in SUM_AT:
                    sums(b - 1, 1 - q, SUM_AT.index(s))
                if more and s in PREP_AT:
                    prep(b + 1, 1 - q, PREP_AT.index(s))
                if s == 31:
                    count(b)
                for h in range(NH):
                    if HIGHS[h][3] == s:
                        high_part(b, h)

        act.sem_inc(acc_out, 2)
        part_0(0, 0)
        part_1(0)
        edge_copies(0)
        for j in range(NPREP):
            prep(0, 0, j, first=True)
        act.wait_ge(job_done, NPREP)
        act.sem_inc(job_done, NSUM)
        main(0, 0, before=False)
        sweep(act, main)
        main(NB - 1, 1, more=False)
        act.wait_ge(job_done, NB * NJOB)
        act.sem_inc(job_done, NPREP)
        updates(NB - 1, last=True)
        for h in range(NSUM):
            sums(NB - 1, 1, h)

    ctx.close()


def layer1_edges(nc, tools, x, upd, agg, src_v, dst_v, ea3_v, ef_v, N, NB, ident, lower, spare, weights):
    lin0, lin1, nl0d, nl1e, fc1, fc2a, fc2e, wo_a, wo_s, wo_v = weights
    ctx = ExitStack()
    sb, bank, sem = tools(ctx)
    RE = NB * T
    G = 2 * V3

    rhat = sb("rhat", [128, RE, 3])
    eps = sb("eps1", [128, 1])
    fc2 = sb("fc2", [128, 2, 4, 128], F32R)

    with ExitStack() as c1:
        sb1, _, sem1 = tools(c1)
        ea3 = sb1("ea3", [128, RE, 3])
        sq = sb1("sq", [128, RE, 3])
        nrm = sb1("nrm", [128, RE])
        inv = sb1("inv", [128, RE])
        a_in = sem1("a_in")
        r_steps = sem1("r_steps")
        f_steps = sem1("f_steps")
        blk = c1.enter_context(nc.Block())

        @blk.sync
        def _(sp):
            sp.dma_start(ea3[0:P, :, :].rearrange("p c f -> p (c f)"), ea3_v).then_inc(a_in, 16)

        @blk.scalar
        def _(act):
            act.wait_ge(r_steps, 3)
            act.activation(nrm[0:P, :], nrm[0:P, :], ACT.Sqrt).then_inc(r_steps, 1)

        @blk.vector
        def _(dve):
            for part in range(2):
                for j in range(4):
                    of, n = (fc2a[:, :], 128) if j == 0 else (fc2e[:, j - 1, :, :].rearrange("p k m -> p (k m)"), V3)
                    if part == 0:
                        dve.tensor_copy(fc2[:, 0, j, 0:n], of).then_inc(f_steps, 1)
                    else:
                        dve.wait_ge(f_steps, 4)
                        dve.tensor_tensor(fc2[:, 1, j, 0:n], of, fc2[:, 0, j, 0:n], ALU.subtract).then_inc(f_steps, 1)
            dve.memset(eps[:, :], EPS).then_inc(r_steps, 1)
            dve.wait_ge(a_in, 16)
            dve.tensor_tensor(sq[0:P, :, :], ea3[0:P, :, :], ea3[0:P, :, :], ALU.mult).then_inc(r_steps, 1)
            dve.wait_ge(r_steps, 2)
            dve.tensor_reduce(nrm[0:P, :], sq[0:P, :, :], AX.X, ALU.add).then_inc(r_steps, 1)
            dve.wait_ge(r_steps, 4)
            dve.reciprocal(inv[0:P, :], nrm[0:P, :]).then_inc(r_steps, 1)
            dve.wait_ge(r_steps, 5)
            dve.tensor_tensor(rhat[0:P, :, :], ea3[0:P, :, :], inv[0:P, :].unsqueeze(2).to_broadcast([P, RE, 3]),
                              ALU.mult).then_inc(r_steps, 1)

    isrc = sb("isrc1", [128, 2, T], I32)
    idst = sb("idst1", [128, 2, T], I32)
    ef = sb("ef", [128, 2, T, 64])
    xg = sb("xg", [128, 2, T, D])
    ug = sb("ug", [128, 2, T, D])
    rh6 = sb("rh6", [128, 2, T, 6])
    rh3 = sb("rh3", [128, T, 3, 3, M1])
    idxf = sb("idxf1", [128, 2, T])
    idxrow = sb("idxrow1", [128, T, P])
    eq = sb("eq1", [128, 2, T, P])
    dup = sb("dup1", [128, T, P])
    cnt = sb("cnt1", [128, T])
    later = sb("later1", [128, T])
    junk = sb("junk1", [128, P])
    gap = sb("gap1", [128, T])
    move = sb("move1", [128, T])
    rowf = sb("rowf1", [128, T])
    row = sb("row1", [128, 2, T], I32)
    xaT = sb("xaT", [M0, W])
    xbT = sb("xbT", [V3, W])
    efT = sb("efT", [64, W])
    hT = sb("hT", [128, W])
    hhl = sb("hhl", [128, W], F32R)
    shT = sb("shT", [V3, 2, 3, W])
    w01T = sb("w01T", [128, 2, W])
    w234T = sb("w234T", [V3, 2, 3, W])
    y = sb("y1", [128, T, D])
    st = sb("st1", [128, T, 6])
    mv = sb("mv1", [128, T, 2])
    std = sb("std1", [128, T])
    rstd = sb("rstd1", [128, T])
    x1n = sb("x1n1", [128, T, D])
    n0T = sb("n0T", [M0, W])
    n1T = sb("n1T", [V3, W])
    tA = sb("tA", [128, W])
    t2 = sb("t2", [V3, W])
    b3 = sb("b3", [V3, W])
    t3 = sb("t3", [V3, W])
    c1_ = sb("c1_", [V3, W])
    c2_ = sb("c2_", [V3, W])
    c3_ = sb("c3_", [V3, W])
    t4 = sb("t4", [V3, W])
    qr = sb("qr", [128, T, M1, 3])
    o = sb("o1", [128, T, G])
    osum = sb("osum1", [128, T, G])

    abank = [bank(f"abank{i}") for i in range(4)]
    dbank = [bank(f"dbank{i}") for i in range(4)]

    ld = [sem("ld1_even"), sem("ld1_odd")]
    gat = [sem("gat1_even"), sem("gat1_odd")]
    a_ready = sem("a_ready1")
    a_done = sem("a_done1")
    d_ready = sem("d_ready1")
    d_done = sem("d_done1")
    rh6_ready = sem("rh6_ready")
    rh3_ready = sem("rh3_ready")
    row_steps = sem("row_steps1")
    cnt_ready = sem("cnt_ready1")
    idxf_ready = sem("idxf_ready1")
    eq_ready = sem("eq_ready1")
    h_high = sem("h_high")
    h_low = sem("h_low")
    prods = sem("prods1")
    o_steps = sem("o_steps")
    ln_steps = sem("ln_steps1")
    std_ready = sem("std_ready1")
    x1n_ready = sem("x1n_ready1")
    scat = sem("scat1")
    osum_free = sem("osum_free1")

    A_SUM, A_XT, A_IN, A_FC1, A_W = 0, 2, 4, 11, 12
    D_V, D_Y, D_OUT = 0, 4, 6

    def aj(b, j):
        return (b + 1) * 16 + j

    def dj(b, j):
        return (b + 1) * 8 + j

    def loaded(b, q):
        return (b - q) * 24 + 48

    def gathered(b, q):
        return (b - q) * 64 + 128

    def sweep(eng, iteration):
        iteration(0, 0, True, True)
        with eng.Fori(0, (NB - 4) // 2) as i:
            iteration(2 * i + 1, 1, True, True)
            iteration(2 * i + 2, 0, True, True)
        iteration(NB - 3, 1, True, True)
        iteration(NB - 2, 0, True, False)
        iteration(NB - 1, 1, False, False)

    block = ctx.enter_context(nc.Block())

    @block.sync
    def _(sp):
        def load(b, q):
            sp.dma_start(isrc[0:P, q, :], src_v[:, ds(b * T, T)]).then_inc(ld[q], 16)
            sp.dma_start(idst[0:P, q, :], dst_v[:, ds(b * T, T)]).then_inc(ld[q], 16)
            sp.dma_start(ef[0:P, q, :, :].rearrange("p t f -> p (t f)"), ef_v[:, ds(b * T * 64, T * 64)]).then_inc(ld[q], 16)

        def iteration(b, q, more, more2):
            if more2:
                sp.wait_ge(idxf_ready, b + 1)
                sp.wait_ge(a_ready, aj(b - 1, A_IN + 2) + 1)
                load(b + 2, q)

        load(0, 0)
        load(1, 1)
        sweep(sp, iteration)

    @block.gpsimd
    def _(pool):
        def gather(b, q, t):
            at = bass.IndirectOffsetOnAxis(ap=idst[0:P, q, t:t + 1], axis=0)
            pool.indirect_dma_start(xg[0:P, q, t, :], None, x, at).then_inc(gat[q], 16)
            pool.indirect_dma_start(ug[0:P, q, t, :], None, upd, at).then_inc(gat[q], 16)

        def units(b, q, first=False):
            if not first:
                hold(pool, d_done, dj(b - 2, D_OUT + 1) + 1)
            for j in range(2):
                pool.tensor_copy(rh6[0:P, q, :, 3 * j:3 * j + 3], rhat[0:P, ds(b * T, T), :]).then_inc(rh6_ready, 1)

        def duplicates(b, q):
            hold(pool, eq_ready, b + 1)
            pool.tensor_tensor(dup[0:P, :, :], eq[0:P, q, :, :], lower[0:P, :].unsqueeze(1).to_broadcast([P, T, P]),
                               ALU.mult).then_inc(row_steps, 1)
            pool.tensor_tensor(gap[0:P, :], spare[0:P, :].to_broadcast([P, T]), idxf[0:P, q, :],
                               ALU.subtract).then_inc(row_steps, 1)

        def rows_of(b, q):
            n = b * 6 + 1
            hold(pool, row_steps, n + 2)
            hold(pool, cnt_ready, b * T + T)
            pool.tensor_scalar(later[0:P, :], cnt[0:P, :], 1.0, None, ALU.min).then_inc(row_steps, 1)
            hold(pool, row_steps, n + 3)
            pool.tensor_tensor(move[0:P, :], later[0:P, :], gap[0:P, :], ALU.mult).then_inc(row_steps, 1)
            hold(pool, row_steps, n + 4)
            pool.tensor_tensor(rowf[0:P, :], move[0:P, :], idxf[0:P, q, :], ALU.add).then_inc(row_steps, 1)
            hold(pool, row_steps, n + 5)
            pool.tensor_copy(row[0:P, q, :], rowf[0:P, :]).then_inc(row_steps, 1)

        def scatter(b, q, t):
            if t:
                hold(pool, scat, b * 64 + t * 16)
            pool.indirect_dma_start(agg, bass.IndirectOffsetOnAxis(ap=row[0:P, q, t:t + 1], axis=0),
                                    osum[0:P, t, :], None, compute_op=ALU.add).then_inc(scat, 16)

        def scatter_ready(b):
            hold(pool, row_steps, b * 6 + 7)
            hold(pool, a_done, aj(b + 1, A_SUM + 1) + 1)

        def scattered(b):
            hold(pool, scat, b * 64 + 64)
            pool.sem_inc(osum_free, 1)

        def iteration(b, q, more, more2):
            before = not (isinstance(b, int) and b == 0)
            duplicates(b, q)
            if before:
                scatter_ready(b - 1)
            if more2:
                hold(pool, ld[q], loaded(b + 2, q))
                hold(pool, a_ready, aj(b - 1, A_IN + 1) + 1)
                hold(pool, d_done, dj(b - 1, D_Y + 1) + 1)
            for t in range(T):
                if before:
                    scatter(b - 1, 1 - q, t)
                if more2:
                    gather(b + 2, q, t)
            if before:
                scattered(b - 1)
            rows_of(b, q)
            if more2:
                units(b + 2, q)

        pool.sem_inc(row_steps, 1)
        pool.sem_inc(osum_free, 1)
        for b in range(2):
            hold(pool, ld[b], loaded(b, b))
            for t in range(T):
                gather(b, b, t)
            units(b, b, first=True)
        sweep(pool, iteration)
        scatter_ready(NB - 1)
        for t in range(T):
            scatter(NB - 1, 1, t)
        scattered(NB - 1)

    @block.tensor
    def _(pe):
        def turn(o_, tiles, K, n_=P):
            for t in range(T):
                m = pe.transpose(o_[0:K, t * P:(t + 1) * P], tiles(t), ident[0:P, 0:P])
            m.then_inc(a_ready, 1)

        def abk(b, j):
            hold(pe, a_done, aj(b, j) - 3)
            return abank[j % 4]

        def dbk(b, j):
            hold(pe, d_done, dj(b, j) - 3)
            return dbank[j % 4]

        def inputs(b, q):
            i = b - 1
            hold(pe, gat[q], gathered(b, q))
            turn(abk(i, A_IN), lambda t: xg[0:P, q, t, 0:M0], M0)
            turn(abk(i, A_IN + 1), lambda t: xg[0:P, q, t, M0:D], V3)
            hold(pe, ld[q], loaded(b, q))
            turn(abk(i, A_IN + 2), lambda t: ef[0:P, q, t, :], 64)
            hold(pe, idxf_ready, b + 1)
            turn(abk(i, A_IN + 3), lambda t: idxf[0:P, q, t:t + 1].to_broadcast([P, P]), P)
            hold(pe, rh3_ready, b * 3 + 3)
            for s in range(3):
                turn(abk(i, A_IN + 4 + s), lambda t: rh3[0:P, t, s, :, :].rearrange("p k m -> p (k m)"), V3)
            bk = abk(i, A_FC1)
            hold(pe, a_done, aj(i, A_IN + 2) + 1)
            pe.matmul(bk[:, 0:W], fc1[:, :], efT[:, :], start=True, stop=True).then_inc(a_ready, 1)

        def node_y(b):
            i = b - 1
            pe.wait_ge(a_done, aj(i, A_IN + 1) + 1)
            for h in range(2):
                bk = dbk(i, D_Y + h)
                for j in range(2):
                    cols = slice((2 * h + j) * P, (2 * h + j + 1) * P)
                    oo = bk[0:P, j * D:(j + 1) * D]
                    pe.matmul(oo[:, 0:M0], xaT[:, cols], lin0[:, :], start=True, stop=True)
                    m = pe.matmul(oo[:, M0:D], xbT[:, cols], lin1[:, :, :].rearrange("p w k -> p (w k)"), start=True, stop=True)
                m.then_inc(d_ready, 1)

        def edge_w(b):
            i = b - 1
            pe.wait_ge(h_low, b + 1)
            for j in range(4):
                bk = abk(i, A_W + j)
                n = 128 if j == 0 else V3
                for part in range(2):
                    m = pe.matmul(bk[0:n, 0:W], fc2[:, part, j, 0:n], hhl[:, :], start=(part == 0), stop=(part == 1))
                m.then_inc(a_ready, 1)

        def sums(b, q):
            hold(pe, o_steps, b * 6 + 6)
            hold(pe, eq_ready, b + 1)
            for h in range(2):
                bk = abk(b + 1, A_SUM + h)
                for j in range(2):
                    t = 2 * h + j
                    m = pe.matmul(bk[0:P, j * G:(j + 1) * G], eq[0:P, q, t, :], o[0:P, t, :], start=True, stop=True)
                m.then_inc(a_ready, 1)

        def iteration(b, q, more, more2):
            if isinstance(b, int) and b == 0:
                pe.wait_ge(a_ready, aj(0, 0))
                pe.sem_inc(a_ready, 2)
            else:
                sums(b - 1, 1 - q)
            hold(pe, x1n_ready, b * 4 + 4)
            turn(abk(b, A_XT), lambda t: x1n[0:P, t, 0:M0], M0)
            turn(abk(b, A_XT + 1), lambda t: x1n[0:P, t, M0:D], V3)
            if more:
                inputs(b + 1, 1 - q)
            pe.wait_ge(a_done, aj(b, A_XT + 1) + 1)
            bk = dbk(b, D_V)
            pe.matmul(bk[:, 0:W], nl0d[:, :], n0T[:, :], start=True, stop=True).then_inc(d_ready, 1)
            for s in range(3):
                bk = dbk(b, D_V + 1 + s)
                pe.matmul(bk[0:V3, 0:W], nl1e[:, s, :], n1T[:, :], start=True, stop=True).then_inc(d_ready, 1)
            if more:
                node_y(b + 1)
                edge_w(b + 1)
            else:
                pe.wait_ge(d_ready, dj(b, D_Y))
                pe.sem_inc(d_ready, 2)
            pe.wait_ge(prods, b * 4 + 4)
            for h in range(2):
                bk = dbk(b, D_OUT + h)
                for j in range(2):
                    cols = slice((2 * h + j) * P, (2 * h + j + 1) * P)
                    oo = bk[0:P, j * 224:(j + 1) * 224]
                    pe.matmul(oo[:, 0:128], tA[:, cols], wo_a[:, :], start=True, stop=False)
                    pe.matmul(oo[:, 32:128], t3[:, cols], wo_s[:, :], start=False, stop=True)
                    pe.matmul(oo[:, 128:224], t2[:, cols], wo_v[:, 0, :, :].rearrange("p w k -> p (w k)"),
                              start=True, stop=False, skip_group_check=True)
                    m = pe.matmul(oo[:, 128:224], t4[:, cols], wo_v[:, 1, :, :].rearrange("p w k -> p (w k)"),
                                  start=False, stop=True, skip_group_check=True)
                m.then_inc(d_ready, 1)

        pe.sem_inc(a_ready, 4)
        pe.sem_inc(d_ready, 4)
        inputs(0, 0)
        node_y(0)
        edge_w(0)
        pe.wait_ge(d_ready, 6)
        pe.sem_inc(d_ready, 2)
        sweep(pe, iteration)
        pe.wait_ge(a_ready, aj(NB - 1, A_IN))
        pe.sem_inc(a_ready, 12)
        sums(NB - 1, 1)

    @block.scalar
    def _(act):
        def out(b, j, to, K, cols=W, func=ACT.Copy):
            act.wait_ge(a_ready, aj(b, j) + 1)
            act.activation(to, abank[j % 4][0:K, 0:cols], func).then_inc(a_done, 1)

        def inputs(b, q, first=False, second=False):
            i = b - 1
            out(i, A_IN, xaT[:, :], M0)
            out(i, A_IN + 1, xbT[:, :], V3)
            out(i, A_IN + 2, efT[:, :], 64)
            if not first:
                act.wait_ge(eq_ready, b)
            out(i, A_IN + 3, idxrow[0:P, :, :].rearrange("p t e -> p (t e)"), P)
            if not (first or second):
                act.wait_ge(prods, (b - 1) * 4)
            for s in range(3):
                out(i, A_IN + 4 + s, shT[:, q, s, :], V3)
            if not first:
                act.wait_ge(h_low, b)
            out(i, A_FC1, hT[:, :], 128, func=ACT.Relu)
            act.wait_ge(a_done, aj(i, A_FC1) + 1)
            act.activation(hhl[:, :], hT[:, :], ACT.Copy).then_inc(h_high, 1)

        def edge_w(b, q):
            out(b - 1, A_W, w01T[:, q, :], 128)
            for j in range(3):
                out(b - 1, A_W + 1 + j, w234T[:, q, j, :], V3)

        def deviation(b):
            act.wait_ge(ln_steps, b * 9 + 8)
            act.activation(std[0:P, :], mv[0:P, :, 1], ACT.Sqrt, bias=eps[0:P, :]).then_inc(std_ready, 1)

        def sums(b):
            act.wait_ge(osum_free, b + 1)
            for h in range(2):
                out(b + 1, A_SUM + h, osum[0:P, 2 * h:2 * h + 2, :].rearrange("p t f -> p (t f)"), P, 2 * G)

        def count(b):
            act.wait_ge(row_steps, b * 6 + 2)
            for t in range(T):
                if t:
                    act.wait_ge(cnt_ready, b * T + t)
                act.activation(junk[0:P, :], dup[0:P, t, :], ACT.Copy, accum_out=cnt[0:P, t:t + 1]).then_inc(cnt_ready, 1)

        def unit_rows(b, q):
            act.wait_ge(rh6_ready, b * 2 + 2)
            for s in range(3):
                act.activation(rh3[0:P, :, s, :, :], rh6[0:P, q, :, s:s + 3].unsqueeze(3).to_broadcast([P, T, 3, M1]),
                               ACT.Copy).then_inc(rh3_ready, 1)

        def iteration(b, q, more, more2):
            if isinstance(b, int) and b == 0:
                act.wait_ge(a_done, aj(0, 0))
                act.sem_inc(a_done, 2)
            else:
                sums(b - 1)
            out(b, A_XT, n0T[:, :], M0)
            out(b, A_XT + 1, n1T[:, :], V3)
            if more:
                inputs(b + 1, 1 - q, second=isinstance(b, int) and b == 0)
            if more:
                edge_w(b + 1, 1 - q)
                deviation(b + 1)
            count(b)
            if more2:
                unit_rows(b + 2, q)

        unit_rows(0, 0)
        act.sem_inc(a_done, 4)
        inputs(0, 0, first=True)
        edge_w(0, 0)
        deviation(0)
        unit_rows(1, 1)
        sweep(act, iteration)
        act.wait_ge(a_done, aj(NB - 1, A_IN))
        act.sem_inc(a_done, 12)
        sums(NB - 1)

    @block.vector
    def _(dve):
        def index(b, q):
            dve.wait_ge(ld[q], loaded(b, q))
            dve.wait_ge(row_steps, b * 6 - 5)
            dve.tensor_copy(idxf[0:P, q, :], isrc[0:P, q, :]).then_inc(idxf_ready, 1)

        def equal(b, q):
            dve.wait_ge(a_done, aj(b - 1, A_IN + 3) + 1)
            if not (isinstance(b, int) and b <= 1):
                dve.wait_ge(a_ready, aj(b - 1, A_SUM + 1) + 1)
                dve.wait_ge(row_steps, b * 6 - 5)
            dve.tensor_tensor(eq[0:P, q, :, :], idxrow[0:P, :, :], idxf[0:P, q, :].unsqueeze(2).to_broadcast([P, T, P]),
                              ALU.is_equal).then_inc(eq_ready, 1)

        def fc_low(b):
            dve.wait_ge(h_high, b + 1)
            dve.tensor_tensor(hhl[64:128, :], hT[64:128, :], hhl[64:128, :], ALU.subtract).then_inc(h_low, 1)

        def products(b, q, more):
            dve.wait_ge(a_done, aj(b - 1, A_W + 3) + 1)
            bk = dbank
            dve.wait_ge(d_ready, dj(b, D_V) + 1)
            dve.tensor_tensor(tA[:, :], bk[0][:, 0:W], w01T[:, q, :], ALU.mult).then_inc(d_done, 1)
            if more:
                fc_low(b + 1)
            dve.wait_ge(d_ready, dj(b, D_V + 1) + 1)
            dve.tensor_tensor(t2[:, :], bk[1][0:V3, 0:W], w234T[:, q, 0, :], ALU.mult).then_inc(prods, 1)
            dve.tensor_tensor(b3[:, :], bk[1][0:V3, 0:W], shT[:, q, 0, :], ALU.mult).then_inc(d_done, 1)
            dve.wait_ge(d_ready, dj(b, D_V + 2) + 1)
            dve.tensor_tensor(c1_[:, :], bk[2][0:V3, 0:W], shT[:, q, 2, :], ALU.mult).then_inc(d_done, 1)
            dve.wait_ge(d_ready, dj(b, D_V + 3) + 1)
            dve.tensor_tensor(c2_[:, :], bk[3][0:V3, 0:W], shT[:, q, 1, :], ALU.mult).then_inc(d_done, 1)
            dve.wait_ge(d_done, dj(b, D_V + 1) + 1)
            dve.tensor_tensor(t3[:, :], b3[:, :], w234T[:, q, 1, :], ALU.mult).then_inc(prods, 1)
            dve.wait_ge(d_done, dj(b, D_V + 3) + 1)
            dve.tensor_tensor(c3_[:, :], c1_[:, :], c2_[:, :], ALU.subtract).then_inc(prods, 1)
            dve.wait_ge(prods, b * 4 + 3)
            dve.tensor_tensor(t4[:, :], c3_[:, :], w234T[:, q, 2, :], ALU.mult).then_inc(prods, 1)

        def moments(b, q):
            dve.wait_ge(gat[q], gathered(b, q))
            for h in range(2):
                dve.wait_ge(d_ready, dj(b - 1, D_Y + h) + 1)
                dve.tensor_tensor(y[0:P, 2 * h:2 * h + 2, :].rearrange("p t f -> p (t f)"), dbank[D_Y % 4 + h][0:P, 0:2 * D],
                                  ug[0:P, q, 2 * h:2 * h + 2, :].rearrange("p t f -> p (t f)"), ALU.add).then_inc(d_done, 1)
            for t in range(T):
                dve.wait_ge(d_done, dj(b - 1, D_Y + t // 2) + 1)
                dve.bn_stats(st[0:P, t, :], y[0:P, t, :]).then_inc(ln_steps, 1)
            for t in range(T):
                hold(dve, ln_steps, b * 9 + t + 1)
                dve.bn_aggr(mv[0:P, t, :], st[0:P, t, :]).then_inc(ln_steps, 1)

        def normed(b):
            dve.wait_ge(std_ready, b + 1)
            dve.reciprocal(rstd[0:P, :], std[0:P, :]).then_inc(ln_steps, 1)
            dve.wait_ge(ln_steps, b * 9 + 9)
            if not (isinstance(b, int) and b == 0):
                dve.wait_ge(a_ready, aj(b - 1, A_XT + 1) + 1)
            for t in range(T):
                dve.tensor_scalar(x1n[0:P, t, :], y[0:P, t, :], mv[0:P, t, 0:1], rstd[0:P, t:t + 1], ALU.subtract,
                                  ALU.mult).then_inc(x1n_ready, 1)

        def outputs(b, q):
            if not (isinstance(b, int) and b == 0):
                dve.wait_ge(a_ready, aj(b, A_SUM + 1) + 1)
            for h in range(2):
                dve.wait_ge(d_ready, dj(b, D_OUT + h) + 1)
                g = dbank[D_OUT % 4 + h][0:P, 0:448].rearrange("p (t c) -> p t c", t=2)
                ts = slice(2 * h, 2 * h + 2)
                dve.tensor_copy(o[0:P, ts, 0:V3], g[:, :, 32:128]).then_inc(o_steps, 1)
                dve.tensor_tensor(qr[0:P, ts, :, :], g[:, :, 0:32].unsqueeze(3).to_broadcast([P, 2, M1, 3]),
                                  rh6[0:P, q, ts, 0:3].unsqueeze(2).to_broadcast([P, 2, M1, 3]), ALU.mult).then_inc(o_steps, 1)
                dve.wait_ge(o_steps, b * 6 + h * 3 + 2)
                dve.tensor_tensor(o[0:P, ts, V3:G], g[:, :, 128:224], qr[0:P, ts, :, :].rearrange("p t w k -> p t (w k)"),
                                  ALU.add).then_inc(o_steps, 1)
                dve.wait_ge(o_steps, b * 6 + h * 3 + 3)
                dve.sem_inc(d_done, 1)

        def iteration(b, q, more, more2):
            if more:
                index(b + 1, 1 - q)
            equal(b, q)
            products(b, q, more)
            if more:
                moments(b + 1, 1 - q)
            else:
                dve.wait_ge(d_done, dj(b, D_Y))
                dve.sem_inc(d_done, 2)
            outputs(b, q)
            if more:
                normed(b + 1)

        dve.sem_inc(d_done, 4)
        dve.wait_ge(ld[0], loaded(0, 0))
        dve.tensor_copy(idxf[0:P, 0, :], isrc[0:P, 0, :]).then_inc(idxf_ready, 1)
        fc_low(0)
        moments(0, 0)
        normed(0)
        dve.wait_ge(d_done, 6)
        dve.sem_inc(d_done, 2)
        sweep(dve, iteration)

    ctx.close()


def nodes(nc, tools, x_v, upd_v, agg_v, out_v, NBN, ident, lin0, lin1, skip0, skip1):
    ctx = ExitStack()
    sb, bank, sem = tools(ctx)
    G = 2 * V3
    xn = sb("xn", [128, 2, T, D])
    un = sb("un", [128, 2, T, D])
    gn = sb("gn", [128, 2, T, G])
    xaT = sb("xaT2", [M0, W])
    xbT = sb("xbT2", [V3, W])
    y = sb("y2", [128, T, D])
    st = sb("st2", [128, T, 6])
    mv = sb("mv2", [128, T, 2])
    ve = sb("ve2", [128, T])
    rs = sb("rs2", [128, T])
    half = sb("half", [128, T])
    x1n = sb("x1n2", [128, 2, T, D])
    n0T = sb("n0T2", [M0, W])
    n1T = sb("n1T2", [V3, W])
    a = sb("a2", [128, T, G])
    sg = sb("sg", [128, T, V3])
    f = sb("f2", [128, T, D])
    z = sb("z2", [128, 2, T, D])
    st_z = sb("st_z", [128, T, 6])
    mv_z = sb("mv_z", [128, T, 2])
    ve_z = sb("ve_z", [128, T])
    rs_z = sb("rs_z", [128, T])
    neg_z = sb("neg_z", [128, T])
    off_z = sb("off_z", [128, T])
    ob = sb("ob", [128, 2, T, D])

    abank = [bank(f"nabank{i}") for i in range(4)]
    dbank = [bank(f"ndbank{i}") for i in range(4)]

    ld_x = [sem("ld_x_even"), sem("ld_x_odd")]
    ld_u = [sem("ld_u_even"), sem("ld_u_odd")]
    ld_g = [sem("ld_g_even"), sem("ld_g_odd")]
    a_ready = sem("a_ready2")
    a_done = sem("a_done2")
    d_ready = sem("d_ready2")
    d_done = sem("d_done2")
    half_ready = sem("half_ready")
    ln_y = sem("ln_y")
    rs_y = sem("rs_y")
    x1n_ready = sem("x1n_ready2")
    sg_ready = sem("sg_ready")
    f_ready = sem("f_ready")
    z_ready = sem("z_ready")
    ln_z = sem("ln_z")
    rs_zr = sem("rs_zr")
    off_ready = sem("off_ready")
    ob_ready = sem("ob_ready")
    stored = [sem("stored_even"), sem("stored_odd")]

    A_XT, A_IN = 0, 2
    D_SK, D_Y = 0, 2

    def aj(b, j):
        return (b + 2) * 4 + j

    dj = aj

    def loaded(b, q):
        return (b - q) * 8 + 16

    def sweep(eng, iteration):
        iteration(0, 0, 3)
        with eng.Fori(0, (NBN - 4) // 2) as i:
            iteration(2 * i + 1, 1, 3)
            iteration(2 * i + 2, 0, 3)
        iteration(NBN - 3, 1, 2)
        iteration(NBN - 2, 0, 1)
        iteration(NBN - 1, 1, 0)

    def early(b, n):
        return isinstance(b, int) and b < n

    block = ctx.enter_context(nc.Block())

    @block.sync
    def _(sp):
        def load(b, q, to, of, n, arrived):
            sp.dma_start(to[0:P, q, :, :].rearrange("p t f -> p (t f)"), of[:, ds(b * n, n)]).then_inc(arrived[q], 16)

        def load_x(b, q):
            load(b, q, xn, x_v, T * D, ld_x)

        def load_u(b, q):
            load(b, q, un, upd_v, T * D, ld_u)

        def load_g(b, q):
            load(b, q, gn, agg_v, T * G, ld_g)

        def iteration(b, q, left):
            if left >= 3:
                sp.wait_ge(a_ready, aj(b - 1, A_IN + 1) + 1)
                load_x(b + 3, 1 - q)
                sp.wait_ge(d_done, dj(b - 1, D_Y + 1) + 1)
                load_u(b + 3, 1 - q)
            if left >= 2:
                sp.wait_ge(d_done, dj(b, D_SK + 1) + 1)
                load_g(b + 2, q)
            if not early(b, 1):
                sp.wait_ge(ob_ready, b * 4)
                store(b - 1, 1 - q)

        def store(b, q):
            sp.dma_start(out_v[:, ds(b * T * D, T * D)], ob[0:P, q, :, :].rearrange("p t f -> p (t f)")).then_inc(stored[q], 16)

        for b in range(2):
            load_x(b, b)
            load_u(b, b)
        for b in range(2):
            load_g(b, b)
        sp.wait_ge(a_ready, aj(-2, A_IN + 1) + 1)
        load_x(2, 0)
        sp.wait_ge(d_done, dj(-2, D_Y + 1) + 1)
        load_u(2, 0)
        sweep(sp, iteration)
        sp.wait_ge(ob_ready, NBN * 4)
        store(NBN - 1, 1)
        sp.wait_ge(stored[0], NBN // 2 * 16)
        sp.wait_ge(stored[1], NBN // 2 * 16)

    @block.tensor
    def _(pe):
        def turn(o_, tiles, K):
            for t in range(T):
                m = pe.transpose(o_[0:K, t * P:(t + 1) * P], tiles(t), ident[0:P, 0:P])
            m.then_inc(a_ready, 1)

        def abk(b, j):
            if not early(b, -1):
                hold(pe, a_done, aj(b, j) - 3)
            return abank[j % 4]

        def dbk(b, j):
            if not early(b, -1):
                hold(pe, d_done, dj(b, j) - 3)
            return dbank[j % 4]

        def inputs(b, q):
            hold(pe, ld_x[q], loaded(b, q))
            turn(abk(b - 2, A_IN), lambda t: xn[0:P, q, t, 0:M0], M0)
            turn(abk(b - 2, A_IN + 1), lambda t: xn[0:P, q, t, M0:D], V3)

        def node_y(b):
            pe.wait_ge(a_done, aj(b - 2, A_IN + 1) + 1)
            for h in range(2):
                bk = dbk(b - 2, D_Y + h)
                for j in range(2):
                    cols = slice((2 * h + j) * P, (2 * h + j + 1) * P)
                    oo = bk[0:P, j * D:(j + 1) * D]
                    pe.matmul(oo[:, 0:M0], xaT[:, cols], lin0[:, :], start=True, stop=True)
                    m = pe.matmul(oo[:, M0:D], xbT[:, cols], lin1[:, :, :].rearrange("p w k -> p (w k)"), start=True, stop=True)
                m.then_inc(d_ready, 1)

        def iteration(b, q, left):
            hold(pe, x1n_ready, b * 4 + 4)
            turn(abk(b, A_XT), lambda t: x1n[0:P, q, t, 0:M0], M0)
            turn(abk(b, A_XT + 1), lambda t: x1n[0:P, q, t, M0:D], V3)
            if left >= 2:
                inputs(b + 2, q)
            else:
                pe.wait_ge(a_ready, aj(b, A_IN))
                pe.sem_inc(a_ready, 2)
            pe.wait_ge(a_done, aj(b, A_XT + 1) + 1)
            for h in range(2):
                bk = dbk(b, D_SK + h)
                for j in range(2):
                    cols = slice((2 * h + j) * P, (2 * h + j + 1) * P)
                    oo = bk[0:P, j * G:(j + 1) * G]
                    pe.matmul(oo[:, 0:V3], n0T[:, cols], skip0[:, :], start=True, stop=True)
                    m = pe.matmul(oo[:, V3:G], n1T[:, cols], skip1[:, :, :].rearrange("p w k -> p (w k)"), start=True, stop=True)
                m.then_inc(d_ready, 1)
            if left >= 2:
                node_y(b + 2)
            else:
                pe.wait_ge(d_ready, dj(b, D_Y))
                pe.sem_inc(d_ready, 2)

        for b in range(2):
            if b:
                pe.wait_ge(a_ready, aj(b - 2, 0))
                pe.wait_ge(d_ready, dj(b - 2, 0))
            pe.sem_inc(a_ready, 2)
            pe.sem_inc(d_ready, 2)
            inputs(b, b)
            node_y(b)
        sweep(pe, iteration)

    @block.scalar
    def _(act):
        def out(b, j, to, K):
            act.wait_ge(a_ready, aj(b, j) + 1)
            act.activation(to, abank[j % 4][0:K, 0:W], ACT.Copy).then_inc(a_done, 1)

        def inputs(b):
            out(b - 2, A_IN, xaT[:, :], M0)
            out(b - 2, A_IN + 1, xbT[:, :], V3)

        def result(b, q):
            act.wait_ge(off_ready, b * 2 + 2)
            if not early(b, 2):
                act.wait_ge(stored[q], (b - q) * 8)
            for t in range(T):
                act.activation(ob[0:P, q, t, :], z[0:P, q, t, :], ACT.Identity, bias=off_z[0:P, t:t + 1],
                               scale=rs_z[0:P, t:t + 1]).then_inc(ob_ready, 1)

        def iteration(b, q, left):
            out(b, A_XT, n0T[:, :], M0)
            out(b, A_XT + 1, n1T[:, :], V3)
            if left >= 2:
                inputs(b + 2)
            else:
                act.wait_ge(a_done, aj(b, A_IN))
                act.sem_inc(a_done, 2)
            act.wait_ge(d_done, dj(b, D_SK + 1) + 1)
            if not early(b, 1):
                act.wait_ge(f_ready, b * 2)
            act.activation(sg[0:P, :, :], a[0:P, :, 0:V3], ACT.Sigmoid).then_inc(sg_ready, 1)
            if not early(b, 1):
                result(b - 1, 1 - q)

        for b in range(2):
            if b:
                act.wait_ge(a_done, aj(b - 2, 0))
            act.sem_inc(a_done, 2)
            inputs(b)
        sweep(act, iteration)
        result(NBN - 1, 1)

    @block.gpsimd
    def _(pool):
        def power(b, moments, mv_, ve_, rs_, done):
            hold(pool, moments, b * 8 + 8)
            if done is rs_zr and not early(b, 1):
                hold(pool, ob_ready, b * 4)
            pool.tensor_scalar(ve_[0:P, :], mv_[0:P, :, 1], EPS, None, ALU.add).then_inc(done, 1)
            hold(pool, done, b * 2 + 1)
            pool.tensor_tensor(rs_[0:P, :], ve_[0:P, :], half[0:P, :], ALU.pow).then_inc(done, 1)

        def offset(b):
            power(b, ln_z, mv_z, ve_z, rs_z, rs_zr)
            pool.tensor_scalar(neg_z[0:P, :], mv_z[0:P, :, 0], -1.0, None, ALU.mult).then_inc(off_ready, 1)
            hold(pool, rs_zr, b * 2 + 2)
            hold(pool, off_ready, b * 2 + 1)
            pool.tensor_tensor(off_z[0:P, :], neg_z[0:P, :], rs_z[0:P, :], ALU.mult).then_inc(off_ready, 1)

        def iteration(b, q, left):
            if left:
                power(b + 1, ln_y, mv, ve, rs, rs_y)
            if not early(b, 1):
                offset(b - 1)
                hold(pool, z_ready, b)
            hold(pool, sg_ready, b + 1)
            pool.tensor_tensor(f[0:P, :, 0:M0], a[0:P, :, 0:M0], sg[0:P, :, 0:M0], ALU.mult).then_inc(f_ready, 1)
            pool.tensor_tensor(f[0:P, :, M0:D].rearrange("p t (w k) -> p t w k", k=3),
                               a[0:P, :, V3:G].rearrange("p t (w k) -> p t w k", k=3),
                               sg[0:P, :, M0:V3].unsqueeze(3).to_broadcast([P, T, M1, 3]), ALU.mult).then_inc(f_ready, 1)
            hold(pool, f_ready, b * 2 + 2)
            if not early(b, 2):
                hold(pool, ob_ready, b * 4 - 4)
            pool.tensor_tensor(z[0:P, q, :, :], f[0:P, :, :], x1n[0:P, q, :, :], ALU.add).then_inc(z_ready, 1)

        pool.memset(half[:, :], -0.5).then_inc(half_ready, 1)
        pool.wait_ge(half_ready, 1)
        power(0, ln_y, mv, ve, rs, rs_y)
        sweep(pool, iteration)
        offset(NBN - 1)

    @block.vector
    def _(dve):
        def moments_of(v, st_, mv_, b, steps):
            for t in range(T):
                dve.bn_stats(st_[0:P, t, :], v[:, t, :]).then_inc(steps, 1)
            for t in range(T):
                hold(dve, steps, b * 8 + t + 1)
                dve.bn_aggr(mv_[0:P, t, :], st_[0:P, t, :]).then_inc(steps, 1)

        def moments(b, q):
            dve.wait_ge(ld_u[q], loaded(b, q))
            if not early(b, 1):
                dve.wait_ge(x1n_ready, b * 4)
            for h in range(2):
                dve.wait_ge(d_ready, dj(b - 2, D_Y + h) + 1)
                dve.tensor_tensor(y[0:P, 2 * h:2 * h + 2, :].rearrange("p t f -> p (t f)"), dbank[D_Y + h][0:P, 0:2 * D],
                                  un[0:P, q, 2 * h:2 * h + 2, :].rearrange("p t f -> p (t f)"), ALU.add).then_inc(d_done, 1)
            dve.wait_ge(d_done, dj(b - 2, D_Y + 1) + 1)
            moments_of(y[0:P], st, mv, b, ln_y)

        def normed(b, q):
            dve.wait_ge(rs_y, b * 2 + 2)
            if not early(b, 2):
                dve.wait_ge(z_ready, b - 1)
            for t in range(T):
                dve.tensor_scalar(x1n[0:P, q, t, :], y[0:P, t, :], mv[0:P, t, 0:1], rs[0:P, t:t + 1], ALU.subtract,
                                  ALU.mult).then_inc(x1n_ready, 1)

        def moments_z(b, q):
            dve.wait_ge(z_ready, b + 1)
            if not early(b, 1):
                dve.wait_ge(off_ready, b * 2)
            moments_of(z[0:P, q], st_z, mv_z, b, ln_z)

        def iteration(b, q, left):
            if left:
                moments(b + 1, 1 - q)
            else:
                dve.wait_ge(d_done, dj(b - 1, D_Y))
                dve.sem_inc(d_done, 2)
            if not early(b, 1):
                moments_z(b - 1, 1 - q)
                dve.wait_ge(f_ready, b * 2)
            dve.wait_ge(ld_g[q], loaded(b, q))
            for h in range(2):
                dve.wait_ge(d_ready, dj(b, D_SK + h) + 1)
                dve.tensor_tensor(a[0:P, 2 * h:2 * h + 2, :].rearrange("p t f -> p (t f)"), dbank[D_SK + h][0:P, 0:2 * G],
                                  gn[0:P, q, 2 * h:2 * h + 2, :].rearrange("p t f -> p (t f)"), ALU.add).then_inc(d_done, 1)
            if left:
                normed(b + 1, 1 - q)

        dve.sem_inc(d_done, 2)
        moments(0, 0)
        normed(0, 0)
        dve.wait_ge(d_done, dj(-1, 0))
        dve.sem_inc(d_done, 2)
        sweep(dve, iteration)
        moments_z(NBN - 1, 1)

    ctx.close()


_INS = ['x', 'src', 'dst', 'edge_attr_3', 'edge_attr_4', 'edge_attr_64', 'L0_gnn_wm000', 'L0_gnn_wm011',
        'L0_gnn_wm101', 'L0_gnn_wm110', 'L0_gnn_lm0', 'L0_gnn_lm1', 'L0_gnn_wu000', 'L0_gnn_wu011', 'L0_gnn_wu101',
        'L0_gnn_wu110', 'L0_gnn_lu0', 'L0_gnn_lu1', 'L1_gnn_W_skip0', 'L1_gnn_W_skip1', 'L1_gnn_W_nl0',
        'L1_gnn_W_nl1', 'L1_gnn_W_fc1', 'L1_gnn_W_fc2', 'L1_gnn_W_out_s', 'L1_gnn_W_out_v']


def kernel(**inputs):
    import numpy as _np
    import concourse.bacc as _bacc
    from concourse import mybir as _mybir
    from concourse.bass_utils import run_bass_kernel_spmd as _run

    nc = _bacc.Bacc("TRN2", target_bir_lowering=False, num_devices=1)
    arrays, args = {}, []
    for name in _INS:
        a = _np.ascontiguousarray(inputs[name])
        arrays[f"in_{name}_dram"] = a
        args.append(nc.dram_tensor(f"in_{name}_dram", a.shape, _mybir.dt.from_np(a.dtype), kind="ExternalInput").ap())
    shape = inputs['x'].shape
    args.append(nc.dram_tensor("out_0_dram", shape, _mybir.dt.from_np(_np.dtype('float32')), kind="ExternalOutput").ap())
    build(nc, *args)
    r = _run(nc, [arrays], core_ids=[0])
    return r.results[0]["out_0_dram"]
```
